# Optimizing a Trainium2 kernel written in Bass

```python
import numpy as np
import jax
import jax.numpy as jnp

def _softmax(x, axis=-1):
    return jax.nn.softmax(x, axis=axis)

def _gelu(x):
    return jax.nn.gelu(x, approximate=True)

def _silu(x):
    return jax.nn.silu(x)

def _sigmoid(x):
    return jax.nn.sigmoid(x)

def _layernorm(x, axis=-1, eps=1e-05):
    m = jnp.mean(x, axis=axis, keepdims=True)
    v = jnp.var(x, axis=axis, keepdims=True)
    return (x - m) / jnp.sqrt(v + eps)

def _scatter_add(tgt, idx, src, axis=0):
    return tgt.at[idx].add(src)

def _segment_sum(src, seg, n):
    return jax.ops.segment_sum(src, seg, n)
kernel_name = 'mk_gnn_resnorm_d4_gnn_r32_47d9ed'

def setup_inputs(seed: int=0):
    np.random.seed(seed)
    _w = jnp.asarray

    def _rec_inputs():
        import jax
        import jax.numpy as jnp
        _gk = jax.random.key(seed)
        x = -8.776e-05 + 1 * jax.random.normal(jax.random.fold_in(_gk, 1), (3125, 256), jnp.float32)
        src = jax.random.randint(jax.random.fold_in(_gk, 2), (50000,), 0, 3125, jnp.int32)
        dst = jax.random.randint(jax.random.fold_in(_gk, 3), (50000,), 0, 3125, jnp.int32)
        _o = jnp.argsort(dst, stable=True)
        src = src[_o]
        dst = dst[_o]
        edge_attr_64 = 0.000102155 + 1.00015 * jax.random.normal(jax.random.fold_in(_gk, 12), (50000, 64), jnp.float32)
        edge_type_16 = jax.random.randint(jax.random.fold_in(_gk, 14), (50000,), 0, 16, jnp.int32)
        edge_weight1 = jax.random.uniform(jax.random.fold_in(_gk, 15), (50000, 1), jnp.float32, 0.0, 0.999998)
        return (x, src, dst, edge_attr_64, edge_type_16, edge_weight1)
    x, src, dst, edge_attr_64, edge_type_16, edge_weight1 = _rec_inputs()

    def _L0_gnn_setup():
        import jax, jax.numpy as jnp
        import numpy as np
        N_NODES = 625
        N_EDGES = 10000
        NUM_RELS = 16
        IN_FEAT = 256
        OUT_FEAT = 256
        key = jax.random.key(seed)
        k_h, k_w, k_n, k_s, k_d, k_r = jax.random.split(key, 6)
        h = jax.random.normal(k_h, (N_NODES, IN_FEAT), dtype=jnp.float32)
        weight = jax.random.normal(k_w, (NUM_RELS, IN_FEAT, OUT_FEAT), dtype=jnp.float32)
        norm = jax.random.uniform(k_n, (N_EDGES, 1), dtype=jnp.float32)
        src = jax.random.randint(k_s, (N_EDGES,), 0, N_NODES, dtype=jnp.int32)
        dst = jax.random.randint(k_d, (N_EDGES,), 0, N_NODES, dtype=jnp.int32)
        rel_type = jax.random.randint(k_r, (N_EDGES,), 0, NUM_RELS, dtype=jnp.int32)
        return {'h': h, 'weight': weight, 'norm': norm, 'src': src, 'dst': dst, 'rel_type': rel_type}
    _L0_gnn_all = _L0_gnn_setup()
    _L0_gnn_in = {k: v for k, v in _L0_gnn_all.items() if k in ('weight',)}
    del _L0_gnn_all

    def _L1_gnn_setup():
        import jax, jax.numpy as jnp
        import numpy as np
        N = 3125
        E = 50000
        D_IN = 256
        HIDDEN = 300
        D_OUT = 256

        def _gcn_conv(x, row, col, w, b, num_nodes):
            h = x @ w
            deg = jax.ops.segment_sum(jnp.ones_like(col, dtype=h.dtype), col, num_segments=num_nodes)
            dinv = jnp.where(deg > 0, jax.lax.rsqrt(deg), 0.0)
            norm = dinv[row] * dinv[col]
            msg = h[row] * norm[:, None]
            out = jax.ops.segment_sum(msg, col, num_segments=num_nodes)
            return out + b
        key = jax.random.key(seed)
        ks = jax.random.split(key, 6)
        x = jax.random.normal(ks[0], (N, D_IN), dtype=jnp.float32)
        edge_index = jax.random.randint(ks[1], (2, E), 0, N, dtype=jnp.int64)
        w1 = jax.random.normal(ks[2], (D_IN, HIDDEN), dtype=jnp.float32) * (1.0 / np.sqrt(D_IN))
        b1 = jnp.zeros((HIDDEN,), dtype=jnp.float32)
        w2 = jax.random.normal(ks[3], (HIDDEN, D_OUT), dtype=jnp.float32) * (1.0 / np.sqrt(HIDDEN))
        b2 = jnp.zeros((D_OUT,), dtype=jnp.float32)
        return {'x': x, 'edge_index': edge_index, 'w1': w1, 'b1': b1, 'w2': w2, 'b2': b2}
    _L1_gnn_all = _L1_gnn_setup()
    _L1_gnn_in = {k: v for k, v in _L1_gnn_all.items() if k in ('w1', 'b1', 'w2', 'b2')}
    del _L1_gnn_all

    def _L2_gnn_setup():
        import jax, jax.numpy as jnp
        import numpy as np
        N_NODES = 50000
        N_EDGES = 15625
        HDIM = 256
        EDIM = 64
        MSG_H = 512
        UPD_H = 512
        LN_EPS = 1e-05

        def _mlp(x, W1, b1, W2, b2):
            return jax.nn.relu(x @ W1 + b1) @ W2 + b2

        def _layer_norm(x, gamma, beta):
            mu = jnp.mean(x, axis=-1, keepdims=True)
            var = jnp.mean(jnp.square(x - mu), axis=-1, keepdims=True)
            return (x - mu) * jax.lax.rsqrt(var + LN_EPS) * gamma + beta
        key = jax.random.key(seed)
        ks = jax.random.split(key, 12)

        def lin_init(k, fan_in, fan_out):
            bound = 1.0 / np.sqrt(fan_in)
            return jax.random.uniform(k, (fan_in, fan_out), jnp.float32, -bound, bound)
        h = jax.random.normal(ks[0], (N_NODES, HDIM), jnp.float32)
        edge_index = jax.random.randint(ks[1], (2, N_EDGES), 0, N_NODES, jnp.int64)
        edge_attr = jax.random.normal(ks[2], (N_EDGES, EDIM), jnp.float32)
        eW1 = lin_init(ks[3], 2 * HDIM + EDIM, MSG_H)
        eb1 = jnp.zeros((MSG_H,), jnp.float32)
        eW2 = lin_init(ks[4], MSG_H, HDIM)
        eb2 = jnp.zeros((HDIM,), jnp.float32)
        nW1 = lin_init(ks[5], 2 * HDIM, UPD_H)
        nb1 = jnp.zeros((UPD_H,), jnp.float32)
        nW2 = lin_init(ks[6], UPD_H, HDIM)
        nb2 = jnp.zeros((HDIM,), jnp.float32)
        ln_gamma = jnp.ones((HDIM,), jnp.float32)
        ln_beta = jnp.zeros((HDIM,), jnp.float32)
        return {'h': h, 'edge_index': edge_index, 'edge_attr': edge_attr, 'eW1': eW1, 'eb1': eb1, 'eW2': eW2, 'eb2': eb2, 'nW1': nW1, 'nb1': nb1, 'nW2': nW2, 'nb2': nb2, 'ln_gamma': ln_gamma, 'ln_beta': ln_beta}
    _L2_gnn_all = _L2_gnn_setup()
    _L2_gnn_in = {k: v for k, v in _L2_gnn_all.items() if k in ('eW1', 'eb1', 'eW2', 'eb2', 'nW1', 'nb1', 'nW2', 'nb2', 'ln_gamma', 'ln_beta')}
    del _L2_gnn_all

    def _L3_gnn_setup():
        import jax, jax.numpy as jnp
        import numpy as np
        HEADS = 4
        OUT_CH = 64
        NEG_SLOPE = 0.2
        key = jax.random.key(seed)
        k1, k2, k3, k4, k5 = jax.random.split(key, 5)
        N, E, IN = (50000, 50000, 256)
        x = jax.random.normal(k1, (N, IN), dtype=jnp.float32)
        edge_index = jax.random.randint(k2, (2, E), 0, N, dtype=jnp.int32)
        W = jax.random.normal(k3, (IN, HEADS * OUT_CH), dtype=jnp.float32) * (1.0 / np.sqrt(IN))
        att_src = jax.random.normal(k4, (HEADS, OUT_CH), dtype=jnp.float32) * 0.1
        att_dst = jax.random.normal(k5, (HEADS, OUT_CH), dtype=jnp.float32) * 0.1
        bias = jnp.zeros((HEADS * OUT_CH,), dtype=jnp.float32)
        return {'x': x, 'edge_index': edge_index, 'W': W, 'att_src': att_src, 'att_dst': att_dst, 'bias': bias}
    _L3_gnn_all = _L3_gnn_setup()
    _L3_gnn_in = {k: v for k, v in _L3_gnn_all.items() if k in ('W', 'att_src', 'att_dst', 'bias')}
    del _L3_gnn_all
    return {'x': x, 'src': src, 'dst': dst, 'edge_attr_64': edge_attr_64, 'edge_type_16': edge_type_16, 'edge_weight1': edge_weight1, 'L0_gnn_weight': _L0_gnn_in['weight'], 'L1_gnn_w1': _L1_gnn_in['w1'], 'L1_gnn_b1': _L1_gnn_in['b1'], 'L1_gnn_w2': _L1_gnn_in['w2'], 'L1_gnn_b2': _L1_gnn_in['b2'], 'L2_gnn_eW1': _L2_gnn_in['eW1'], 'L2_gnn_eb1': _L2_gnn_in['eb1'], 'L2_gnn_eW2': _L2_gnn_in['eW2'], 'L2_gnn_eb2': _L2_gnn_in['eb2'], 'L2_gnn_nW1': _L2_gnn_in['nW1'], 'L2_gnn_nb1': _L2_gnn_in['nb1'], 'L2_gnn_nW2': _L2_gnn_in['nW2'], 'L2_gnn_nb2': _L2_gnn_in['nb2'], 'L2_gnn_ln_gamma': _L2_gnn_in['ln_gamma'], 'L2_gnn_ln_beta': _L2_gnn_in['ln_beta'], 'L3_gnn_W': _L3_gnn_in['W'], 'L3_gnn_att_src': _L3_gnn_in['att_src'], 'L3_gnn_att_dst': _L3_gnn_in['att_dst'], 'L3_gnn_bias': _L3_gnn_in['bias']}

def reference(x, src, dst, edge_attr_64, edge_type_16, edge_weight1, L0_gnn_weight, L1_gnn_w1, L1_gnn_b1, L1_gnn_w2, L1_gnn_b2, L2_gnn_eW1, L2_gnn_eb1, L2_gnn_eW2, L2_gnn_eb2, L2_gnn_nW1, L2_gnn_nb1, L2_gnn_nW2, L2_gnn_nb2, L2_gnn_ln_gamma, L2_gnn_ln_beta, L3_gnn_W, L3_gnn_att_src, L3_gnn_att_dst, L3_gnn_bias):
    import jax
    import jax.numpy as jnp

    def _L0_gnn_ref(h, weight, norm, src, dst, rel_type):
        import jax, jax.numpy as jnp
        import numpy as np
        N_NODES = 625
        N_EDGES = 10000
        NUM_RELS = 16
        IN_FEAT = 256
        OUT_FEAT = 256
        transformed = jnp.einsum('ni,rio->rno', h, weight)
        msg = transformed[rel_type, src] * norm
        out = jax.ops.segment_sum(msg, dst, num_segments=h.shape[0])
        return out

    def _L1_gnn_ref(x, edge_index, w1, b1, w2, b2):
        import jax, jax.numpy as jnp
        import numpy as np
        N = 3125
        E = 50000
        D_IN = 256
        HIDDEN = 300
        D_OUT = 256

        def _gcn_conv(x, row, col, w, b, num_nodes):
            h = x @ w
            deg = jax.ops.segment_sum(jnp.ones_like(col, dtype=h.dtype), col, num_segments=num_nodes)
            dinv = jnp.where(deg > 0, jax.lax.rsqrt(deg), 0.0)
            norm = dinv[row] * dinv[col]
            msg = h[row] * norm[:, None]
            out = jax.ops.segment_sum(msg, col, num_segments=num_nodes)
            return out + b
        num_nodes = x.shape[0]
        loops = jnp.arange(num_nodes, dtype=edge_index.dtype)
        row = jnp.concatenate([edge_index[0], loops])
        col = jnp.concatenate([edge_index[1], loops])
        h = _gcn_conv(x, row, col, w1, b1, num_nodes)
        h = jax.nn.relu(h)
        out = _gcn_conv(h, row, col, w2, b2, num_nodes)
        return out

    def _L2_gnn_ref(h, edge_index, edge_attr, eW1, eb1, eW2, eb2, nW1, nb1, nW2, nb2, ln_gamma, ln_beta):
        import jax, jax.numpy as jnp
        import numpy as np
        N_NODES = 50000
        N_EDGES = 15625
        HDIM = 256
        EDIM = 64
        MSG_H = 512
        UPD_H = 512
        LN_EPS = 1e-05

        def _mlp(x, W1, b1, W2, b2):
            return jax.nn.relu(x @ W1 + b1) @ W2 + b2

        def _layer_norm(x, gamma, beta):
            mu = jnp.mean(x, axis=-1, keepdims=True)
            var = jnp.mean(jnp.square(x - mu), axis=-1, keepdims=True)
            return (x - mu) * jax.lax.rsqrt(var + LN_EPS) * gamma + beta
        src = edge_index[0]
        dst = edge_index[1]
        m_in = jnp.concatenate([h[src], h[dst], edge_attr], axis=1)
        m = _mlp(m_in, eW1, eb1, eW2, eb2)
        agg = jax.ops.segment_sum(m, dst, num_segments=h.shape[0])
        h_upd = _mlp(jnp.concatenate([h, agg], axis=1), nW1, nb1, nW2, nb2)
        return _layer_norm(h + h_upd, ln_gamma, ln_beta)

    def _L3_gnn_ref(x, edge_index, W, att_src, att_dst, bias):
        import jax, jax.numpy as jnp
        import numpy as np
        HEADS = 4
        OUT_CH = 64
        NEG_SLOPE = 0.2
        N = x.shape[0]
        loop = jnp.arange(N, dtype=edge_index.dtype)
        src = jnp.concatenate([edge_index[0], loop])
        dst = jnp.concatenate([edge_index[1], loop])
        h = (x @ W).reshape(N, HEADS, OUT_CH)
        a_src = jnp.einsum('nhc,hc->nh', h, att_src)
        a_dst = jnp.einsum('nhc,hc->nh', h, att_dst)
        e = a_src[src] + a_dst[dst]
        e = jnp.where(e >= 0, e, NEG_SLOPE * e)
        e_max = jax.ops.segment_max(e, dst, num_segments=N)
        e_exp = jnp.exp(e - e_max[dst])
        denom = jax.ops.segment_sum(e_exp, dst, num_segments=N)
        alpha = e_exp / denom[dst]
        msgs = h[src] * alpha[:, :, None]
        out = jax.ops.segment_sum(msgs, dst, num_segments=N)
        out = out.reshape(N, HEADS * OUT_CH) + bias
        out = jax.nn.relu(out)
        norm = jnp.sqrt(jnp.sum(out * out, axis=-1, keepdims=True))
        out = out / jnp.maximum(norm, 1e-12)
        return out
    edge_index = jnp.stack([src, dst])
    x = _layernorm(x + _L0_gnn_ref(x, L0_gnn_weight, edge_weight1, src, dst, edge_type_16), axis=-1)
    x = _layernorm(x + _L1_gnn_ref(x, edge_index, L1_gnn_w1, L1_gnn_b1, L1_gnn_w2, L1_gnn_b2), axis=-1)
    x = _layernorm(x + _L2_gnn_ref(x, edge_index, edge_attr_64, L2_gnn_eW1, L2_gnn_eb1, L2_gnn_eW2, L2_gnn_eb2, L2_gnn_nW1, L2_gnn_nb1, L2_gnn_nW2, L2_gnn_nb2, L2_gnn_ln_gamma, L2_gnn_ln_beta), axis=-1)
    x = _layernorm(x + _L3_gnn_ref(x, edge_index, L3_gnn_W, L3_gnn_att_src, L3_gnn_att_dst, L3_gnn_bias), axis=-1)
    return x

_drawn_inputs = setup_inputs


def setup_inputs(seed=0):
    import zlib

    import numpy as np

    out = dict(_drawn_inputs(seed))
    spreads = {'L1_gnn_b1': (0.0, 0.1),
     'L1_gnn_b2': (0.0, 0.1),
     'L2_gnn_eb1': (0.0, 0.1),
     'L2_gnn_eb2': (0.0, 0.1),
     'L2_gnn_nb1': (0.0, 0.437),
     'L2_gnn_nb2': (0.0, 0.1),
     'L2_gnn_ln_gamma': (1.0, 0.2),
     'L2_gnn_ln_beta': (0.0, 0.1),
     'L3_gnn_bias': (0.0, 0.513)}
    factors = {'L3_gnn_att_dst': 64.0, 'L3_gnn_att_src': 4.243}
    for name, (base, spread) in spreads.items():
        noise = np.random.default_rng([zlib.crc32(name.encode()), seed]).standard_normal(out[name].shape)
        drawn = base * np.exp(spread * noise) if base else spread * noise
        out[name] = jnp.asarray(drawn.astype(out[name].dtype))
    for name, factor in factors.items():
        out[name] = (out[name] * factor).astype(out[name].dtype)
    return out
```

```python
from contextlib import ExitStack

import numpy as np
import concourse.bass as bass
import concourse.mybir as mybir
from concourse.alu_op_type import AluOpType as ALU

F32 = mybir.dt.float32
I32 = mybir.dt.int32
ACT = mybir.ActivationFunctionType
AX = mybir.AxisListType

P = 128
N = 3125
E = 50000
D = 256
RELS = 16
HID1 = 300
HC = 3
HR = HID1 // HC
HID2 = 512
EDIM = 64
HEADS = 4
CH = D // HEADS
NW = 26
NP = NW * P
GROUP = 4
NG = -(-E // (P * GROUP))
EP = NG * GROUP * P
NT = NG * GROUP
RING = 2 * GROUP
HG = NG // 2
HW = NW // 2
PAD_NODE = N + 74
WIDE = 512
EPS = 1e-5
SLOPE = 0.2
assert NG % 2 == 0 and NW % 2 == 0 and N <= PAD_NODE < NP


class State:
    pass


def phase_end(nc, ctx):
    ctx.callback(nc.all_engine_barrier)


def phase_semaphore(nc, ctx, name):
    handle = nc.alloc_semaphore(name)
    ctx.callback(nc.clear_and_free_semaphores, [handle])
    return handle


def within(nc, value, top):
    return nc.s_assert_within(value, 0, top, skip_runtime_bounds_check_because="the group ranges are computed from node numbers below N")


def group_range(nc, eng, st, group):
    first = eng.value_load(st.ranges[0:1, bass.ds(3 * group, 1)], min_val=0, max_val=NW - 1)
    count = eng.value_load(st.ranges[0:1, bass.ds(3 * group + 1, 1)], min_val=1, max_val=NW)
    before = eng.value_load(st.ranges[0:1, bass.ds(3 * group + 2, 1)], min_val=0, max_val=NG * NW)
    return first, count, before


def prepare(nc, st, ins):
    with ExitStack() as ctx:
        phase_end(nc, ctx)
        def sb(name, shape, dt):
            return ctx.enter_context(nc.sbuf_tensor("pre_" + name, shape, dt))

        def sem(name):
            return phase_semaphore(nc, ctx, "pre_" + name)

        src_i = sb("src_i", [P, NT], I32)
        type_i = sb("type_i", [P, NT], I32)
        dst_g = sb("dst_g", [NG, GROUP * P], I32)
        low_high = sb("low_high", [NG, 2], I32)
        windows = sb("windows", [NG, 2], I32)
        windows_f = sb("windows_f", [NG, 2], F32)
        table = sb("table", [NG, 3], F32)
        table_i = sb("table_i", [NG, 3], I32)
        earlier = sb("earlier", [NG, NG], F32)
        ones = sb("ones", [P, P], F32)
        src_f = sb("src_f", [P, NT], F32)
        steps_psum = ctx.enter_context(nc.psum_tensor("pre_steps", [P, 512], F32))
        loaded, summed, filled, iotas, chain, counted, stepped, spilled, fetched = (
            sem(n) for n in ("loaded", "summed", "filled", "iotas", "chain", "counted", "stepped", "spilled", "fetched"))
        block = ctx.enter_context(nc.Block())

        @block.sync
        def _(sp):
            sp.dma_start(st.dst_row[:], ins["dst"]).then_inc(loaded, 16)
            sp.dma_start(src_i[:], ins["src"]).then_inc(loaded, 16)
            sp.dma_start(type_i[:], ins["edge_type"]).then_inc(loaded, 16)
            sp.dma_start(dst_g[:], ins["dst_by_group"]).then_inc(loaded, 16)
            sp.dma_start(st.weight[:], ins["edge_weight"]).then_inc(loaded, 16)
            sp.wait_ge(loaded, 5 * 16)
            sp.wait_ge(stepped, 1)
            sp.dma_start(st.ranges_dram, table_i[:]).then_inc(spilled, 16)
            sp.wait_ge(spilled, 16)
            sp.dma_start(st.ranges[:], st.ranges_dram.rearrange("(a g) c -> a (g c)", a=1)).then_inc(fetched, 16)
            sp.wait_ge(fetched, 16)

        @block.gpsimd
        def _(pool):
            pool.memset(ones[:], 1.0).then_inc(filled, 1)
            pool.iota(st.iota[:], pattern=[[1, P]], base=0, channel_multiplier=0,
                      allow_small_or_imprecise_dtypes=True).then_inc(iotas, 1)
            pool.iota(st.window_start[:], pattern=[[P, NW]], base=0, channel_multiplier=0,
                      allow_small_or_imprecise_dtypes=True).then_inc(iotas, 1)
            pool.wait_ge(filled, 1)
            pool.affine_select(out=st.ident[:], in_=ones[:], compare_op=ALU.is_equal, fill=0.0, base=0,
                               pattern=[[-1, P]], channel_multiplier=1).then_inc(iotas, 1)
            pool.affine_select(out=earlier[:], in_=ones[0:NG, 0:NG], compare_op=ALU.is_gt, fill=0.0, base=0,
                               pattern=[[1, NG]], channel_multiplier=-1).then_inc(filled, 1)

        @block.vector
        def _(dve):
            done = [0]

            def link(ins_):
                done[0] += 1
                ins_.then_inc(chain, 1)
                dve.wait_ge(chain, done[0])

            dve.wait_ge(loaded, 5 * 16)
            dve.tensor_copy(st.dst[:], st.dst_row[:])
            dve.tensor_copy(st.src[:], src_i[:])
            link(dve.tensor_copy(src_f[:], src_i[:]))
            dve.scalar_tensor_tensor(out=st.src_type[:], in0=src_f[:], scalar=float(RELS), in1=type_i[:],
                                     op0=ALU.mult, op1=ALU.add)
            dve.tensor_reduce(low_high[:, 0:1], dst_g[:], AX.X, ALU.min)
            link(dve.tensor_reduce(low_high[:, 1:2], dst_g[:], AX.X, ALU.max))
            link(dve.tensor_single_scalar(windows[:], low_high[:], 7, ALU.arith_shift_right))
            link(dve.tensor_copy(windows_f[:], windows[:]))
            dve.tensor_copy(table[:, 0:1], windows_f[:, 0:1])
            dve.scalar_tensor_tensor(out=table[:, 1:2], in0=windows_f[:, 1:2], scalar=1.0,
                                     in1=windows_f[:, 0:1], op0=ALU.add, op1=ALU.subtract).then_inc(counted, 1)
            dve.wait_ge(summed, 1)
            link(dve.tensor_copy(table[:, 2:3], steps_psum[0:NG, 0:1]))
            dve.tensor_copy(table_i[:], table[:]).then_inc(stepped, 1)

        @block.tensor
        def _(pe):
            pe.wait_ge(filled, 2)
            pe.wait_ge(counted, 1)
            pe.matmul(steps_psum[0:NG, 0:1], earlier[:], table[:, 1:2], start=True, stop=True).then_inc(summed, 1)


def transform_by_relation(nc, st, ins):
    KC = D // P
    PAIRS = RELS // 2
    with ExitStack() as ctx:
        phase_end(nc, ctx)
        def sb(name, shape, dt):
            return ctx.enter_context(nc.sbuf_tensor("rel_" + name, shape, dt))

        def sem(name):
            return phase_semaphore(nc, ctx, "rel_" + name)

        weights = sb("weights", [P, KC, RELS * D], F32)
        x_t = sb("x_t", [P, 2, KC, P], F32)
        rows = sb("rows", [P, 2, RELS * D], F32)
        banks = [ctx.enter_context(nc.psum_tensor(f"rel_pair{b}", [P, 2 * D], F32)) for b in range(PAIRS)]
        w_in, x_in0, x_in1, paired, out_act, out_dve = (
            sem(n) for n in ("w_in", "x_in0", "x_in1", "paired", "out_act", "out_dve"))
        x_in = [x_in0, x_in1]
        stored = [sem("stored0"), sem("stored1")]
        x_sb_in = sem("x_sb_in")
        turn = sem("turn")
        block = ctx.enter_context(nc.Block())

        @block.sync
        def _(sp):
            for k in range(KC):
                sp.dma_start(weights[:, k, :].rearrange("k (r o) -> k r o", r=RELS),
                             ins["L0_weight"].rearrange("r (c k) o -> c k r o", c=KC)[k]).then_inc(w_in, 16)
            sp.dma_start(st.x[:].rearrange("p (w f) -> p w f", w=NW),
                         ins["x"].rearrange("(w p) f -> p w f", p=P)).then_inc(x_sb_in, 16)
            with sp.Fori(0, HW) as it:
                for h in range(2):
                    sp.wait_ge(paired, PAIRS * (2 * it + h) + PAIRS)
                    sp.dma_start(x_t[:, h, :, :],
                                 ins["x_t"].rearrange("(c k) n -> k c n", c=KC)[:, :, bass.ds((2 * it + h) * P, P)]
                                 ).then_inc(x_in[h], 16)
            sp.wait_ge(x_sb_in, 16)

        @block.tensor
        def _(pe):
            pe.sem_inc(paired, 2 * PAIRS)
            pe.wait_ge(w_in, KC * 16)
            with pe.Fori(0, HW) as it:
                for h in range(2):
                    pe.wait_ge(x_in[h], 16 * it + 16)
                    for b in range(PAIRS):
                        pe.wait_ge([out_act, out_dve][b % 2], (2 * it + h) * (PAIRS // 2) + b // 2 + 1)
                        for k in range(KC):
                            last = pe.matmul(banks[b][:], x_t[:, h, k, :], weights[:, k, 2 * D * b:2 * D * (b + 1)],
                                             start=(k == 0), stop=(k == KC - 1))
                        last.then_inc(paired, 1)

        @block.scalar
        def _(act):
            act.sem_inc(out_act, PAIRS // 2)
            act.sem_inc(stored[0], 16)
            act.sem_inc(stored[1], 16)
            with act.Fori(0, HW) as it:
                for h in range(2):
                    act.wait_ge(stored[h], 16 * it + 16)
                    for b in range(0, PAIRS, 2):
                        act.wait_ge(paired, PAIRS * (2 * it + h + 2) + b + 1)
                        act.activation(rows[:, h, 2 * D * b:2 * D * (b + 1)], banks[b][:], ACT.Copy).then_inc(out_act, 1)
                    act.wait_ge(out_act, (2 * it + h + 2) * (PAIRS // 2))
                    act.wait_ge(out_dve, (2 * it + h + 2) * (PAIRS // 2))
                    act.sem_inc(turn, 1)
                    act.dma_start(st.rel_rows.rearrange("(n r) f -> n (r f)", r=RELS)[bass.ds((2 * it + h) * P, P), :],
                                  rows[:, h, :]).then_inc(stored[h], 16)
            for h in range(2):
                act.wait_ge(stored[h], 16 * (HW + 1))

        @block.vector
        def _(dve):
            dve.sem_inc(out_dve, PAIRS // 2)
            with dve.Fori(0, HW) as it:
                for h in range(2):
                    dve.wait_ge(stored[h], 16 * it + 16)
                    for b in range(1, PAIRS, 2):
                        dve.wait_ge(paired, PAIRS * (2 * it + h + 2) + b + 1)
                        dve.tensor_copy(rows[:, h, 2 * D * b:2 * D * (b + 1)], banks[b][:]).then_inc(out_dve, 1)


def aggregate(nc, st, name, table, index, weight):
    width = D if weight is None else D + 1
    with ExitStack() as ctx:
        phase_end(nc, ctx)
        def sem(part):
            return phase_semaphore(nc, ctx, name + part)

        ring = ctx.enter_context(nc.sbuf_tensor(name + "ring", [P, RING, D], F32))
        stage = ctx.enter_context(nc.sbuf_tensor(name + "stage", [P, RING], I32))
        onehot = ctx.enter_context(nc.sbuf_tensor(name + "onehot", [P, GROUP, P], F32))
        rows = ring if weight is None else ctx.enter_context(nc.sbuf_tensor(name + "rows", [P, RING, D + 4], F32))
        total = ctx.enter_context(nc.psum_tensor(name + "total", [P, 512], F32))
        arrived = [sem(f"arrived{k}") for k in range(RING)]
        staged, hot, hot_used, added, group_done, scaled, turn, ones_set = (
            sem(n) for n in ("staged", "hot", "hot_used", "added", "group_done", "scaled", "turn", "ones_set"))
        block = ctx.enter_context(nc.Block())

        @block.gpsimd
        def _(pool):
            if weight is not None:
                pool.memset(rows[:, :, D:D + 1], 1.0).then_inc(ones_set, 1)
            with pool.Fori(0, HG) as it:
                for h in range(2):
                    pool.wait_ge(group_done, 2 * it + h + 1)
                    pool.sem_inc(turn, 1)
                    pool.tensor_copy(stage[:, GROUP * h:GROUP * (h + 1)],
                                     index[:, bass.ds((2 * it + h) * GROUP, GROUP)]).then_inc(staged, 1)
                    pool.wait_ge(staged, 2 * it + h + 1)
                    pool.sem_inc(turn, 1)
                    for k in range(GROUP * h, GROUP * (h + 1)):
                        pool.indirect_dma_start(ring[:, k, :], None, table,
                                                bass.IndirectOffsetOnAxis(ap=stage[:, k:k + 1], axis=0)
                                                ).then_inc(arrived[k], 16)

        if weight is not None:
            @block.scalar
            def _(act):
                with act.Fori(0, HG) as it:
                    for h in range(2):
                        act.wait_ge(group_done, 2 * it + h + 1)
                        for k in range(GROUP * h, GROUP * (h + 1)):
                            act.wait_ge(arrived[k], 16 * it + 16)
                            act.sem_inc(turn, 1)
                            act.activation(rows[:, k, 0:D], ring[:, k, :], ACT.Copy,
                                           scale=weight[:, bass.ds(it * RING + k, 1)]).then_inc(scaled, 1)

        @block.vector
        def _(dve):
            dve.sem_inc(added, 1)
            with dve.Fori(0, HG) as it:
                for h in range(2):
                    first, count, before = group_range(nc, dve, st, 2 * it + h)
                    with dve.Fori(0, count) as j:
                        window = within(nc, first + j, NW - 1)
                        step = before + j
                        for k in range(GROUP):
                            dve.wait_ge(hot_used, GROUP * step + k + 1)
                            dve.tensor_scalar(onehot[:, k, :], st.iota[:], st.window_start[:, bass.ds(window, 1)],
                                              st.dst[:, bass.ds(it * RING + GROUP * h + k, 1)],
                                              ALU.add, ALU.is_equal).then_inc(hot, 1)
                        dve.wait_ge(hot_used, GROUP * step + 2 * GROUP)
                        here = st.acc[:, bass.ds(window * WIDE, width)]
                        dve.tensor_tensor(here, here, total[:, 0:width], ALU.add).then_inc(added, 1)

        @block.tensor
        def _(pe):
            pe.sem_inc(hot_used, GROUP)
            pe.sem_inc(group_done, 2)
            if weight is not None:
                pe.wait_ge(ones_set, 1)
            with pe.Fori(0, HG) as it:
                for h in range(2):
                    _, count, before = group_range(nc, pe, st, 2 * it + h)
                    if weight is None:
                        for k in range(GROUP * h, GROUP * (h + 1)):
                            pe.wait_ge(arrived[k], 16 * it + 16)
                    else:
                        pe.wait_ge(scaled, RING * it + GROUP * (h + 1))
                    pe.sem_inc(turn, 1)
                    with pe.Fori(0, count) as j:
                        step = before + j
                        pe.wait_ge(added, step + 1)
                        for k in range(GROUP):
                            pe.wait_ge(hot, GROUP * step + k + 1)
                            pe.matmul(total[:, 0:width], onehot[:, k, :], rows[:, GROUP * h + k, 0:width],
                                      start=(k == 0), stop=(k == GROUP - 1)).then_inc(hot_used, 1)
                    pe.drain().then_inc(group_done, 1)


def layer_norm(nc, st, name, source, stride, column=0, out=None, out_column=0, gamma_beta=None):
    out, out_stride = (st.x, D) if out is None else (out, WIDE)
    with ExitStack() as ctx:
        phase_end(nc, ctx)
        def sb(part, shape):
            return ctx.enter_context(nc.sbuf_tensor(name + part, shape, F32))

        def sem(part):
            return phase_semaphore(nc, ctx, name + part)

        stats, total, diff, square, std = sb("stats", [P, NW, 6]), sb("total", [P, NW]), sb("diff", [P, NW]), \
            sb("square", [P, NW]), sb("std", [P, NW])
        mean, var, rstd = sb("mean", [P, NW]), sb("var", [P, NW]), sb("rstd", [P, NW])
        counted, chain, var_set, rooted, normed = (sem(n) for n in ("counted", "chain", "var_set", "rooted", "normed"))
        loaded = sem("loaded")
        if gamma_beta is not None:
            gamma, beta = sb("gamma", [P, D]), sb("beta", [P, D])
        block = ctx.enter_context(nc.Block())

        if gamma_beta is not None:
            @block.sync
            def _(sp):
                sp.dma_start(gamma[:], gamma_beta[0].partition_broadcast(P)).then_inc(loaded, 16)
                sp.dma_start(beta[:], gamma_beta[1].partition_broadcast(P)).then_inc(loaded, 16)
                sp.wait_ge(loaded, 32)

        @block.vector
        def _(dve):
            done = [0]

            def link(ins_):
                done[0] += 1
                ins_.then_inc(chain, 1)
                dve.wait_ge(chain, done[0])

            with dve.Fori(0, NW) as w:
                dve.bn_stats(stats[:, :, :].rearrange("p w s -> p (w s)")[:, bass.ds(6 * w, 6)],
                             source[:, bass.ds(stride * w + column, D)]).then_inc(counted, 1)
            dve.wait_ge(counted, NW)
            dve.tensor_tensor(total[:], stats[:, :, 1], stats[:, :, 4], ALU.add)
            dve.tensor_tensor(square[:], stats[:, :, 2], stats[:, :, 5], ALU.add)
            link(dve.tensor_tensor(diff[:], stats[:, :, 1], stats[:, :, 4], ALU.subtract))
            dve.tensor_single_scalar(mean[:], total[:], 0.5, ALU.mult)
            link(dve.scalar_tensor_tensor(out=diff[:], in0=diff[:], scalar=0.25, in1=diff[:], op0=ALU.mult, op1=ALU.mult))
            link(dve.scalar_tensor_tensor(out=var[:], in0=square[:], scalar=1.0 / D, in1=diff[:], op0=ALU.mult, op1=ALU.add))
            dve.tensor_single_scalar(var[:], var[:], EPS, ALU.add).then_inc(var_set, 1)
            dve.wait_ge(rooted, 1)
            link(dve.reciprocal(rstd[:], std[:]))
            with dve.Fori(0, NW) as w:
                dve.tensor_scalar(out[:, bass.ds(out_stride * w + out_column, D)], source[:, bass.ds(stride * w + column, D)],
                                  mean[:, bass.ds(w, 1)], rstd[:, bass.ds(w, 1)], ALU.subtract, ALU.mult).then_inc(normed, 1)
            dve.wait_ge(normed, NW)
            if gamma_beta is not None:
                dve.wait_ge(loaded, 32)
                view = out[:].rearrange("p (w f) -> p w f", w=NW)[:, :, out_column:out_column + D]
                link(dve.tensor_tensor(view, view, gamma[:].unsqueeze(1).broadcast_to([P, NW, D]), ALU.mult))
                link(dve.tensor_tensor(view, view, beta[:].unsqueeze(1).broadcast_to([P, NW, D]), ALU.add))

        @block.scalar
        def _(act):
            act.wait_ge(var_set, 1)
            act.activation(std[:], var[:], ACT.Sqrt).then_inc(rooted, 1)


def scale_to_table(nc, st, name, table):
    with ExitStack() as ctx:
        phase_end(nc, ctx)
        def sem(part):
            return phase_semaphore(nc, ctx, name + part)

        scaled, stored, chain, rooted = (sem(n) for n in ("scaled", "stored", "chain", "rooted"))
        std = ctx.enter_context(nc.sbuf_tensor(name + "std", [P, NW], F32))
        block = ctx.enter_context(nc.Block())

        @block.vector
        def _(dve):
            acc = st.acc[:].rearrange("p (w f) -> p w f", w=NW)
            dve.tensor_copy(st.in_edges[:], acc[:, :, D]).then_inc(chain, 1)
            dve.tensor_single_scalar(st.degree[:], acc[:, :, D], 1.0, ALU.add).then_inc(chain, 1)
            dve.wait_ge(rooted, 1)
            dve.reciprocal(st.dinv[:], std[:]).then_inc(chain, 1)
            dve.wait_ge(chain, 3)
            with dve.Fori(0, NW) as w:
                dve.tensor_scalar(st.acc[:, bass.ds(WIDE * w, D)], st.x[:, bass.ds(D * w, D)],
                                  st.dinv[:, bass.ds(w, 1)], None, ALU.mult).then_inc(scaled, 1)

        @block.scalar
        def _(act):
            act.wait_ge(chain, 2)
            act.activation(std[:], st.degree[:], ACT.Sqrt).then_inc(rooted, 1)

        @block.sync
        def _(sp):
            sp.wait_ge(scaled, NW)
            sp.dma_start(table.rearrange("(w p) f -> p w f", p=P),
                         st.acc[:].rearrange("p (w f) -> p w f", w=NW)[:, :, 0:D]).then_inc(stored, 16)
            sp.wait_ge(stored, 16)


def layer1_nodes(nc, st, ins):
    KC = D // P
    with ExitStack() as ctx:
        phase_end(nc, ctx)
        def sb(name, shape):
            return ctx.enter_context(nc.sbuf_tensor("l1_" + name, shape, F32))

        def psum(name):
            return [ctx.enter_context(nc.psum_tensor(f"l1_{name}{h}", [P, 512], F32)) for h in range(2)]

        def sem(name):
            return phase_semaphore(nc, ctx, "l1_" + name)

        w1, w2, b1 = sb("w1", [P, KC, HID1]), sb("w2", [HR, HC, D]), sb("b1", [HR, HC])
        y, y_t, z_t = sb("y", [P, 2, D]), sb("y_t", [P, 2, KC, P]), sb("z_t", [HR, 2, HC, P])
        turned, hidden, back = psum("turned"), psum("hidden"), psum("back")
        loaded, y_set, y_turned, y_t_set, z_sum, z_set, back_sum, acc_set, stored = (
            sem(n) for n in ("loaded", "y_set", "y_turned", "y_t_set", "z_sum", "z_set", "back_sum", "acc_set", "stored"))
        turn = sem("turn")
        block = ctx.enter_context(nc.Block())

        @block.sync
        def _(sp):
            sp.dma_start(w1[:], ins["L1_w1"].rearrange("(c k) h -> k c h", c=KC)).then_inc(loaded, 16)
            sp.dma_start(w2[:], ins["L1_w2"].rearrange("(c k) f -> k c f", c=HC)).then_inc(loaded, 16)
            sp.dma_start(b1[:], ins["L1_b1"].rearrange("(c k) -> k c", c=HC), allow_slow_non_contiguous=True).then_inc(loaded, 16)
            sp.wait_ge(loaded, 48)
            sp.wait_ge(acc_set, NW + 2)
            sp.dma_start(st.table2.rearrange("(w p) f -> p w f", p=P),
                         st.acc[:].rearrange("p (w f) -> p w f", w=NW)[:, :, 0:D]).then_inc(stored, 16)
            sp.wait_ge(stored, 16)

        @block.vector
        def _(dve):
            dve.sem_inc(acc_set, 2)
            with dve.Fori(0, HW) as it:
                for h in range(2):
                    dve.wait_ge(y_turned, 2 * it + h + 1)
                    dve.tensor_scalar(y[:, h, :], st.acc[:, bass.ds((2 * it + h) * WIDE, D)],
                                      st.dinv[:, bass.ds(2 * it + h, 1)], None, ALU.mult).then_inc(y_set, 1)
                for h in range(2):
                    dve.wait_ge(back_sum, 2 * it + h + 3)
                    dve.tensor_scalar(st.acc[:, bass.ds((2 * it + h) * WIDE, D)], back[h][:, 0:D],
                                      st.dinv[:, bass.ds(2 * it + h, 1)], None, ALU.mult).then_inc(acc_set, 1)

        @block.tensor
        def _(pe):
            pe.sem_inc(y_turned, 2)
            pe.sem_inc(back_sum, 2)
            pe.wait_ge(loaded, 48)
            with pe.Fori(0, HW) as it:
                for h in range(2):
                    pe.wait_ge(y_set, 2 * it + h + 1)
                    for k in range(KC):
                        last = pe.transpose(turned[h][:, k * P:(k + 1) * P], y[:, h, k * P:(k + 1) * P], st.ident[:])
                    last.then_inc(y_turned, 1)
                for h in range(2):
                    pe.wait_ge(y_t_set, 2 * it + h + 1)
                    for c in range(HC):
                        for k in range(KC):
                            last = pe.matmul(hidden[h][0:HR, c * P:(c + 1) * P], w1[:, k, c * HR:(c + 1) * HR],
                                             y_t[:, h, k, :], start=(k == 0), stop=(k == KC - 1))
                    last.then_inc(z_sum, 1)
                for h in range(2):
                    pe.wait_ge(z_set, 2 * it + h + 1)
                    pe.wait_ge(acc_set, 2 * it + h + 1)
                    for c in range(HC):
                        last = pe.matmul(back[h][:, 0:D], z_t[:, h, c, :], w2[:, c, :], start=(c == 0), stop=(c == HC - 1))
                    last.then_inc(back_sum, 1)

        @block.scalar
        def _(act):
            with act.Fori(0, HW) as it:
                for h in range(2):
                    act.wait_ge(y_turned, 2 * it + h + 3)
                    act.activation(y_t[:, h, :, :], turned[h][:, 0:D].rearrange("p (k n) -> p k n", k=KC), ACT.Copy
                                   ).then_inc(y_t_set, 1)
                for h in range(2):
                    act.wait_ge(z_sum, 2 * it + h + 1)
                    act.wait_ge(back_sum, 2 * it + h + 1)
                    for c in range(HC):
                        last = act.activation(z_t[:, h, c, :], hidden[h][0:HR, c * P:(c + 1) * P], ACT.Relu,
                                              bias=b1[:, c:c + 1])
                    last.then_inc(z_set, 1)


def layer1_end(nc, st, ins):
    with ExitStack() as ctx:
        phase_end(nc, ctx)
        b2 = ctx.enter_context(nc.sbuf_tensor("l1_b2", [P, D], F32))
        loaded, added = (phase_semaphore(nc, ctx, "l1_end_" + n) for n in ("loaded", "added"))
        block = ctx.enter_context(nc.Block())

        @block.sync
        def _(sp):
            sp.dma_start(b2[:], ins["L1_b2"].partition_broadcast(P)).then_inc(loaded, 16)
            sp.wait_ge(loaded, 16)

        @block.vector
        def _(dve):
            acc = st.acc[:].rearrange("p (w f) -> p w f", w=NW)[:, :, 0:D]
            with dve.Fori(0, NW) as w:
                here = st.acc[:, bass.ds(WIDE * w, D)]
                dve.scalar_tensor_tensor(out=here, in0=here, scalar=st.dinv[:, bass.ds(w, 1)],
                                         in1=st.x[:, bass.ds(D * w, D)], op0=ALU.mult, op1=ALU.add).then_inc(added, 1)
            dve.wait_ge(added, NW)
            dve.wait_ge(loaded, 16)
            dve.tensor_tensor(acc, acc, b2[:].unsqueeze(1).broadcast_to([P, NW, D]), ALU.add).then_inc(added, 1)


def layer1(nc, st, ins):
    scale_to_table(nc, st, "l1_scale_", st.table1)
    aggregate(nc, st, "l1a_", st.table1, st.src, None)
    layer1_nodes(nc, st, ins)
    aggregate(nc, st, "l1b_", st.table2, st.src, None)
    layer1_end(nc, st, ins)
    layer_norm(nc, st, "ln1_", st.acc, WIDE)


def layer2_tables(nc, st, ins):
    KC = D // P
    with ExitStack() as ctx:
        phase_end(nc, ctx)
        def sb(name, shape):
            return ctx.enter_context(nc.sbuf_tensor("l2t_" + name, shape, F32))

        def psum(name):
            return [ctx.enter_context(nc.psum_tensor(f"l2t_{name}{h}", [P, 512], F32)) for h in range(2)]

        def sem(name):
            return phase_semaphore(nc, ctx, "l2t_" + name)

        w_nodes, b1 = sb("w_nodes", [P, 2 * KC, HID2]), sb("b1", [P, HID2])
        x, x_t, rows = sb("x", [P, 2, D]), sb("x_t", [P, 2, KC, P]), sb("rows", [P, 2, 2 * HID2])
        turned, of_src, of_dst = psum("turned"), psum("of_src"), psum("of_dst")
        loaded, x_set, x_turned, x_t_set, src_sum, dst_sum, src_out, dst_out, cleared = (
            sem(n) for n in ("loaded", "x_set", "x_turned", "x_t_set", "src_sum", "dst_sum", "src_out", "dst_out", "cleared"))
        stored = [sem("stored0"), sem("stored1")]
        turn = sem("turn")
        block = ctx.enter_context(nc.Block())

        @block.sync
        def _(sp):
            sp.dma_start(w_nodes[:], ins["L2_eW1"][0:2 * D, :].rearrange("(c k) h -> k c h", k=P)).then_inc(loaded, 16)
            sp.dma_start(b1[:], ins["L2_eb1"].partition_broadcast(P)).then_inc(loaded, 16)
            sp.sem_inc(stored[0], 16)
            sp.sem_inc(stored[1], 16)
            sp.wait_ge(loaded, 32)
            with sp.Fori(0, HW) as it:
                for h in range(2):
                    sp.wait_ge(src_out, 2 * it + h + 3)
                    sp.wait_ge(dst_out, 2 * it + h + 3)
                    here = bass.ds((2 * it + h) * P, P)
                    sp.dma_start(st.src_rows[here, :], rows[:, h, 0:HID2]).then_inc(stored[h], 16)
                    sp.dma_start(st.dst_rows[here, :], rows[:, h, HID2:2 * HID2]).then_inc(stored[h], 16)
            for h in range(2):
                sp.wait_ge(stored[h], 32 * HW + 16)

        @block.gpsimd
        def _(pool):
            pool.memset(st.acc[:], 0.0).then_inc(cleared, 1)

        @block.scalar
        def _(act):
            act.sem_inc(src_out, 2)
            with act.Fori(0, HW) as it:
                for h in range(2):
                    act.wait_ge(x_turned, 2 * it + h + 1)
                    act.sem_inc(turn, 1)
                    act.activation(x[:, h, :], st.x[:, bass.ds((2 * it + h) * D, D)], ACT.Copy).then_inc(x_set, 1)
                for h in range(2):
                    act.wait_ge(x_turned, 2 * it + h + 3)
                    act.wait_ge(dst_sum, 2 * it + h + 1)
                    act.activation(x_t[:, h, :, :], turned[h][:, 0:D].rearrange("p (k n) -> p k n", k=KC), ACT.Copy
                                   ).then_inc(x_t_set, 1)
                for h in range(2):
                    act.wait_ge(src_sum, 2 * it + h + 1)
                    act.wait_ge(stored[h], 32 * it + 16)
                    act.activation(rows[:, h, 0:HID2], of_src[h][:], ACT.Copy).then_inc(src_out, 1)

        @block.vector
        def _(dve):
            dve.sem_inc(dst_out, 2)
            dve.wait_ge(loaded, 32)
            with dve.Fori(0, HW) as it:
                for h in range(2):
                    dve.wait_ge(dst_sum, 2 * it + h + 3)
                    dve.wait_ge(stored[h], 32 * it + 16)
                    dve.tensor_tensor(rows[:, h, HID2:2 * HID2], of_dst[h][:], b1[:], ALU.add).then_inc(dst_out, 1)

        @block.tensor
        def _(pe):
            pe.sem_inc(x_turned, 2)
            pe.sem_inc(dst_sum, 2)
            pe.wait_ge(loaded, 32)
            with pe.Fori(0, HW) as it:
                for h in range(2):
                    pe.wait_ge(x_set, 2 * it + h + 1)
                    for k in range(KC):
                        last = pe.transpose(turned[h][:, k * P:(k + 1) * P], x[:, h, k * P:(k + 1) * P], st.ident[:])
                    last.then_inc(x_turned, 1)
                for h in range(2):
                    pe.wait_ge(x_t_set, 2 * it + h + 1)
                    pe.wait_ge(src_out, 2 * it + h + 1)
                    pe.wait_ge(dst_out, 2 * it + h + 1)
                    for part, bank, summed in ((0, of_src, src_sum), (1, of_dst, dst_sum)):
                        for k in range(KC):
                            last = pe.matmul(bank[h][:], x_t[:, h, k, :], w_nodes[:, KC * part + k, :],
                                             start=(k == 0), stop=(k == KC - 1))
                        last.then_inc(summed, 1)


def layer2_edges(nc, st, ins):
    with ExitStack() as ctx:
        phase_end(nc, ctx)
        def sb(name, shape, dt=F32):
            return ctx.enter_context(nc.sbuf_tensor("l2e_" + name, shape, dt))

        def sem(name):
            return phase_semaphore(nc, ctx, "l2e_" + name)

        w_edge, attr_t = sb("w_edge", [EDIM, HID2]), sb("attr_t", [EDIM, 2, GROUP * P])
        from_src, from_dst, hidden = (sb(n, [P, RING, HID2]) for n in ("from_src", "from_dst", "hidden"))
        stage_src, stage_dst = sb("stage_src", [P, RING], I32), sb("stage_dst", [P, RING], I32)
        onehot = sb("onehot", [P, GROUP, P])
        edge_sum = [ctx.enter_context(nc.psum_tensor(f"l2e_edge_sum{k}", [P, HID2], F32)) for k in range(GROUP)]
        total = ctx.enter_context(nc.psum_tensor("l2e_total", [P, HID2], F32))
        src_in = [sem(f"src_in{k}") for k in range(RING)]
        dst_in = [sem(f"dst_in{k}") for k in range(RING)]
        attr_in = [sem("attr_in0"), sem("attr_in1")]
        w_in, staged, attr_summed, half_added, all_added, relued, hot, hot_used, added, group_done, turn = (
            sem(n) for n in ("w_in", "staged", "attr_summed", "half_added", "all_added", "relued", "hot", "hot_used",
                             "added", "group_done", "turn"))
        block = ctx.enter_context(nc.Block())

        @block.sync
        def _(sp):
            sp.dma_start(w_edge[:], ins["L2_eW1"][2 * D:2 * D + EDIM, :]).then_inc(w_in, 16)
            with sp.Fori(0, HG) as it:
                for h in range(2):
                    sp.wait_ge(group_done, 2 * it + h + 1)
                    sp.dma_start(attr_t[:, h, :], ins["edge_attr_t"][:, bass.ds((2 * it + h) * GROUP * P, GROUP * P)]
                                 ).then_inc(attr_in[h], 16)
            sp.wait_ge(w_in, 16)

        @block.gpsimd
        def _(pool):
            with pool.Fori(0, HG) as it:
                for h in range(2):
                    half = slice(GROUP * h, GROUP * (h + 1))
                    pool.wait_ge(group_done, 2 * it + h + 1)
                    pool.sem_inc(turn, 1)
                    for stage, index in ((stage_src, st.src), (stage_dst, st.dst_row)):
                        pool.tensor_copy(stage[:, half], index[:, bass.ds((2 * it + h) * GROUP, GROUP)]).then_inc(staged, 1)
                    pool.wait_ge(staged, 4 * it + 2 * h + 2)
                    pool.sem_inc(turn, 1)
                    for k in range(GROUP * h, GROUP * (h + 1)):
                        for ring, stage, table, arrived in ((from_src, stage_src, st.src_rows, src_in),
                                                            (from_dst, stage_dst, st.dst_rows, dst_in)):
                            pool.indirect_dma_start(ring[:, k, :], None, table,
                                                    bass.IndirectOffsetOnAxis(ap=stage[:, k:k + 1], axis=0)
                                                    ).then_inc(arrived[k], 16)

        @block.scalar
        def _(act):
            with act.Fori(0, HG) as it:
                for k in range(RING):
                    act.wait_ge(all_added, RING * it + k + 1)
                    act.activation(hidden[:, k, :], hidden[:, k, :], ACT.Relu).then_inc(relued, 1)

        @block.vector
        def _(dve):
            dve.sem_inc(added, 1)
            with dve.Fori(0, HG) as it:
                for h in range(2):
                    for k in range(GROUP * h, GROUP * (h + 1)):
                        dve.wait_ge(attr_summed, RING * it + k + 1)
                        dve.wait_ge(src_in[k], 16 * it + 16)
                        dve.tensor_tensor(hidden[:, k, :], edge_sum[k % GROUP][:], from_src[:, k, :], ALU.add
                                          ).then_inc(half_added, 1)
                    for k in range(GROUP * h, GROUP * (h + 1)):
                        dve.wait_ge(half_added, RING * it + k + 1 + GROUP)
                        dve.wait_ge(dst_in[k], 16 * it + 16)
                        dve.tensor_tensor(hidden[:, k, :], hidden[:, k, :], from_dst[:, k, :], ALU.add
                                          ).then_inc(all_added, 1)
                    first, count, before = group_range(nc, dve, st, 2 * it + h)
                    with dve.Fori(0, count) as j:
                        window = within(nc, first + j, NW - 1)
                        step = before + j
                        for k in range(GROUP):
                            dve.wait_ge(hot_used, GROUP * step + k + 1)
                            dve.tensor_scalar(onehot[:, k, :], st.iota[:], st.window_start[:, bass.ds(window, 1)],
                                              st.dst[:, bass.ds(it * RING + GROUP * h + k, 1)],
                                              ALU.add, ALU.is_equal).then_inc(hot, 1)
                        dve.wait_ge(hot_used, GROUP * step + 2 * GROUP)
                        here = st.acc[:, bass.ds(window * WIDE, HID2)]
                        dve.tensor_tensor(here, here, total[:], ALU.add).then_inc(added, 1)

        @block.tensor
        def _(pe):
            pe.sem_inc(hot_used, GROUP)
            pe.sem_inc(group_done, 2)
            pe.sem_inc(half_added, GROUP)
            pe.wait_ge(w_in, 16)
            with pe.Fori(0, HG) as it:
                for h in range(2):
                    _, count, before = group_range(nc, pe, st, 2 * it + h)
                    pe.wait_ge(attr_in[h], 16 * it + 16)
                    for k in range(GROUP):
                        pe.wait_ge(half_added, RING * it + GROUP * h + k + 1)
                        pe.matmul(edge_sum[k][:], attr_t[:, h, k * P:(k + 1) * P], w_edge[:],
                                  start=True, stop=True).then_inc(attr_summed, 1)
                    pe.wait_ge(relued, RING * it + GROUP * (h + 1))
                    pe.sem_inc(turn, 1)
                    with pe.Fori(0, count) as j:
                        step = before + j
                        pe.wait_ge(added, step + 1)
                        for k in range(GROUP):
                            pe.wait_ge(hot, GROUP * step + k + 1)
                            pe.matmul(total[:], onehot[:, k, :], hidden[:, GROUP * h + k, :],
                                      start=(k == 0), stop=(k == GROUP - 1)).then_inc(hot_used, 1)
                    pe.drain().then_inc(group_done, 1)


def layer2_nodes(nc, st, ins):
    KC, HCH = D // P, HID2 // P
    with ExitStack() as ctx:
        phase_end(nc, ctx)
        def sb(name, shape):
            return ctx.enter_context(nc.sbuf_tensor("l2n_" + name, shape, F32))

        def psum(name):
            return [ctx.enter_context(nc.psum_tensor(f"l2n_{name}{h}", [P, 512], F32)) for h in range(2)]

        def sem(name):
            return phase_semaphore(nc, ctx, "l2n_" + name)

        e_w2, n_w1, n_w2 = sb("e_w2", [P, HCH, D]), sb("n_w1", [P, 2 * KC, HID2]), sb("n_w2", [P, HCH, D])
        e_b2, n_b1, n_b2 = sb("e_b2", [P, D]), sb("n_b1", [P, HCH]), sb("n_b2", [P, D])
        sums, sums_t = sb("sums", [P, 2, HID2]), sb("sums_t", [P, 2, HCH, P])
        both, both_t = sb("both", [P, 2, 2 * D]), sb("both_t", [P, 2, 2 * KC, P])
        hidden_t = sb("hidden_t", [P, 2, HCH, P])
        sums_turned, both_turned, hidden = psum("sums_turned"), psum("both_turned"), psum("hidden")
        outs = psum("outs")
        (loaded, slots_set, turned_a, sums_t_set, agg_sum, agg_set, turned_b, both_t_set, hidden_sum, hidden_set,
         upd_sum, upd_set, turn) = (sem(n) for n in (
             "loaded", "slots_set", "turned_a", "sums_t_set", "agg_sum", "agg_set", "turned_b", "both_t_set",
             "hidden_sum", "hidden_set", "upd_sum", "upd_set", "turn"))
        LOADS = 6
        block = ctx.enter_context(nc.Block())

        @block.sync
        def _(sp):
            sp.dma_start(e_w2[:], ins["L2_eW2"].rearrange("(c k) f -> k c f", k=P)).then_inc(loaded, 16)
            sp.dma_start(n_w1[:], ins["L2_nW1"].rearrange("(c k) f -> k c f", k=P)).then_inc(loaded, 16)
            sp.dma_start(n_w2[:], ins["L2_nW2"].rearrange("(c k) f -> k c f", k=P)).then_inc(loaded, 16)
            sp.dma_start(n_b1[:], ins["L2_nb1"].rearrange("(c k) -> k c", k=P), allow_slow_non_contiguous=True).then_inc(loaded, 16)
            sp.dma_start(e_b2[:], ins["L2_eb2"].partition_broadcast(P)).then_inc(loaded, 16)
            sp.dma_start(n_b2[:], ins["L2_nb2"].partition_broadcast(P)).then_inc(loaded, 16)
            sp.wait_ge(loaded, LOADS * 16)

        @block.scalar
        def _(act):
            act.wait_ge(loaded, LOADS * 16)
            with act.Fori(0, HW) as it:
                for h in range(2):
                    act.wait_ge(turned_a, 2 * it + h + 1)
                    act.wait_ge(turned_b, 2 * it + h + 1)
                    act.sem_inc(turn, 1)
                    act.activation(sums[:, h, :], st.acc[:, bass.ds((2 * it + h) * WIDE, HID2)], ACT.Copy)
                    act.activation(both[:, h, 0:D], st.x[:, bass.ds((2 * it + h) * D, D)], ACT.Copy).then_inc(slots_set, 1)
                for h in range(2):
                    act.wait_ge(turned_a, 2 * it + h + 3)
                    act.wait_ge(agg_sum, 2 * it + h + 1)
                    act.activation(sums_t[:, h, :, :], sums_turned[h][:].rearrange("p (k n) -> p k n", k=HCH), ACT.Copy
                                   ).then_inc(sums_t_set, 1)
                for h in range(2):
                    act.wait_ge(turned_b, 2 * it + h + 3)
                    act.wait_ge(hidden_sum, 2 * it + h + 1)
                    act.activation(both_t[:, h, :, :], both_turned[h][:].rearrange("p (k n) -> p k n", k=2 * KC), ACT.Copy
                                   ).then_inc(both_t_set, 1)
                for h in range(2):
                    act.wait_ge(hidden_sum, 2 * it + h + 3)
                    act.wait_ge(upd_sum, 2 * it + h + 1)
                    for c in range(HCH):
                        last = act.activation(hidden_t[:, h, c, :], hidden[h][:, c * P:(c + 1) * P], ACT.Relu,
                                              bias=n_b1[:, c:c + 1])
                    last.then_inc(hidden_set, 1)

        @block.vector
        def _(dve):
            dve.sem_inc(upd_set, 2)
            dve.wait_ge(loaded, LOADS * 16)
            with dve.Fori(0, HW) as it:
                for h in range(2):
                    dve.wait_ge(agg_sum, 2 * it + h + 3)
                    dve.scalar_tensor_tensor(out=both[:, h, D:2 * D], in0=e_b2[:],
                                             scalar=st.in_edges[:, bass.ds(2 * it + h, 1)], in1=outs[h][:, 0:D],
                                             op0=ALU.mult, op1=ALU.add).then_inc(agg_set, 1)
                for h in range(2):
                    dve.wait_ge(upd_sum, 2 * it + h + 3)
                    dve.tensor_tensor(st.acc[:, bass.ds((2 * it + h) * WIDE, D)], outs[h][:, D:2 * D], n_b2[:], ALU.add
                                      ).then_inc(upd_set, 1)

        @block.tensor
        def _(pe):
            for credit in (turned_a, turned_b, agg_sum, hidden_sum, upd_sum):
                pe.sem_inc(credit, 2)
            pe.wait_ge(loaded, LOADS * 16)
            with pe.Fori(0, HW) as it:
                for h in range(2):
                    pe.wait_ge(slots_set, 2 * it + h + 1)
                    for k in range(HCH):
                        last = pe.transpose(sums_turned[h][:, k * P:(k + 1) * P], sums[:, h, k * P:(k + 1) * P], st.ident[:])
                    last.then_inc(turned_a, 1)
                for h in range(2):
                    pe.wait_ge(sums_t_set, 2 * it + h + 1)
                    pe.wait_ge(upd_set, 2 * it + h + 1)
                    for k in range(HCH):
                        last = pe.matmul(outs[h][:, 0:D], sums_t[:, h, k, :], e_w2[:, k, :],
                                         start=(k == 0), stop=(k == HCH - 1))
                    last.then_inc(agg_sum, 1)
                for h in range(2):
                    pe.wait_ge(agg_set, 2 * it + h + 1)
                    for k in range(2 * KC):
                        last = pe.transpose(both_turned[h][:, k * P:(k + 1) * P], both[:, h, k * P:(k + 1) * P], st.ident[:])
                    last.then_inc(turned_b, 1)
                for h in range(2):
                    pe.wait_ge(both_t_set, 2 * it + h + 1)
                    for c in range(HCH):
                        for k in range(2 * KC):
                            last = pe.matmul(hidden[h][:, c * P:(c + 1) * P], n_w1[:, k, c * P:(c + 1) * P],
                                             both_t[:, h, k, :], start=(k == 0), stop=(k == 2 * KC - 1))
                    last.then_inc(hidden_sum, 1)
                for h in range(2):
                    pe.wait_ge(hidden_set, 2 * it + h + 1)
                    for k in range(HCH):
                        last = pe.matmul(outs[h][:, D:2 * D], hidden_t[:, h, k, :], n_w2[:, k, :],
                                         start=(k == 0), stop=(k == HCH - 1))
                    last.then_inc(upd_sum, 1)


def add_x(nc, st, name, column):
    with ExitStack() as ctx:
        phase_end(nc, ctx)
        added = phase_semaphore(nc, ctx, name + "added")
        block = ctx.enter_context(nc.Block())

        @block.vector
        def _(dve):
            acc = st.acc[:].rearrange("p (w f) -> p w f", w=NW)[:, :, column:column + D]
            dve.tensor_tensor(acc, acc, st.x[:].rearrange("p (w f) -> p w f", w=NW), ALU.add).then_inc(added, 1)


def layer2(nc, st, ins):
    layer2_tables(nc, st, ins)
    layer2_edges(nc, st, ins)
    layer2_nodes(nc, st, ins)
    add_x(nc, st, "l2_first_", 0)
    layer_norm(nc, st, "ln2_", st.acc, WIDE, out=st.acc, out_column=D, gamma_beta=(ins["L2_ln_gamma"], ins["L2_ln_beta"]))
    add_x(nc, st, "l2_second_", D)
    layer_norm(nc, st, "ln3_", st.acc, WIDE, column=D)


def layer3_nodes(nc, st, ins):
    KC = D // P
    ROW = D + HEADS
    with ExitStack() as ctx:
        phase_end(nc, ctx)
        def sb(name, shape):
            return ctx.enter_context(nc.sbuf_tensor("l3n_" + name, shape, F32))

        def psum(name):
            return [ctx.enter_context(nc.psum_tensor(f"l3n_{name}{h}", [P, 512], F32)) for h in range(2)]

        def sem(name):
            return phase_semaphore(nc, ctx, "l3n_" + name)

        w, att = sb("w", [P, KC, D]), sb("att", [P, 2, D])
        x, x_t, scaled = sb("x", [P, 2, D]), sb("x_t", [P, 2, KC, P]), sb("scaled", [P, 2, 2, D])
        least, most = sb("least", [P, HEADS]), sb("most", [P, HEADS])
        turned, product = psum("turned"), psum("product")
        loaded, x_set, x_turned, x_t_set, summed, h_set, scaled_set, logits_set, chain, negated, reduced, rows_set, stored, turn = (
            sem(n) for n in ("loaded", "x_set", "x_turned", "x_t_set", "summed", "h_set", "scaled_set", "logits_set",
                             "chain", "negated", "reduced", "rows_set", "stored", "turn"))
        block = ctx.enter_context(nc.Block())
        acc = st.acc[:].rearrange("p (w f) -> p w f", w=NW)
        logits = st.logits[:].rearrange("p (w c) -> p w c", w=NW)

        @block.sync
        def _(sp):
            sp.dma_start(w[:], ins["L3_W"].rearrange("(c k) f -> k c f", k=P)).then_inc(loaded, 16)
            sp.dma_start(att[:, 0, :], ins["L3_att_src"].rearrange("h c -> (h c)").partition_broadcast(P)).then_inc(loaded, 16)
            sp.dma_start(att[:, 1, :], ins["L3_att_dst"].rearrange("h c -> (h c)").partition_broadcast(P)).then_inc(loaded, 16)
            sp.wait_ge(loaded, 48)
            sp.wait_ge(rows_set, 2)
            sp.dma_start(st.gat_rows.rearrange("(w p) f -> p w f", p=P), acc[:, :, 0:ROW]).then_inc(stored, 16)
            sp.dma_start(st.gat_logits.rearrange("(w p) f -> p w f", p=P),
                         st.maxima[:].rearrange("p (w c) -> p w c", w=NW)).then_inc(stored, 16)
            sp.wait_ge(stored, 32)

        @block.scalar
        def _(act):
            with act.Fori(0, HW) as it:
                for h in range(2):
                    act.wait_ge(x_turned, 2 * it + h + 1)
                    act.sem_inc(turn, 1)
                    act.activation(x[:, h, :], st.x[:, bass.ds((2 * it + h) * D, D)], ACT.Copy).then_inc(x_set, 1)
                for h in range(2):
                    act.wait_ge(x_turned, 2 * it + h + 3)
                    act.wait_ge(summed, 2 * it + h + 1)
                    act.activation(x_t[:, h, :, :], turned[h][:, 0:D].rearrange("p (k n) -> p k n", k=KC), ACT.Copy
                                   ).then_inc(x_t_set, 1)

        @block.tensor
        def _(pe):
            pe.sem_inc(x_turned, 2)
            pe.sem_inc(summed, 2)
            pe.wait_ge(loaded, 48)
            with pe.Fori(0, HW) as it:
                for h in range(2):
                    pe.wait_ge(x_set, 2 * it + h + 1)
                    for k in range(KC):
                        last = pe.transpose(turned[h][:, k * P:(k + 1) * P], x[:, h, k * P:(k + 1) * P], st.ident[:])
                    last.then_inc(x_turned, 1)
                for h in range(2):
                    pe.wait_ge(x_t_set, 2 * it + h + 1)
                    pe.wait_ge(scaled_set, 2 * it + h + 1)
                    for k in range(KC):
                        last = pe.matmul(product[h][:, 0:D], x_t[:, h, k, :], w[:, k, :], start=(k == 0), stop=(k == KC - 1))
                    last.then_inc(summed, 1)

        @block.vector
        def _(dve):
            dve.sem_inc(scaled_set, 2)
            dve.wait_ge(loaded, 48)
            with dve.Fori(0, HW) as it:
                for h in range(2):
                    dve.wait_ge(summed, 2 * it + h + 3)
                    dve.sem_inc(turn, 1)
                    dve.tensor_copy(st.acc[:, bass.ds((2 * it + h) * WIDE, D)], product[h][:, 0:D]).then_inc(h_set, 1)
                    dve.wait_ge(logits_set, 2 * it + h + 1)
                    dve.tensor_tensor(scaled[:, h, :, :], product[h][:, 0:D].unsqueeze(1).broadcast_to([P, 2, D]), att[:], ALU.mult
                                      ).then_inc(scaled_set, 1)
                for h in range(2):
                    dve.wait_ge(scaled_set, 2 * it + h + 3)
                    dve.sem_inc(turn, 1)
                    dve.tensor_reduce(st.logits[:, bass.ds((2 * it + h) * 2 * HEADS, 2 * HEADS)],
                                      scaled[:, h, :, :].rearrange("p s (a c) -> p (s a) c", c=CH), AX.X, ALU.add
                                      ).then_inc(logits_set, 1)
            dve.wait_ge(h_set, NW)
            dve.wait_ge(logits_set, NW + 2)
            dve.tensor_copy(acc[:, :, D:ROW], logits[:, :, 0:HEADS]).then_inc(rows_set, 1)
            dve.tensor_reduce(least[:], logits[:, :, 0:HEADS].rearrange("p w a -> p a w"), AX.X, ALU.min).then_inc(chain, 1)
            dve.wait_ge(chain, 1)
            dve.tensor_single_scalar(most[:], least[:], -1.0, ALU.mult).then_inc(negated, 1)
            dve.wait_ge(reduced, 1)
            dve.tensor_single_scalar(st.shift[:], st.shift[:], 1.0, ALU.add).then_inc(chain, 1)
            dve.wait_ge(chain, 2)
            dve.tensor_tensor(st.maxima[:].rearrange("p (w c) -> p w c", w=NW), logits[:, :, 0:HEADS],
                              st.shift[:].unsqueeze(1).broadcast_to([P, NW, HEADS]), ALU.add).then_inc(rows_set, 1)

        @block.gpsimd
        def _(pool):
            pool.sem_inc(logits_set, 2)
            pool.wait_ge(negated, 1)
            pool.partition_all_reduce(st.shift[:], most[:], P, bass.bass_isa.ReduceOp.max).then_inc(reduced, 1)


def layer3_maxima(nc, st):
    with ExitStack() as ctx:
        phase_end(nc, ctx)
        def sb(name, shape, dt=F32):
            return ctx.enter_context(nc.sbuf_tensor("l3m_" + name, shape, dt))

        def sem(name):
            return phase_semaphore(nc, ctx, "l3m_" + name)

        ring, stage, onehot = sb("ring", [P, RING, HEADS]), sb("stage", [P, RING], I32), sb("onehot", [P, GROUP, P])
        diagonal, highest = sb("diagonal", [P, RING, HEADS, P]), sb("highest", [P, HEADS])
        spread = ctx.enter_context(nc.psum_tensor("l3m_spread", [P, GROUP, HEADS, P], F32))
        arrived = [sem(f"arrived{k}") for k in range(RING)]
        staged, diag_set, hot, hot_used, reduced, merged, group_done, turn = (
            sem(n) for n in ("staged", "diag_set", "hot", "hot_used", "reduced", "merged", "group_done", "turn"))
        block = ctx.enter_context(nc.Block())

        @block.gpsimd
        def _(pool):
            with pool.Fori(0, HG) as it:
                for h in range(2):
                    pool.wait_ge(group_done, 2 * it + h + 1)
                    pool.sem_inc(turn, 1)
                    pool.tensor_copy(stage[:, GROUP * h:GROUP * (h + 1)],
                                     st.src[:, bass.ds((2 * it + h) * GROUP, GROUP)]).then_inc(staged, 1)
                    pool.wait_ge(staged, 2 * it + h + 1)
                    pool.sem_inc(turn, 1)
                    for k in range(GROUP * h, GROUP * (h + 1)):
                        pool.indirect_dma_start(ring[:, k, :], None, st.gat_logits,
                                                bass.IndirectOffsetOnAxis(ap=stage[:, k:k + 1], axis=0)
                                                ).then_inc(arrived[k], 16)

        @block.scalar
        def _(act):
            with act.Fori(0, HG) as it:
                for h in range(2):
                    act.wait_ge(group_done, 2 * it + h + 1)
                    for k in range(GROUP * h, GROUP * (h + 1)):
                        act.wait_ge(arrived[k], 16 * it + 16)
                        for a in range(HEADS):
                            last = act.activation(diagonal[:, k, a, :], st.ident[:], ACT.Copy, scale=ring[:, k, a:a + 1])
                        last.then_inc(diag_set, 1)

        @block.vector
        def _(dve):
            with dve.Fori(0, HG) as it:
                for h in range(2):
                    first, count, before = group_range(nc, dve, st, 2 * it + h)
                    with dve.Fori(0, count) as j:
                        window = within(nc, first + j, NW - 1)
                        step = before + j
                        for k in range(GROUP):
                            dve.wait_ge(hot_used, GROUP * step + k + 1)
                            dve.tensor_scalar(onehot[:, k, :], st.iota[:], st.window_start[:, bass.ds(window, 1)],
                                              st.dst[:, bass.ds(it * RING + GROUP * h + k, 1)],
                                              ALU.add, ALU.is_equal).then_inc(hot, 1)
                        dve.wait_ge(hot_used, GROUP * step + 2 * GROUP)
                        dve.wait_ge(merged, step + 1)
                        dve.tensor_reduce(highest[:], spread[:].rearrange("p k a e -> p a k e"), AX.XY, ALU.max
                                          ).then_inc(reduced, 1)
                        dve.wait_ge(reduced, step + 2)
                        here = st.maxima[:, bass.ds(window * HEADS, HEADS)]
                        dve.tensor_tensor(here, here, highest[:], ALU.max).then_inc(merged, 1)

        @block.tensor
        def _(pe):
            pe.sem_inc(hot_used, GROUP)
            pe.sem_inc(group_done, 2)
            pe.sem_inc(reduced, 1)
            pe.sem_inc(merged, 1)
            with pe.Fori(0, HG) as it:
                for h in range(2):
                    _, count, before = group_range(nc, pe, st, 2 * it + h)
                    pe.wait_ge(diag_set, RING * it + GROUP * (h + 1))
                    pe.sem_inc(turn, 1)
                    with pe.Fori(0, count) as j:
                        step = before + j
                        pe.wait_ge(reduced, step + 1)
                        for k in range(GROUP):
                            pe.wait_ge(hot, GROUP * step + k + 1)
                            pe.matmul(spread[:, k, :, :], onehot[:, k, :], diagonal[:, GROUP * h + k, :, :],
                                      start=True, stop=True).then_inc(hot_used, 1)
                    pe.drain().then_inc(group_done, 1)


def layer3_self_loops(nc, st):
    with ExitStack() as ctx:
        phase_end(nc, ctx)
        def sb(name, shape):
            return ctx.enter_context(nc.sbuf_tensor("l3s_" + name, shape, F32))

        def sem(name):
            return phase_semaphore(nc, ctx, "l3s_" + name)

        raw, self_logit = sb("raw", [P, NW, HEADS]), sb("self_logit", [P, NW, HEADS])
        chain, logit_set, weight_set = (sem(n) for n in ("chain", "logit_set", "weight_set"))
        block = ctx.enter_context(nc.Block())
        acc = st.acc[:].rearrange("p (w f) -> p w f", w=NW)
        logits = st.logits[:].rearrange("p (w c) -> p w c", w=NW)
        at_dst = st.at_dst[:].rearrange("p (w c) -> p w c", w=NW)

        @block.vector
        def _(dve):
            done = [0]

            def link(ins_):
                done[0] += 1
                ins_.then_inc(chain, 1)
                dve.wait_ge(chain, done[0])

            dve.tensor_copy(at_dst[:, :, 0:HEADS], logits[:, :, HEADS:2 * HEADS])
            link(dve.tensor_tensor(raw[:], st.maxima[:].rearrange("p (w c) -> p w c", w=NW),
                                   st.shift[:].unsqueeze(1).broadcast_to([P, NW, HEADS]), ALU.subtract))
            link(dve.tensor_tensor(raw[:], raw[:], logits[:, :, HEADS:2 * HEADS], ALU.add))
            link(dve.scalar_tensor_tensor(out=at_dst[:, :, HEADS:2 * HEADS], in0=raw[:], scalar=SLOPE, in1=raw[:],
                                          op0=ALU.mult, op1=ALU.max))
            link(dve.tensor_tensor(self_logit[:], logits[:, :, 0:HEADS], logits[:, :, HEADS:2 * HEADS], ALU.add))
            link(dve.scalar_tensor_tensor(out=raw[:], in0=self_logit[:], scalar=SLOPE, in1=self_logit[:],
                                          op0=ALU.mult, op1=ALU.max))
            dve.tensor_tensor(self_logit[:], raw[:], at_dst[:, :, HEADS:2 * HEADS], ALU.subtract).then_inc(logit_set, 1)
            dve.wait_ge(weight_set, 1)
            h4 = acc[:, :, 0:D].rearrange("p w (a c) -> p w a c", a=HEADS)
            link(dve.tensor_tensor(h4, h4, acc[:, :, D:D + HEADS].unsqueeze(3).broadcast_to([P, NW, HEADS, CH]), ALU.mult))

        @block.scalar
        def _(act):
            act.wait_ge(logit_set, 1)
            act.activation(acc[:, :, D:D + HEADS], self_logit[:], ACT.Exp).then_inc(weight_set, 1)


def layer3_edges(nc, st):
    ROW = D + HEADS
    with ExitStack() as ctx:
        phase_end(nc, ctx)
        def sb(name, shape, dt=F32):
            return ctx.enter_context(nc.sbuf_tensor("l3e_" + name, shape, dt))

        def sem(name):
            return phase_semaphore(nc, ctx, "l3e_" + name)

        ring, rows, stage = sb("ring", [P, RING, ROW]), sb("rows", [P, RING, ROW]), sb("stage", [P, RING], I32)
        onehot, onehot_t = sb("onehot", [P, GROUP, P]), sb("onehot_t", [P, GROUP, P])
        of_dst, logit, leaky = (sb(n, s) for n, s in (("of_dst", [P, GROUP, 2 * HEADS]), ("logit", [P, GROUP, HEADS]),
                                                      ("leaky", [P, GROUP, HEADS])))
        turned = ctx.enter_context(nc.psum_tensor("l3e_turned", [P, GROUP, 512], F32))
        fetched = ctx.enter_context(nc.psum_tensor("l3e_fetched", [P, 512], F32))
        total = ctx.enter_context(nc.psum_tensor("l3e_total", [P, 512], F32))
        arrived = [sem(f"arrived{k}") for k in range(RING)]
        (staged, hot, hot_used, turned_out, got, got_added, chain, logit_set, weight_set, rows_set, added, group_done,
         turn) = (sem(n) for n in ("staged", "hot", "hot_used", "turned_out", "got", "got_added", "chain", "logit_set",
                                   "weight_set", "rows_set", "added", "group_done", "turn"))
        block = ctx.enter_context(nc.Block())
        CHAIN = 4

        @block.gpsimd
        def _(pool):
            with pool.Fori(0, HG) as it:
                for h in range(2):
                    pool.wait_ge(group_done, 2 * it + h + 1)
                    pool.sem_inc(turn, 1)
                    pool.tensor_copy(stage[:, GROUP * h:GROUP * (h + 1)],
                                     st.src[:, bass.ds((2 * it + h) * GROUP, GROUP)]).then_inc(staged, 1)
                    pool.wait_ge(staged, 2 * it + h + 1)
                    pool.sem_inc(turn, 1)
                    for k in range(GROUP * h, GROUP * (h + 1)):
                        pool.indirect_dma_start(ring[:, k, :], None, st.gat_rows,
                                                bass.IndirectOffsetOnAxis(ap=stage[:, k:k + 1], axis=0)
                                                ).then_inc(arrived[k], 16)

        @block.scalar
        def _(act):
            with act.Fori(0, HG) as it:
                for h in range(2):
                    _, count, before = group_range(nc, act, st, 2 * it + h)
                    with act.Fori(0, count) as j:
                        step = before + j
                        for k in range(GROUP):
                            act.wait_ge(hot_used, GROUP * (before + step) + k + 1 + GROUP)
                            act.wait_ge(got, GROUP * step + k + 1)
                            act.activation(onehot_t[:, k, :], turned[:, k, 0:P], ACT.Copy).then_inc(turned_out, 1)
                    act.wait_ge(logit_set, 2 * it + h + 1)
                    act.activation(rows[:, GROUP * h:GROUP * (h + 1), D:ROW], logit[:], ACT.Exp).then_inc(weight_set, 1)

        @block.vector
        def _(dve):
            def build(hots, window, tile):
                for k in range(GROUP):
                    dve.wait_ge(hot_used, hots + k + 1)
                    dve.tensor_scalar(onehot[:, k, :], st.iota[:], st.window_start[:, bass.ds(window, 1)],
                                      st.dst[:, bass.ds(tile + k, 1)], ALU.add, ALU.is_equal).then_inc(hot, 1)

            dve.sem_inc(added, 1)
            dve.sem_inc(got_added, 1)
            with dve.Fori(0, HG) as it:
                for h in range(2):
                    half = slice(GROUP * h, GROUP * (h + 1))
                    tile = it * RING + GROUP * h
                    chained = (2 * it + h) * CHAIN
                    first, count, before = group_range(nc, dve, st, 2 * it + h)
                    dve.memset(of_dst[:], 0.0).then_inc(chain, 1)
                    dve.wait_ge(chain, chained + 1)
                    dve.sem_inc(turn, 1)
                    with dve.Fori(0, count) as j:
                        step = before + j
                        build(GROUP * (before + step), within(nc, first + j, NW - 1), tile)
                        dve.wait_ge(got, GROUP * step + 2 * GROUP)
                        dve.tensor_tensor(of_dst[:], of_dst[:],
                                          fetched[:, 0:GROUP * 2 * HEADS].rearrange("p (k c) -> p k c", k=GROUP), ALU.add).then_inc(got_added, 1)
                    dve.wait_ge(got_added, before + count + 1)
                    for k in range(GROUP * h, GROUP * (h + 1)):
                        dve.wait_ge(arrived[k], 16 * it + 16)
                    dve.tensor_tensor(logit[:], ring[:, half, D:ROW], of_dst[:, :, 0:HEADS], ALU.add).then_inc(chain, 1)
                    dve.wait_ge(chain, chained + 2)
                    dve.scalar_tensor_tensor(out=leaky[:], in0=logit[:], scalar=SLOPE, in1=logit[:],
                                             op0=ALU.mult, op1=ALU.max).then_inc(chain, 1)
                    dve.wait_ge(chain, chained + 3)
                    dve.tensor_tensor(logit[:], leaky[:], of_dst[:, :, HEADS:2 * HEADS], ALU.subtract).then_inc(logit_set, 1)
                    dve.wait_ge(weight_set, 2 * it + h + 1)
                    for k in range(GROUP * h, GROUP * (h + 1)):
                        dve.tensor_tensor(rows[:, k, 0:D].rearrange("p (a c) -> p a c", a=HEADS),
                                          ring[:, k, 0:D].rearrange("p (a c) -> p a c", a=HEADS),
                                          rows[:, k, D:ROW].unsqueeze(2).broadcast_to([P, HEADS, CH]), ALU.mult
                                          ).then_inc(rows_set, 1)
                    dve.wait_ge(rows_set, RING * it + GROUP * (h + 1))
                    dve.sem_inc(chain, 1)
                    with dve.Fori(0, count) as j:
                        step = before + j
                        window = within(nc, first + j, NW - 1)
                        build(GROUP * (before + count + step), window, tile)
                        dve.wait_ge(hot_used, GROUP * (before + count + step) + 2 * GROUP)
                        here = st.acc[:, bass.ds(window * WIDE, ROW)]
                        dve.tensor_tensor(here, here, total[:, 0:ROW], ALU.add).then_inc(added, 1)

        @block.tensor
        def _(pe):
            pe.sem_inc(hot_used, GROUP)
            pe.sem_inc(got, GROUP)
            pe.sem_inc(group_done, 2)
            with pe.Fori(0, HG) as it:
                for h in range(2):
                    first, count, before = group_range(nc, pe, st, 2 * it + h)
                    with pe.Fori(0, count) as j:
                        window = within(nc, first + j, NW - 1)
                        step = before + j
                        for k in range(GROUP):
                            pe.wait_ge(hot, GROUP * (before + step) + k + 1)
                            pe.transpose(turned[:, k, 0:P], onehot[:, k, :], st.ident[:]).then_inc(hot_used, 1)
                        pe.wait_ge(got_added, step + 1)
                        for k in range(GROUP):
                            pe.wait_ge(turned_out, GROUP * step + k + 1)
                            pe.sem_inc(turn, 1)
                            pe.matmul(fetched[:, 2 * HEADS * k:2 * HEADS * (k + 1)], onehot_t[:, k, :], st.at_dst[:, bass.ds(2 * HEADS * window, 2 * HEADS)],
                                      start=True, stop=True).then_inc(got, 1)
                    pe.wait_ge(rows_set, RING * it + GROUP * (h + 1))
                    pe.sem_inc(turn, 1)
                    with pe.Fori(0, count) as j:
                        step = before + j
                        pe.wait_ge(added, step + 1)
                        for k in range(GROUP):
                            pe.wait_ge(hot, GROUP * (before + count + step) + k + 1)
                            pe.matmul(total[:, 0:ROW], onehot[:, k, :], rows[:, GROUP * h + k, :],
                                      start=(k == 0), stop=(k == GROUP - 1)).then_inc(hot_used, 1)
                    pe.drain().then_inc(group_done, 1)


def layer3_end(nc, st, ins):
    with ExitStack() as ctx:
        phase_end(nc, ctx)
        def sb(name, shape):
            return ctx.enter_context(nc.sbuf_tensor("l3z_" + name, shape, F32))

        def sem(name):
            return phase_semaphore(nc, ctx, "l3z_" + name)

        bias, per_weight = sb("bias", [P, D]), sb("per_weight", [P, NW, HEADS])
        squares, norm, per_norm = sb("squares", [P, NW]), sb("norm", [P, NW]), sb("per_norm", [P, NW])
        loaded, chain, biased, relued, summed, rooted = (
            sem(n) for n in ("loaded", "chain", "biased", "relued", "summed", "rooted"))
        block = ctx.enter_context(nc.Block())
        acc = st.acc[:].rearrange("p (w f) -> p w f", w=NW)
        value, spare = acc[:, :, 0:D], acc[:, :, D:2 * D]

        @block.sync
        def _(sp):
            sp.dma_start(bias[:], ins["L3_bias"].partition_broadcast(P)).then_inc(loaded, 16)
            sp.wait_ge(loaded, 16)

        @block.vector
        def _(dve):
            done = [0]

            def link(ins_):
                done[0] += 1
                ins_.then_inc(chain, 1)
                dve.wait_ge(chain, done[0])

            link(dve.reciprocal(per_weight[:], acc[:, :, D:D + HEADS]))
            value4 = value.rearrange("p w (a c) -> p w a c", a=HEADS)
            link(dve.tensor_tensor(value4, value4, per_weight[:].unsqueeze(3).broadcast_to([P, NW, HEADS, CH]), ALU.mult))
            dve.wait_ge(loaded, 16)
            dve.tensor_tensor(value, value, bias[:].unsqueeze(1).broadcast_to([P, NW, D]), ALU.add).then_inc(biased, 1)
            dve.wait_ge(relued, 2)
            dve.tensor_reduce(squares[:], spare, AX.X, ALU.add).then_inc(summed, 1)
            dve.wait_ge(rooted, 1)
            link(dve.tensor_single_scalar(norm[:], norm[:], 1e-12, ALU.max))
            link(dve.reciprocal(per_norm[:], norm[:]))
            link(dve.tensor_tensor(value, value, per_norm[:].unsqueeze(2).broadcast_to([P, NW, D]), ALU.mult))
            link(dve.tensor_tensor(value, value, st.x[:].rearrange("p (w f) -> p w f", w=NW), ALU.add))

        @block.scalar
        def _(act):
            act.wait_ge(biased, 1)
            act.activation(value, value, ACT.Relu).then_inc(relued, 1)
            act.wait_ge(relued, 1)
            act.activation(spare, value, ACT.Square).then_inc(relued, 1)
            act.wait_ge(summed, 1)
            act.activation(norm[:], squares[:], ACT.Sqrt).then_inc(rooted, 1)


def layer3(nc, st, ins):
    layer3_nodes(nc, st, ins)
    layer3_maxima(nc, st)
    layer3_self_loops(nc, st)
    layer3_edges(nc, st)
    layer3_end(nc, st, ins)
    layer_norm(nc, st, "ln4_", st.acc, WIDE)


def start_layer0(nc, st):
    with ExitStack() as ctx:
        phase_end(nc, ctx)
        copied = phase_semaphore(nc, ctx, "start0_copied")
        block = ctx.enter_context(nc.Block())

        @block.vector
        def _(dve):
            acc = st.acc[:].rearrange("p (w f) -> p w f", w=NW)
            dve.memset(acc[:, :, D:D + 1], 0.0).then_inc(copied, 1)
            dve.tensor_copy(acc[:, :, 0:D], st.x[:].rearrange("p (w f) -> p w f", w=NW)).then_inc(copied, 1)


def finish(nc, st, out):
    with ExitStack() as ctx:
        phase_end(nc, ctx)
        stored = phase_semaphore(nc, ctx, "finish_stored")
        block = ctx.enter_context(nc.Block())
        full = N // P

        @block.sync
        def _(sp):
            sp.dma_start(out[0:full * P, :].rearrange("(w p) f -> p w f", p=P),
                         st.x[:, 0:full * D].rearrange("p (w f) -> p w f", f=D)).then_inc(stored, 16)
            sp.dma_start(out[full * P:N, :], st.x[0:N - full * P, full * D:(full + 1) * D]).then_inc(stored, 16)
            sp.wait_ge(stored, 32)


def build(nc, ins, out):
    with ExitStack() as ctx:
        st = State()

        def sb(name, shape, dt=F32):
            return ctx.enter_context(nc.sbuf_tensor(name, shape, dt))

        st.x = sb("x", [P, NW * D])
        st.iota = sb("iota", [P, P])
        st.ident = sb("ident", [P, P])
        st.window_start = sb("window_start", [P, NW])
        st.dst = sb("dst", [P, NT])
        st.src = sb("src", [P, NT], I32)
        st.src_type = sb("src_type", [P, NT], I32)
        st.weight = sb("weight", [P, NT])
        st.ranges = sb("ranges", [1, 3 * NG], I32)
        st.dst_row = sb("dst_row", [P, NT], I32)
        st.degree = sb("degree", [P, NW])
        st.in_edges = sb("in_edges", [P, NW])
        st.dinv = sb("dinv", [P, NW])

        def rows(name, width):
            return nc.dram_tensor(name, [NP, width], F32, kind="Internal").ap()

        st.logits = sb("logits", [P, NW * 2 * HEADS])
        st.at_dst = sb("at_dst", [P, NW * 2 * HEADS])
        st.maxima = sb("maxima", [P, NW * HEADS])
        st.shift = sb("shift", [P, HEADS])
        st.gat_rows = rows("attention_table", D + HEADS)
        st.gat_logits = rows("attention_logit_table", HEADS)
        st.table1 = rows("conv1_table", D)
        st.table2 = rows("conv2_table", D)
        st.src_rows = rows("message_src_table", HID2)
        st.dst_rows = rows("message_dst_table", HID2)
        st.ranges_dram = nc.dram_tensor("group_table", [NG, 3], I32, kind="Internal").ap()
        st.rel_rows = nc.dram_tensor("relation_table", [NP * RELS, D], F32, kind="Internal").ap()
        prepare(nc, st, ins)
        transform_by_relation(nc, st, ins)
        st.acc = sb("acc", [P, NW * WIDE])
        start_layer0(nc, st)
        aggregate(nc, st, "l0_", st.rel_rows, st.src_type, st.weight)
        layer_norm(nc, st, "ln0_", st.acc, WIDE)
        layer1(nc, st, ins)
        layer2(nc, st, ins)
        layer3(nc, st, ins)
        finish(nc, st, out)


def kernel(**inputs):
    import concourse.bacc as bacc
    from concourse.bass_utils import run_bass_kernel_spmd

    given = {name: np.asarray(a) for name, a in inputs.items()}

    def padded(a, fill):
        rows = np.full((EP,), fill, a.dtype)
        rows[:E] = a.reshape(-1)
        return rows

    def by_tile(a):
        return np.ascontiguousarray(a.reshape(NT, P).T)

    x = np.zeros((NP, D), given["x"].dtype)
    x[:N] = given["x"]
    attr = np.zeros((EP, EDIM), given["edge_attr_64"].dtype)
    attr[:E] = given["edge_attr_64"]
    dst = padded(given["dst"], PAD_NODE)
    arrays = {
        "x": x, "x_t": np.ascontiguousarray(x.T),
        "src": by_tile(padded(given["src"], 0)), "dst": by_tile(dst),
        "dst_by_group": dst.reshape(NG, GROUP * P),
        "edge_type": by_tile(padded(given["edge_type_16"], 0)),
        "edge_weight": by_tile(padded(given["edge_weight1"], 0)),
        "edge_attr_t": np.ascontiguousarray(attr.T),
    }
    for name, a in given.items():
        if name.startswith("L"):
            arrays[name.replace("_gnn", "")] = np.ascontiguousarray(a)
    nc = bacc.Bacc("TRN2", target_bir_lowering=False, num_devices=1)
    ins = {name: nc.dram_tensor("in_" + name, a.shape, mybir.dt.from_np(a.dtype), kind="ExternalInput").ap()
           for name, a in arrays.items()}
    out = nc.dram_tensor("out", [N, D], F32, kind="ExternalOutput").ap()
    build(nc, ins, out)
    result = run_bass_kernel_spmd(nc, [{"in_" + name: a for name, a in arrays.items()}], core_ids=[0])
    return result.results[0]["out"]
```

```python
from contextlib import ExitStack

import numpy as np
import concourse.bass as bass
import concourse.mybir as mybir
from concourse.alu_op_type import AluOpType as ALU

F32 = mybir.dt.float32
I32 = mybir.dt.int32
ACT = mybir.ActivationFunctionType
AX = mybir.AxisListType

P = 128
N = 3125
E = 50000
D = 256
RELS = 16
HID1 = 300
HC = 3
HR = HID1 // HC
HID2 = 512
EDIM = 64
HEADS = 4
CH = D // HEADS
NW = 26
NP = NW * P
GROUP = 4
NG = -(-E // (P * GROUP))
EP = NG * GROUP * P
NT = NG * GROUP
RING = 2 * GROUP
HG = NG // 2
HW = NW // 2
PAD_NODE = N + 74
WIDE = 512
EPS = 1e-5
SLOPE = 0.2
assert NG % 2 == 0 and NW % 2 == 0 and N <= PAD_NODE < NP


class State:
    pass


def phase_end(nc, ctx):
    ctx.callback(nc.all_engine_barrier)


def phase_semaphore(nc, ctx, name):
    handle = nc.alloc_semaphore(name)
    ctx.callback(nc.clear_and_free_semaphores, [handle])
    return handle


def within(nc, value, top):
    return nc.s_assert_within(value, 0, top, skip_runtime_bounds_check_because="the group ranges are computed from node numbers below N")


def group_ranges(nc, eng, st, trip):
    word = eng.value_load(st.ranges[0:1, bass.ds(trip, 1)])

    def field(low, bits, most):
        value = (word >> low) & ((1 << bits) - 1)
        return eng.snap(nc.s_assert_within(value, 0, most, skip_runtime_bounds_check_because="prepare packs it so"))

    before = field(20, 12, NG * (NW - 1))
    first0, more0 = field(0, 5, NW - 1), field(5, 5, NW - 1)
    first1, more1 = field(10, 5, NW - 1), field(15, 5, NW - 1)
    return (first0, more0, before), (first1, more1, eng.snap(before + more0))


def one_hot(dve, st, out, window, tile):
    return dve.tensor_scalar(out, st.iota[:], st.window_start[:, bass.ds(window, 1)], st.dst[:, bass.ds(tile, 1)],
                             ALU.add, ALU.is_equal)


def more_steps(nc, dve, st, ranges, it, h, x_onehot, x_total, width, added, x_hot, x_used, x_added):
    first, more, before = ranges[h]
    with dve.If(more > 0):
        with dve.Fori(0, more) as j:
            window = within(nc, first + 1 + j, NW - 1)
            extra = before + j
            for k in range(GROUP):
                dve.wait_ge(x_used, GROUP * extra + k + 1)
                one_hot(dve, st, x_onehot[:, k, :], window, it * RING + GROUP * h + k).then_inc(x_hot, 1)
            dve.wait_ge(x_used, GROUP * extra + 2 * GROUP)
            dve.wait_ge(added, 2 * it + h + 3)
            dve.wait_ge(x_added, extra + 1)
            here = st.acc[:, bass.ds(window * WIDE, width)]
            dve.tensor_tensor(here, here, x_total[:, 0:width], ALU.add).then_inc(x_added, 1)


def prepare(nc, st, ins):
    with ExitStack() as ctx:
        phase_end(nc, ctx)
        def sb(name, shape, dt):
            return ctx.enter_context(nc.sbuf_tensor("pre_" + name, shape, dt))

        def sem(name):
            return phase_semaphore(nc, ctx, "pre_" + name)

        src_i = sb("src_i", [P, NT], I32)
        type_i = sb("type_i", [P, NT], I32)
        dst_g = sb("dst_g", [NG, GROUP * P], I32)
        low_high = sb("low_high", [NG, 2], I32)
        windows = sb("windows", [NG, 2], I32)
        windows_f = sb("windows_f", [NG, 2], F32)
        table = sb("table", [NG, 3], F32)
        table_i = sb("table_i", [NG, 3], I32)
        row = sb("row", [1, 3 * NG], I32)
        earlier = sb("earlier", [NG, NG], F32)
        ones = sb("ones", [P, P], F32)
        src_f = sb("src_f", [P, NT], F32)
        steps_psum = ctx.enter_context(nc.psum_tensor("pre_steps", [P, 512], F32))
        loaded, summed, filled, iotas, chain, counted, stepped, spilled, fetched = (
            sem(n) for n in ("loaded", "summed", "filled", "iotas", "chain", "counted", "stepped", "spilled", "fetched"))
        block = ctx.enter_context(nc.Block())

        @block.sync
        def _(sp):
            sp.dma_start(st.dst_row[:], ins["dst"]).then_inc(loaded, 16)
            sp.dma_start(src_i[:], ins["src"]).then_inc(loaded, 16)
            sp.dma_start(type_i[:], ins["edge_type"]).then_inc(loaded, 16)
            sp.dma_start(dst_g[:], ins["dst_by_group"]).then_inc(loaded, 16)
            sp.dma_start(st.weight[:], ins["edge_weight"]).then_inc(loaded, 16)
            sp.wait_ge(loaded, 5 * 16)
            sp.wait_ge(stepped, 1)
            sp.dma_start(st.ranges_dram, table_i[:]).then_inc(spilled, 16)
            sp.wait_ge(spilled, 16)
            sp.dma_start(row[:], st.ranges_dram.rearrange("(a g) c -> a (g c)", a=1)).then_inc(fetched, 16)
            sp.wait_ge(fetched, 16)

        @block.gpsimd
        def _(pool):
            pool.memset(ones[:], 1.0).then_inc(filled, 1)
            pool.iota(st.iota[:], pattern=[[1, P]], base=0, channel_multiplier=0,
                      allow_small_or_imprecise_dtypes=True).then_inc(iotas, 1)
            pool.iota(st.window_start[:], pattern=[[P, NW]], base=0, channel_multiplier=0,
                      allow_small_or_imprecise_dtypes=True).then_inc(iotas, 1)
            pool.wait_ge(filled, 1)
            pool.affine_select(out=st.ident[:], in_=ones[:], compare_op=ALU.is_equal, fill=0.0, base=0,
                               pattern=[[-1, P]], channel_multiplier=1).then_inc(iotas, 1)
            pool.affine_select(out=earlier[:], in_=ones[0:NG, 0:NG], compare_op=ALU.is_gt, fill=0.0, base=0,
                               pattern=[[1, NG]], channel_multiplier=-1).then_inc(filled, 1)

        @block.vector
        def _(dve):
            done = [0]

            def link(ins_):
                done[0] += 1
                ins_.then_inc(chain, 1)
                dve.wait_ge(chain, done[0])

            dve.wait_ge(loaded, 5 * 16)
            dve.tensor_copy(st.dst[:], st.dst_row[:])
            dve.tensor_copy(st.src[:], src_i[:])
            link(dve.tensor_copy(src_f[:], src_i[:]))
            dve.scalar_tensor_tensor(out=st.src_type[:], in0=src_f[:], scalar=float(RELS), in1=type_i[:],
                                     op0=ALU.mult, op1=ALU.add)
            dve.tensor_reduce(low_high[:, 0:1], dst_g[:], AX.X, ALU.min)
            link(dve.tensor_reduce(low_high[:, 1:2], dst_g[:], AX.X, ALU.max))
            link(dve.tensor_single_scalar(windows[:], low_high[:], 7, ALU.arith_shift_right))
            link(dve.tensor_copy(windows_f[:], windows[:]))
            dve.tensor_copy(table[:, 0:1], windows_f[:, 0:1])
            dve.tensor_tensor(table[:, 1:2], windows_f[:, 1:2], windows_f[:, 0:1], ALU.subtract).then_inc(counted, 1)
            dve.wait_ge(summed, 1)
            link(dve.tensor_copy(table[:, 2:3], steps_psum[0:NG, 0:1]))
            dve.tensor_copy(table_i[:], table[:]).then_inc(stepped, 1)
            dve.wait_ge(fetched, 16)
            pair = row[:].rearrange("a (t f) -> a t f", f=6)
            places = ((0, 0), (1, 5), (3, 10), (4, 15), (2, 20))
            for column, low in places[1:]:
                link(dve.tensor_single_scalar(pair[:, :, column], pair[:, :, column], low, ALU.logical_shift_left))
            link(dve.tensor_copy(st.ranges[:], pair[:, :, 0]))
            for column, _ in places[1:]:
                link(dve.tensor_tensor(st.ranges[:], st.ranges[:], pair[:, :, column], ALU.bitwise_or))

        @block.tensor
        def _(pe):
            pe.wait_ge(filled, 2)
            pe.wait_ge(counted, 1)
            pe.matmul(steps_psum[0:NG, 0:1], earlier[:], table[:, 1:2], start=True, stop=True).then_inc(summed, 1)


def transform_by_relation(nc, st, ins):
    KC = D // P
    PAIRS = RELS // 2
    with ExitStack() as ctx:
        phase_end(nc, ctx)
        def sb(name, shape, dt):
            return ctx.enter_context(nc.sbuf_tensor("rel_" + name, shape, dt))

        def sem(name):
            return phase_semaphore(nc, ctx, "rel_" + name)

        weights = sb("weights", [P, KC, RELS * D], F32)
        x_t = sb("x_t", [P, 2, KC, P], F32)
        rows = sb("rows", [P, 2, RELS * D], F32)
        banks = [ctx.enter_context(nc.psum_tensor(f"rel_pair{b}", [P, 2 * D], F32)) for b in range(PAIRS)]
        w_in, x_in0, x_in1, paired, out_act, out_dve = (
            sem(n) for n in ("w_in", "x_in0", "x_in1", "paired", "out_act", "out_dve"))
        x_in = [x_in0, x_in1]
        stored = [sem("stored0"), sem("stored1")]
        x_sb_in = sem("x_sb_in")
        turn = sem("turn")
        block = ctx.enter_context(nc.Block())

        @block.sync
        def _(sp):
            for k in range(KC):
                sp.dma_start(weights[:, k, :].rearrange("k (r o) -> k r o", r=RELS),
                             ins["L0_weight"].rearrange("r (c k) o -> c k r o", c=KC)[k]).then_inc(w_in, 16)
            sp.dma_start(st.x[:].rearrange("p (w f) -> p w f", w=NW),
                         ins["x"].rearrange("(w p) f -> p w f", p=P)).then_inc(x_sb_in, 16)
            with sp.Fori(0, HW) as it:
                for h in range(2):
                    sp.wait_ge(paired, PAIRS * (2 * it + h) + PAIRS)
                    sp.dma_start(x_t[:, h, :, :],
                                 ins["x_t"].rearrange("(c k) n -> k c n", c=KC)[:, :, bass.ds((2 * it + h) * P, P)]
                                 ).then_inc(x_in[h], 16)
            sp.wait_ge(x_sb_in, 16)

        @block.tensor
        def _(pe):
            pe.sem_inc(paired, 2 * PAIRS)
            pe.wait_ge(w_in, KC * 16)
            with pe.Fori(0, HW) as it:
                for h in range(2):
                    pe.wait_ge(x_in[h], 16 * it + 16)
                    for b in range(PAIRS):
                        pe.wait_ge([out_act, out_dve][b % 2], (2 * it + h) * (PAIRS // 2) + b // 2 + 1)
                        for k in range(KC):
                            last = pe.matmul(banks[b][:], x_t[:, h, k, :], weights[:, k, 2 * D * b:2 * D * (b + 1)],
                                             start=(k == 0), stop=(k == KC - 1))
                        last.then_inc(paired, 1)

        @block.scalar
        def _(act):
            act.sem_inc(out_act, PAIRS // 2)
            act.sem_inc(stored[0], 16)
            act.sem_inc(stored[1], 16)
            with act.Fori(0, HW) as it:
                for h in range(2):
                    act.wait_ge(stored[h], 16 * it + 16)
                    for b in range(0, PAIRS, 2):
                        act.wait_ge(paired, PAIRS * (2 * it + h + 2) + b + 1)
                        act.activation(rows[:, h, 2 * D * b:2 * D * (b + 1)], banks[b][:], ACT.Copy).then_inc(out_act, 1)
                    act.wait_ge(out_act, (2 * it + h + 2) * (PAIRS // 2))
                    act.wait_ge(out_dve, (2 * it + h + 2) * (PAIRS // 2))
                    act.sem_inc(turn, 1)
                    act.dma_start(st.rel_rows.rearrange("(n r) f -> n (r f)", r=RELS)[bass.ds((2 * it + h) * P, P), :],
                                  rows[:, h, :]).then_inc(stored[h], 16)
            for h in range(2):
                act.wait_ge(stored[h], 16 * (HW + 1))

        @block.vector
        def _(dve):
            dve.sem_inc(out_dve, PAIRS // 2)
            with dve.Fori(0, HW) as it:
                for h in range(2):
                    dve.wait_ge(stored[h], 16 * it + 16)
                    for b in range(1, PAIRS, 2):
                        dve.wait_ge(paired, PAIRS * (2 * it + h + 2) + b + 1)
                        dve.tensor_copy(rows[:, h, 2 * D * b:2 * D * (b + 1)], banks[b][:]).then_inc(out_dve, 1)


def aggregate(nc, st, name, table, index, weight):
    width = D if weight is None else D + 1
    with ExitStack() as ctx:
        phase_end(nc, ctx)

        def sem(part):
            return phase_semaphore(nc, ctx, name + part)

        ring = ctx.enter_context(nc.sbuf_tensor(name + "ring", [P, RING, D], F32))
        stage = ctx.enter_context(nc.sbuf_tensor(name + "stage", [P, RING], I32))
        onehot = ctx.enter_context(nc.sbuf_tensor(name + "onehot", [P, RING, P], F32))
        x_onehot = ctx.enter_context(nc.sbuf_tensor(name + "x_onehot", [P, GROUP, P], F32))
        rows = ring if weight is None else ctx.enter_context(nc.sbuf_tensor(name + "rows", [P, RING, D + 4], F32))
        total = [ctx.enter_context(nc.psum_tensor(name + f"total{h}", [P, 512], F32)) for h in range(2)]
        x_total = ctx.enter_context(nc.psum_tensor(name + "x_total", [P, 512], F32))
        arrived = [sem(f"arrived{k}") for k in range(RING)]
        staged, hot, hot_used, added, x_hot, x_used, x_added, group_done, scaled, turn, ones_set = (
            sem(n) for n in ("staged", "hot", "hot_used", "added", "x_hot", "x_used", "x_added", "group_done", "scaled",
                             "turn", "ones_set"))
        block = ctx.enter_context(nc.Block())

        @block.gpsimd
        def _(pool):
            if weight is not None:
                pool.memset(rows[:, :, D:D + 1], 1.0).then_inc(ones_set, 1)
            with pool.Fori(0, HG) as it:
                for h in range(2):
                    pool.wait_ge(group_done, 2 * it + h + 1)
                    pool.sem_inc(turn, 1)
                    pool.tensor_copy(stage[:, GROUP * h:GROUP * (h + 1)],
                                     index[:, bass.ds((2 * it + h) * GROUP, GROUP)]).then_inc(staged, 1)
                    pool.wait_ge(staged, 2 * it + h + 1)
                    pool.sem_inc(turn, 1)
                    for k in range(GROUP * h, GROUP * (h + 1)):
                        pool.indirect_dma_start(ring[:, k, :], None, table,
                                                bass.IndirectOffsetOnAxis(ap=stage[:, k:k + 1], axis=0)
                                                ).then_inc(arrived[k], 16)

        if weight is not None:
            @block.scalar
            def _(act):
                with act.Fori(0, HG) as it:
                    for h in range(2):
                        act.wait_ge(group_done, 2 * it + h + 1)
                        for k in range(GROUP * h, GROUP * (h + 1)):
                            act.wait_ge(arrived[k], 16 * it + 16)
                            act.sem_inc(turn, 1)
                            act.activation(rows[:, k, 0:D], ring[:, k, :], ACT.Copy,
                                           scale=weight[:, bass.ds(it * RING + k, 1)]).then_inc(scaled, 1)

        @block.vector
        def _(dve):
            dve.sem_inc(added, 2)
            dve.sem_inc(x_added, 1)

            def build(it, h, window):
                for k in range(GROUP * h, GROUP * (h + 1)):
                    dve.wait_ge(hot_used, RING * it + k + 1)
                    one_hot(dve, st, onehot[:, k, :], window, it * RING + k).then_inc(hot, 1)

            def trip(it, ahead):
                ranges = group_ranges(nc, dve, st, it)
                later = group_ranges(nc, dve, st, it + 1) if ahead else None
                for h in range(2):
                    if ahead:
                        build(it + 1, h, later[h][0])
                    first, _, before = ranges[h]
                    dve.wait_ge(hot_used, RING * it + GROUP * (h + 1) + 2 * GROUP)
                    dve.wait_ge(added, 2 * it + h + 2)
                    dve.wait_ge(x_added, before + 1)
                    here = st.acc[:, bass.ds(first * WIDE, width)]
                    dve.tensor_tensor(here, here, total[h][:, 0:width], ALU.add).then_inc(added, 1)
                    more_steps(nc, dve, st, ranges, it, h, x_onehot, x_total, width, added, x_hot, x_used, x_added)

            ranges = group_ranges(nc, dve, st, 0)
            for h in range(2):
                build(0, h, ranges[h][0])
            with dve.Fori(0, HG - 1) as it:
                trip(it, True)
            trip(HG - 1, False)

        @block.tensor
        def _(pe):
            pe.sem_inc(hot_used, RING)
            pe.sem_inc(x_used, GROUP)
            pe.sem_inc(group_done, 2)
            if weight is not None:
                pe.wait_ge(ones_set, 1)
            with pe.Fori(0, HG) as it:
                ranges = group_ranges(nc, pe, st, it)
                for h in range(2):
                    pe.wait_ge(added, 2 * it + h + 1)
                    for k in range(GROUP * h, GROUP * (h + 1)):
                        if weight is None:
                            pe.wait_ge(arrived[k], 16 * it + 16)
                        else:
                            pe.wait_ge(scaled, RING * it + k + 1)
                        pe.wait_ge(hot, RING * it + k + 1)
                        pe.matmul(total[h][:, 0:width], onehot[:, k, :], rows[:, k, 0:width],
                                  start=(k % GROUP == 0), stop=(k % GROUP == GROUP - 1)).then_inc(hot_used, 1)
                    _, more, before = ranges[h]
                    with pe.If(more > 0):
                        with pe.Fori(0, more) as j:
                            extra = before + j
                            pe.wait_ge(x_added, extra + 1)
                            for k in range(GROUP):
                                pe.wait_ge(x_hot, GROUP * extra + k + 1)
                                pe.matmul(x_total[:, 0:width], x_onehot[:, k, :], rows[:, GROUP * h + k, 0:width],
                                          start=(k == 0), stop=(k == GROUP - 1)).then_inc(x_used, 1)
                    pe.drain().then_inc(group_done, 1)


def layer_norm(nc, st, name, source, stride, column=0, out=None, out_column=0, gamma_beta=None):
    out, out_stride = (st.x, D) if out is None else (out, WIDE)
    with ExitStack() as ctx:
        phase_end(nc, ctx)
        def sb(part, shape):
            return ctx.enter_context(nc.sbuf_tensor(name + part, shape, F32))

        def sem(part):
            return phase_semaphore(nc, ctx, name + part)

        stats, total, diff, square, std = sb("stats", [P, NW, 6]), sb("total", [P, NW]), sb("diff", [P, NW]), \
            sb("square", [P, NW]), sb("std", [P, NW])
        mean, var, rstd = sb("mean", [P, NW]), sb("var", [P, NW]), sb("rstd", [P, NW])
        counted, chain, var_set, rooted, normed = (sem(n) for n in ("counted", "chain", "var_set", "rooted", "normed"))
        loaded = sem("loaded")
        if gamma_beta is not None:
            gamma, beta = sb("gamma", [P, D]), sb("beta", [P, D])
        block = ctx.enter_context(nc.Block())

        if gamma_beta is not None:
            @block.sync
            def _(sp):
                sp.dma_start(gamma[:], gamma_beta[0].partition_broadcast(P)).then_inc(loaded, 16)
                sp.dma_start(beta[:], gamma_beta[1].partition_broadcast(P)).then_inc(loaded, 16)
                sp.wait_ge(loaded, 32)

        @block.vector
        def _(dve):
            done = [0]

            def link(ins_):
                done[0] += 1
                ins_.then_inc(chain, 1)
                dve.wait_ge(chain, done[0])

            with dve.Fori(0, NW) as w:
                dve.bn_stats(stats[:, :, :].rearrange("p w s -> p (w s)")[:, bass.ds(6 * w, 6)],
                             source[:, bass.ds(stride * w + column, D)]).then_inc(counted, 1)
            dve.wait_ge(counted, NW)
            dve.tensor_tensor(total[:], stats[:, :, 1], stats[:, :, 4], ALU.add)
            dve.tensor_tensor(square[:], stats[:, :, 2], stats[:, :, 5], ALU.add)
            link(dve.tensor_tensor(diff[:], stats[:, :, 1], stats[:, :, 4], ALU.subtract))
            dve.tensor_single_scalar(mean[:], total[:], 0.5, ALU.mult)
            link(dve.scalar_tensor_tensor(out=diff[:], in0=diff[:], scalar=0.25, in1=diff[:], op0=ALU.mult, op1=ALU.mult))
            link(dve.scalar_tensor_tensor(out=var[:], in0=square[:], scalar=1.0 / D, in1=diff[:], op0=ALU.mult, op1=ALU.add))
            dve.tensor_single_scalar(var[:], var[:], EPS, ALU.add).then_inc(var_set, 1)
            dve.wait_ge(rooted, 1)
            link(dve.reciprocal(rstd[:], std[:]))
            with dve.Fori(0, NW) as w:
                dve.tensor_scalar(out[:, bass.ds(out_stride * w + out_column, D)], source[:, bass.ds(stride * w + column, D)],
                                  mean[:, bass.ds(w, 1)], rstd[:, bass.ds(w, 1)], ALU.subtract, ALU.mult).then_inc(normed, 1)
            dve.wait_ge(normed, NW)
            if gamma_beta is not None:
                dve.wait_ge(loaded, 32)
                view = out[:].rearrange("p (w f) -> p w f", w=NW)[:, :, out_column:out_column + D]
                link(dve.tensor_tensor(view, view, gamma[:].unsqueeze(1).broadcast_to([P, NW, D]), ALU.mult))
                link(dve.tensor_tensor(view, view, beta[:].unsqueeze(1).broadcast_to([P, NW, D]), ALU.add))

        @block.scalar
        def _(act):
            act.wait_ge(var_set, 1)
            act.activation(std[:], var[:], ACT.Sqrt).then_inc(rooted, 1)


def scale_to_table(nc, st, name, table):
    with ExitStack() as ctx:
        phase_end(nc, ctx)
        def sem(part):
            return phase_semaphore(nc, ctx, name + part)

        scaled, stored, chain, rooted = (sem(n) for n in ("scaled", "stored", "chain", "rooted"))
        std = ctx.enter_context(nc.sbuf_tensor(name + "std", [P, NW], F32))
        block = ctx.enter_context(nc.Block())

        @block.vector
        def _(dve):
            acc = st.acc[:].rearrange("p (w f) -> p w f", w=NW)
            dve.tensor_copy(st.in_edges[:], acc[:, :, D]).then_inc(chain, 1)
            dve.tensor_single_scalar(st.degree[:], acc[:, :, D], 1.0, ALU.add).then_inc(chain, 1)
            dve.wait_ge(rooted, 1)
            dve.reciprocal(st.dinv[:], std[:]).then_inc(chain, 1)
            dve.wait_ge(chain, 3)
            with dve.Fori(0, NW) as w:
                dve.tensor_scalar(st.acc[:, bass.ds(WIDE * w, D)], st.x[:, bass.ds(D * w, D)],
                                  st.dinv[:, bass.ds(w, 1)], None, ALU.mult).then_inc(scaled, 1)

        @block.scalar
        def _(act):
            act.wait_ge(chain, 2)
            act.activation(std[:], st.degree[:], ACT.Sqrt).then_inc(rooted, 1)

        @block.sync
        def _(sp):
            sp.wait_ge(scaled, NW)
            sp.dma_start(table.rearrange("(w p) f -> p w f", p=P),
                         st.acc[:].rearrange("p (w f) -> p w f", w=NW)[:, :, 0:D]).then_inc(stored, 16)
            sp.wait_ge(stored, 16)


def layer1_nodes(nc, st, ins):
    KC = D // P
    with ExitStack() as ctx:
        phase_end(nc, ctx)
        def sb(name, shape):
            return ctx.enter_context(nc.sbuf_tensor("l1_" + name, shape, F32))

        def psum(name):
            return [ctx.enter_context(nc.psum_tensor(f"l1_{name}{h}", [P, 512], F32)) for h in range(2)]

        def sem(name):
            return phase_semaphore(nc, ctx, "l1_" + name)

        w1, w2, b1 = sb("w1", [P, KC, HID1]), sb("w2", [HR, HC, D]), sb("b1", [HR, HC])
        y, y_t, z_t = sb("y", [P, 2, D]), sb("y_t", [P, 2, KC, P]), sb("z_t", [HR, 2, HC, P])
        turned, hidden, back = psum("turned"), psum("hidden"), psum("back")
        loaded, y_set, y_turned, y_t_set, z_sum, z_set, back_sum, acc_set, stored = (
            sem(n) for n in ("loaded", "y_set", "y_turned", "y_t_set", "z_sum", "z_set", "back_sum", "acc_set", "stored"))
        turn = sem("turn")
        block = ctx.enter_context(nc.Block())

        @block.sync
        def _(sp):
            sp.dma_start(w1[:], ins["L1_w1"].rearrange("(c k) h -> k c h", c=KC)).then_inc(loaded, 16)
            sp.dma_start(w2[:], ins["L1_w2"].rearrange("(c k) f -> k c f", c=HC)).then_inc(loaded, 16)
            sp.dma_start(b1[:], ins["L1_b1"].rearrange("(c k) -> k c", c=HC), allow_slow_non_contiguous=True).then_inc(loaded, 16)
            sp.wait_ge(loaded, 48)
            sp.wait_ge(acc_set, NW + 2)
            sp.dma_start(st.table2.rearrange("(w p) f -> p w f", p=P),
                         st.acc[:].rearrange("p (w f) -> p w f", w=NW)[:, :, 0:D]).then_inc(stored, 16)
            sp.wait_ge(stored, 16)

        @block.vector
        def _(dve):
            dve.sem_inc(acc_set, 2)
            with dve.Fori(0, HW) as it:
                for h in range(2):
                    dve.wait_ge(y_turned, 2 * it + h + 1)
                    dve.tensor_scalar(y[:, h, :], st.acc[:, bass.ds((2 * it + h) * WIDE, D)],
                                      st.dinv[:, bass.ds(2 * it + h, 1)], None, ALU.mult).then_inc(y_set, 1)
                for h in range(2):
                    dve.wait_ge(back_sum, 2 * it + h + 3)
                    dve.tensor_scalar(st.acc[:, bass.ds((2 * it + h) * WIDE, D)], back[h][:, 0:D],
                                      st.dinv[:, bass.ds(2 * it + h, 1)], None, ALU.mult).then_inc(acc_set, 1)

        @block.tensor
        def _(pe):
            pe.sem_inc(y_turned, 2)
            pe.sem_inc(back_sum, 2)
            pe.wait_ge(loaded, 48)
            with pe.Fori(0, HW) as it:
                for h in range(2):
                    pe.wait_ge(y_set, 2 * it + h + 1)
                    for k in range(KC):
                        last = pe.transpose(turned[h][:, k * P:(k + 1) * P], y[:, h, k * P:(k + 1) * P], st.ident[:])
                    last.then_inc(y_turned, 1)
                for h in range(2):
                    pe.wait_ge(y_t_set, 2 * it + h + 1)
                    for c in range(HC):
                        for k in range(KC):
                            last = pe.matmul(hidden[h][0:HR, c * P:(c + 1) * P], w1[:, k, c * HR:(c + 1) * HR],
                                             y_t[:, h, k, :], start=(k == 0), stop=(k == KC - 1))
                    last.then_inc(z_sum, 1)
                for h in range(2):
                    pe.wait_ge(z_set, 2 * it + h + 1)
                    pe.wait_ge(acc_set, 2 * it + h + 1)
                    for c in range(HC):
                        last = pe.matmul(back[h][:, 0:D], z_t[:, h, c, :], w2[:, c, :], start=(c == 0), stop=(c == HC - 1))
                    last.then_inc(back_sum, 1)

        @block.scalar
        def _(act):
            with act.Fori(0, HW) as it:
                for h in range(2):
                    act.wait_ge(y_turned, 2 * it + h + 3)
                    act.activation(y_t[:, h, :, :], turned[h][:, 0:D].rearrange("p (k n) -> p k n", k=KC), ACT.Copy
                                   ).then_inc(y_t_set, 1)
                for h in range(2):
                    act.wait_ge(z_sum, 2 * it + h + 1)
                    act.wait_ge(back_sum, 2 * it + h + 1)
                    for c in range(HC):
                        last = act.activation(z_t[:, h, c, :], hidden[h][0:HR, c * P:(c + 1) * P], ACT.Relu,
                                              bias=b1[:, c:c + 1])
                    last.then_inc(z_set, 1)


def layer1_end(nc, st, ins):
    with ExitStack() as ctx:
        phase_end(nc, ctx)
        b2 = ctx.enter_context(nc.sbuf_tensor("l1_b2", [P, D], F32))
        loaded, added = (phase_semaphore(nc, ctx, "l1_end_" + n) for n in ("loaded", "added"))
        block = ctx.enter_context(nc.Block())

        @block.sync
        def _(sp):
            sp.dma_start(b2[:], ins["L1_b2"].partition_broadcast(P)).then_inc(loaded, 16)
            sp.wait_ge(loaded, 16)

        @block.vector
        def _(dve):
            acc = st.acc[:].rearrange("p (w f) -> p w f", w=NW)[:, :, 0:D]
            with dve.Fori(0, NW) as w:
                here = st.acc[:, bass.ds(WIDE * w, D)]
                dve.scalar_tensor_tensor(out=here, in0=here, scalar=st.dinv[:, bass.ds(w, 1)],
                                         in1=st.x[:, bass.ds(D * w, D)], op0=ALU.mult, op1=ALU.add).then_inc(added, 1)
            dve.wait_ge(added, NW)
            dve.wait_ge(loaded, 16)
            dve.tensor_tensor(acc, acc, b2[:].unsqueeze(1).broadcast_to([P, NW, D]), ALU.add).then_inc(added, 1)


def layer1(nc, st, ins):
    scale_to_table(nc, st, "l1_scale_", st.table1)
    aggregate(nc, st, "l1a_", st.table1, st.src, None)
    layer1_nodes(nc, st, ins)
    aggregate(nc, st, "l1b_", st.table2, st.src, None)
    layer1_end(nc, st, ins)
    layer_norm(nc, st, "ln1_", st.acc, WIDE)


def layer2_tables(nc, st, ins):
    KC = D // P
    with ExitStack() as ctx:
        phase_end(nc, ctx)
        def sb(name, shape):
            return ctx.enter_context(nc.sbuf_tensor("l2t_" + name, shape, F32))

        def psum(name):
            return [ctx.enter_context(nc.psum_tensor(f"l2t_{name}{h}", [P, 512], F32)) for h in range(2)]

        def sem(name):
            return phase_semaphore(nc, ctx, "l2t_" + name)

        w_nodes, b1 = sb("w_nodes", [P, 2 * KC, HID2]), sb("b1", [P, HID2])
        x, x_t, rows = sb("x", [P, 2, D]), sb("x_t", [P, 2, KC, P]), sb("rows", [P, 2, 2 * HID2])
        turned, of_src, of_dst = psum("turned"), psum("of_src"), psum("of_dst")
        loaded, x_set, x_turned, x_t_set, src_sum, dst_sum, src_out, dst_out, cleared = (
            sem(n) for n in ("loaded", "x_set", "x_turned", "x_t_set", "src_sum", "dst_sum", "src_out", "dst_out", "cleared"))
        stored = [sem("stored0"), sem("stored1")]
        turn = sem("turn")
        block = ctx.enter_context(nc.Block())

        @block.sync
        def _(sp):
            sp.dma_start(w_nodes[:], ins["L2_eW1"][0:2 * D, :].rearrange("(c k) h -> k c h", k=P)).then_inc(loaded, 16)
            sp.dma_start(b1[:], ins["L2_eb1"].partition_broadcast(P)).then_inc(loaded, 16)
            sp.sem_inc(stored[0], 16)
            sp.sem_inc(stored[1], 16)
            sp.wait_ge(loaded, 32)
            with sp.Fori(0, HW) as it:
                for h in range(2):
                    sp.wait_ge(src_out, 2 * it + h + 3)
                    sp.wait_ge(dst_out, 2 * it + h + 3)
                    here = bass.ds((2 * it + h) * P, P)
                    sp.dma_start(st.src_rows[here, :], rows[:, h, 0:HID2]).then_inc(stored[h], 16)
                    sp.dma_start(st.dst_rows[here, :], rows[:, h, HID2:2 * HID2]).then_inc(stored[h], 16)
            for h in range(2):
                sp.wait_ge(stored[h], 32 * HW + 16)

        @block.gpsimd
        def _(pool):
            pool.memset(st.acc[:], 0.0).then_inc(cleared, 1)

        @block.scalar
        def _(act):
            act.sem_inc(src_out, 2)
            with act.Fori(0, HW) as it:
                for h in range(2):
                    act.wait_ge(x_turned, 2 * it + h + 1)
                    act.sem_inc(turn, 1)
                    act.activation(x[:, h, :], st.x[:, bass.ds((2 * it + h) * D, D)], ACT.Copy).then_inc(x_set, 1)
                for h in range(2):
                    act.wait_ge(x_turned, 2 * it + h + 3)
                    act.wait_ge(dst_sum, 2 * it + h + 1)
                    act.activation(x_t[:, h, :, :], turned[h][:, 0:D].rearrange("p (k n) -> p k n", k=KC), ACT.Copy
                                   ).then_inc(x_t_set, 1)
                for h in range(2):
                    act.wait_ge(src_sum, 2 * it + h + 1)
                    act.wait_ge(stored[h], 32 * it + 16)
                    act.activation(rows[:, h, 0:HID2], of_src[h][:], ACT.Copy).then_inc(src_out, 1)

        @block.vector
        def _(dve):
            dve.sem_inc(dst_out, 2)
            dve.wait_ge(loaded, 32)
            with dve.Fori(0, HW) as it:
                for h in range(2):
                    dve.wait_ge(dst_sum, 2 * it + h + 3)
                    dve.wait_ge(stored[h], 32 * it + 16)
                    dve.tensor_tensor(rows[:, h, HID2:2 * HID2], of_dst[h][:], b1[:], ALU.add).then_inc(dst_out, 1)

        @block.tensor
        def _(pe):
            pe.sem_inc(x_turned, 2)
            pe.sem_inc(dst_sum, 2)
            pe.wait_ge(loaded, 32)
            with pe.Fori(0, HW) as it:
                for h in range(2):
                    pe.wait_ge(x_set, 2 * it + h + 1)
                    for k in range(KC):
                        last = pe.transpose(turned[h][:, k * P:(k + 1) * P], x[:, h, k * P:(k + 1) * P], st.ident[:])
                    last.then_inc(x_turned, 1)
                for h in range(2):
                    pe.wait_ge(x_t_set, 2 * it + h + 1)
                    pe.wait_ge(src_out, 2 * it + h + 1)
                    pe.wait_ge(dst_out, 2 * it + h + 1)
                    for part, bank, summed in ((0, of_src, src_sum), (1, of_dst, dst_sum)):
                        for k in range(KC):
                            last = pe.matmul(bank[h][:], x_t[:, h, k, :], w_nodes[:, KC * part + k, :],
                                             start=(k == 0), stop=(k == KC - 1))
                        last.then_inc(summed, 1)


def layer2_edges(nc, st, ins):
    with ExitStack() as ctx:
        phase_end(nc, ctx)

        def sb(name, shape, dt=F32):
            return ctx.enter_context(nc.sbuf_tensor("l2e_" + name, shape, dt))

        def sem(name):
            return phase_semaphore(nc, ctx, "l2e_" + name)

        w_edge, attr_t = sb("w_edge", [EDIM, HID2]), sb("attr_t", [EDIM, 2, GROUP * P])
        from_src, from_dst, hidden = (sb(n, [P, RING, HID2]) for n in ("from_src", "from_dst", "hidden"))
        stage_src, stage_dst = sb("stage_src", [P, RING], I32), sb("stage_dst", [P, RING], I32)
        onehot, x_onehot = sb("onehot", [P, RING, P]), sb("x_onehot", [P, GROUP, P])
        edge_sum = [ctx.enter_context(nc.psum_tensor(f"l2e_edge_sum{k}", [P, HID2], F32)) for k in range(GROUP)]
        total = [ctx.enter_context(nc.psum_tensor(f"l2e_total{h}", [P, HID2], F32)) for h in range(2)]
        x_total = ctx.enter_context(nc.psum_tensor("l2e_x_total", [P, HID2], F32))
        src_in = [sem(f"src_in{k}") for k in range(RING)]
        dst_in = [sem(f"dst_in{k}") for k in range(RING)]
        attr_in = [sem("attr_in0"), sem("attr_in1")]
        w_in, staged, attr_summed, half_added, all_added, relued, hot, hot_used, added, x_hot, x_used, x_added, turn = (
            sem(n) for n in ("w_in", "staged", "attr_summed", "half_added", "all_added", "relued", "hot", "hot_used",
                             "added", "x_hot", "x_used", "x_added", "turn"))
        block = ctx.enter_context(nc.Block())

        @block.sync
        def _(sp):
            sp.dma_start(w_edge[:], ins["L2_eW1"][2 * D:2 * D + EDIM, :]).then_inc(w_in, 16)
            with sp.Fori(0, HG) as it:
                for h in range(2):
                    sp.wait_ge(attr_summed, RING * it + GROUP * (h + 1))
                    sp.dma_start(attr_t[:, h, :], ins["edge_attr_t"][:, bass.ds((2 * it + h) * GROUP * P, GROUP * P)]
                                 ).then_inc(attr_in[h], 16)
            sp.wait_ge(w_in, 16)

        @block.gpsimd
        def _(pool):
            pool.sem_inc(all_added, RING)
            with pool.Fori(0, HG) as it:
                for h in range(2):
                    half = slice(GROUP * h, GROUP * (h + 1))
                    pool.wait_ge(all_added, RING * it + GROUP * (h + 1))
                    pool.sem_inc(turn, 1)
                    for stage, index in ((stage_src, st.src), (stage_dst, st.dst_row)):
                        pool.tensor_copy(stage[:, half], index[:, bass.ds((2 * it + h) * GROUP, GROUP)]).then_inc(staged, 1)
                    pool.wait_ge(staged, 4 * it + 2 * h + 2)
                    pool.sem_inc(turn, 1)
                    for k in range(GROUP * h, GROUP * (h + 1)):
                        for ring, stage, table, arrived in ((from_src, stage_src, st.src_rows, src_in),
                                                            (from_dst, stage_dst, st.dst_rows, dst_in)):
                            pool.indirect_dma_start(ring[:, k, :], None, table,
                                                    bass.IndirectOffsetOnAxis(ap=stage[:, k:k + 1], axis=0)
                                                    ).then_inc(arrived[k], 16)

        @block.scalar
        def _(act):
            with act.Fori(0, HG) as it:
                for k in range(RING):
                    act.wait_ge(all_added, RING * it + k + 1 + RING)
                    act.activation(hidden[:, k, :], hidden[:, k, :], ACT.Relu).then_inc(relued, 1)

        @block.vector
        def _(dve):
            dve.sem_inc(added, 2)
            dve.sem_inc(x_added, 1)

            def build(it, h, window):
                for k in range(GROUP * h, GROUP * (h + 1)):
                    dve.wait_ge(hot_used, RING * it + k + 1)
                    one_hot(dve, st, onehot[:, k, :], window, it * RING + k).then_inc(hot, 1)

            def messages(it, h):
                for k in range(GROUP * h, GROUP * (h + 1)):
                    dve.wait_ge(attr_summed, RING * it + k + 1 + RING)
                    dve.wait_ge(src_in[k], 16 * it + 16)
                    dve.tensor_tensor(hidden[:, k, :], edge_sum[k % GROUP][:], from_src[:, k, :], ALU.add
                                      ).then_inc(half_added, 1)
                for k in range(GROUP * h, GROUP * (h + 1)):
                    dve.wait_ge(half_added, RING * it + k + 1 + GROUP)
                    dve.wait_ge(dst_in[k], 16 * it + 16)
                    dve.tensor_tensor(hidden[:, k, :], hidden[:, k, :], from_dst[:, k, :], ALU.add
                                      ).then_inc(all_added, 1)

            def trip(it, ahead):
                ranges = group_ranges(nc, dve, st, it)
                later = group_ranges(nc, dve, st, it + 1) if ahead else None
                for h in range(2):
                    first, _, before = ranges[h]
                    dve.wait_ge(hot_used, RING * it + GROUP * (h + 1) + 2 * GROUP)
                    dve.wait_ge(added, 2 * it + h + 2)
                    dve.wait_ge(x_added, before + 1)
                    here = st.acc[:, bass.ds(first * WIDE, HID2)]
                    dve.tensor_tensor(here, here, total[h][:], ALU.add).then_inc(added, 1)
                    more_steps(nc, dve, st, ranges, it, h, x_onehot, x_total, HID2, added, x_hot, x_used, x_added)
                    if ahead:
                        build(it + 1, h, later[h][0])
                        messages(it + 1, h)

            ranges = group_ranges(nc, dve, st, 0)
            for h in range(2):
                build(0, h, ranges[h][0])
                messages(0, h)
            with dve.Fori(0, HG - 1) as it:
                trip(it, True)
            trip(HG - 1, False)

        @block.tensor
        def _(pe):
            pe.sem_inc(hot_used, RING)
            pe.sem_inc(x_used, GROUP)
            pe.sem_inc(half_added, GROUP)
            pe.sem_inc(attr_summed, RING)
            pe.wait_ge(w_in, 16)

            def attributes(it, h):
                pe.wait_ge(attr_in[h], 16 * it + 16)
                for k in range(GROUP):
                    pe.wait_ge(half_added, RING * it + GROUP * h + k + 1)
                    pe.matmul(edge_sum[k][:], attr_t[:, h, k * P:(k + 1) * P], w_edge[:],
                              start=True, stop=True).then_inc(attr_summed, 1)

            def trip(it, ahead):
                ranges = group_ranges(nc, pe, st, it)
                for h in range(2):
                    pe.wait_ge(added, 2 * it + h + 1)
                    for k in range(GROUP * h, GROUP * (h + 1)):
                        pe.wait_ge(relued, RING * it + k + 1)
                        pe.wait_ge(hot, RING * it + k + 1)
                        pe.matmul(total[h][:], onehot[:, k, :], hidden[:, k, :],
                                  start=(k % GROUP == 0), stop=(k % GROUP == GROUP - 1)).then_inc(hot_used, 1)
                    _, more, before = ranges[h]
                    with pe.If(more > 0):
                        with pe.Fori(0, more) as j:
                            extra = before + j
                            pe.wait_ge(x_added, extra + 1)
                            for k in range(GROUP):
                                pe.wait_ge(x_hot, GROUP * extra + k + 1)
                                pe.matmul(x_total[:], x_onehot[:, k, :], hidden[:, GROUP * h + k, :],
                                          start=(k == 0), stop=(k == GROUP - 1)).then_inc(x_used, 1)
                    if ahead:
                        attributes(it + 1, h)

            attributes(0, 0)
            attributes(0, 1)
            with pe.Fori(0, HG - 1) as it:
                trip(it, True)
            trip(HG - 1, False)


def layer2_nodes(nc, st, ins):
    KC, HCH = D // P, HID2 // P
    with ExitStack() as ctx:
        phase_end(nc, ctx)
        def sb(name, shape):
            return ctx.enter_context(nc.sbuf_tensor("l2n_" + name, shape, F32))

        def psum(name):
            return [ctx.enter_context(nc.psum_tensor(f"l2n_{name}{h}", [P, 512], F32)) for h in range(2)]

        def sem(name):
            return phase_semaphore(nc, ctx, "l2n_" + name)

        e_w2, n_w1, n_w2 = sb("e_w2", [P, HCH, D]), sb("n_w1", [P, 2 * KC, HID2]), sb("n_w2", [P, HCH, D])
        e_b2, n_b1, n_b2 = sb("e_b2", [P, D]), sb("n_b1", [P, HCH]), sb("n_b2", [P, D])
        sums, sums_t = sb("sums", [P, 2, HID2]), sb("sums_t", [P, 2, HCH, P])
        both, both_t = sb("both", [P, 2, 2 * D]), sb("both_t", [P, 2, 2 * KC, P])
        hidden_t = sb("hidden_t", [P, 2, HCH, P])
        sums_turned, both_turned, hidden = psum("sums_turned"), psum("both_turned"), psum("hidden")
        outs = psum("outs")
        (loaded, slots_set, turned_a, sums_t_set, agg_sum, agg_set, turned_b, both_t_set, hidden_sum, hidden_set,
         upd_sum, upd_set, turn) = (sem(n) for n in (
             "loaded", "slots_set", "turned_a", "sums_t_set", "agg_sum", "agg_set", "turned_b", "both_t_set",
             "hidden_sum", "hidden_set", "upd_sum", "upd_set", "turn"))
        LOADS = 6
        block = ctx.enter_context(nc.Block())

        @block.sync
        def _(sp):
            sp.dma_start(e_w2[:], ins["L2_eW2"].rearrange("(c k) f -> k c f", k=P)).then_inc(loaded, 16)
            sp.dma_start(n_w1[:], ins["L2_nW1"].rearrange("(c k) f -> k c f", k=P)).then_inc(loaded, 16)
            sp.dma_start(n_w2[:], ins["L2_nW2"].rearrange("(c k) f -> k c f", k=P)).then_inc(loaded, 16)
            sp.dma_start(n_b1[:], ins["L2_nb1"].rearrange("(c k) -> k c", k=P), allow_slow_non_contiguous=True).then_inc(loaded, 16)
            sp.dma_start(e_b2[:], ins["L2_eb2"].partition_broadcast(P)).then_inc(loaded, 16)
            sp.dma_start(n_b2[:], ins["L2_nb2"].partition_broadcast(P)).then_inc(loaded, 16)
            sp.wait_ge(loaded, LOADS * 16)

        @block.scalar
        def _(act):
            act.wait_ge(loaded, LOADS * 16)
            with act.Fori(0, HW) as it:
                for h in range(2):
                    act.wait_ge(turned_a, 2 * it + h + 1)
                    act.wait_ge(turned_b, 2 * it + h + 1)
                    act.sem_inc(turn, 1)
                    act.activation(sums[:, h, :], st.acc[:, bass.ds((2 * it + h) * WIDE, HID2)], ACT.Copy)
                    act.activation(both[:, h, 0:D], st.x[:, bass.ds((2 * it + h) * D, D)], ACT.Copy).then_inc(slots_set, 1)
                for h in range(2):
                    act.wait_ge(turned_a, 2 * it + h + 3)
                    act.wait_ge(agg_sum, 2 * it + h + 1)
                    act.activation(sums_t[:, h, :, :], sums_turned[h][:].rearrange("p (k n) -> p k n", k=HCH), ACT.Copy
                                   ).then_inc(sums_t_set, 1)
                for h in range(2):
                    act.wait_ge(turned_b, 2 * it + h + 3)
                    act.wait_ge(hidden_sum, 2 * it + h + 1)
                    act.activation(both_t[:, h, :, :], both_turned[h][:].rearrange("p (k n) -> p k n", k=2 * KC), ACT.Copy
                                   ).then_inc(both_t_set, 1)
                for h in range(2):
                    act.wait_ge(hidden_sum, 2 * it + h + 3)
                    act.wait_ge(upd_sum, 2 * it + h + 1)
                    for c in range(HCH):
                        last = act.activation(hidden_t[:, h, c, :], hidden[h][:, c * P:(c + 1) * P], ACT.Relu,
                                              bias=n_b1[:, c:c + 1])
                    last.then_inc(hidden_set, 1)

        @block.vector
        def _(dve):
            dve.sem_inc(upd_set, 2)
            dve.wait_ge(loaded, LOADS * 16)
            with dve.Fori(0, HW) as it:
                for h in range(2):
                    dve.wait_ge(agg_sum, 2 * it + h + 3)
                    dve.scalar_tensor_tensor(out=both[:, h, D:2 * D], in0=e_b2[:],
                                             scalar=st.in_edges[:, bass.ds(2 * it + h, 1)], in1=outs[h][:, 0:D],
                                             op0=ALU.mult, op1=ALU.add).then_inc(agg_set, 1)
                for h in range(2):
                    dve.wait_ge(upd_sum, 2 * it + h + 3)
                    dve.tensor_tensor(st.acc[:, bass.ds((2 * it + h) * WIDE, D)], outs[h][:, D:2 * D], n_b2[:], ALU.add
                                      ).then_inc(upd_set, 1)

        @block.tensor
        def _(pe):
            for credit in (turned_a, turned_b, agg_sum, hidden_sum, upd_sum):
                pe.sem_inc(credit, 2)
            pe.wait_ge(loaded, LOADS * 16)
            with pe.Fori(0, HW) as it:
                for h in range(2):
                    pe.wait_ge(slots_set, 2 * it + h + 1)
                    for k in range(HCH):
                        last = pe.transpose(sums_turned[h][:, k * P:(k + 1) * P], sums[:, h, k * P:(k + 1) * P], st.ident[:])
                    last.then_inc(turned_a, 1)
                for h in range(2):
                    pe.wait_ge(sums_t_set, 2 * it + h + 1)
                    pe.wait_ge(upd_set, 2 * it + h + 1)
                    for k in range(HCH):
                        last = pe.matmul(outs[h][:, 0:D], sums_t[:, h, k, :], e_w2[:, k, :],
                                         start=(k == 0), stop=(k == HCH - 1))
                    last.then_inc(agg_sum, 1)
                for h in range(2):
                    pe.wait_ge(agg_set, 2 * it + h + 1)
                    for k in range(2 * KC):
                        last = pe.transpose(both_turned[h][:, k * P:(k + 1) * P], both[:, h, k * P:(k + 1) * P], st.ident[:])
                    last.then_inc(turned_b, 1)
                for h in range(2):
                    pe.wait_ge(both_t_set, 2 * it + h + 1)
                    for c in range(HCH):
                        for k in range(2 * KC):
                            last = pe.matmul(hidden[h][:, c * P:(c + 1) * P], n_w1[:, k, c * P:(c + 1) * P],
                                             both_t[:, h, k, :], start=(k == 0), stop=(k == 2 * KC - 1))
                    last.then_inc(hidden_sum, 1)
                for h in range(2):
                    pe.wait_ge(hidden_set, 2 * it + h + 1)
                    for k in range(HCH):
                        last = pe.matmul(outs[h][:, D:2 * D], hidden_t[:, h, k, :], n_w2[:, k, :],
                                         start=(k == 0), stop=(k == HCH - 1))
                    last.then_inc(upd_sum, 1)


def add_x(nc, st, name, column):
    with ExitStack() as ctx:
        phase_end(nc, ctx)
        added = phase_semaphore(nc, ctx, name + "added")
        block = ctx.enter_context(nc.Block())

        @block.vector
        def _(dve):
            acc = st.acc[:].rearrange("p (w f) -> p w f", w=NW)[:, :, column:column + D]
            dve.tensor_tensor(acc, acc, st.x[:].rearrange("p (w f) -> p w f", w=NW), ALU.add).then_inc(added, 1)


def layer2(nc, st, ins):
    layer2_tables(nc, st, ins)
    layer2_edges(nc, st, ins)
    layer2_nodes(nc, st, ins)
    add_x(nc, st, "l2_first_", 0)
    layer_norm(nc, st, "ln2_", st.acc, WIDE, out=st.acc, out_column=D, gamma_beta=(ins["L2_ln_gamma"], ins["L2_ln_beta"]))
    add_x(nc, st, "l2_second_", D)
    layer_norm(nc, st, "ln3_", st.acc, WIDE, column=D)


def layer3_nodes(nc, st, ins):
    KC = D // P
    ROW = D + HEADS
    with ExitStack() as ctx:
        phase_end(nc, ctx)
        def sb(name, shape):
            return ctx.enter_context(nc.sbuf_tensor("l3n_" + name, shape, F32))

        def psum(name):
            return [ctx.enter_context(nc.psum_tensor(f"l3n_{name}{h}", [P, 512], F32)) for h in range(2)]

        def sem(name):
            return phase_semaphore(nc, ctx, "l3n_" + name)

        w, att = sb("w", [P, KC, D]), sb("att", [P, 2, D])
        x, x_t, scaled = sb("x", [P, 2, D]), sb("x_t", [P, 2, KC, P]), sb("scaled", [P, 2, 2, D])
        least, most = sb("least", [P, HEADS]), sb("most", [P, HEADS])
        turned, product = psum("turned"), psum("product")
        loaded, x_set, x_turned, x_t_set, summed, h_set, scaled_set, logits_set, chain, negated, reduced, rows_set, stored, turn = (
            sem(n) for n in ("loaded", "x_set", "x_turned", "x_t_set", "summed", "h_set", "scaled_set", "logits_set",
                             "chain", "negated", "reduced", "rows_set", "stored", "turn"))
        block = ctx.enter_context(nc.Block())
        acc = st.acc[:].rearrange("p (w f) -> p w f", w=NW)
        logits = st.logits[:].rearrange("p (w c) -> p w c", w=NW)

        @block.sync
        def _(sp):
            sp.dma_start(w[:], ins["L3_W"].rearrange("(c k) f -> k c f", k=P)).then_inc(loaded, 16)
            sp.dma_start(att[:, 0, :], ins["L3_att_src"].rearrange("h c -> (h c)").partition_broadcast(P)).then_inc(loaded, 16)
            sp.dma_start(att[:, 1, :], ins["L3_att_dst"].rearrange("h c -> (h c)").partition_broadcast(P)).then_inc(loaded, 16)
            sp.wait_ge(loaded, 48)
            sp.wait_ge(rows_set, 2)
            sp.dma_start(st.gat_rows.rearrange("(w p) f -> p w f", p=P), acc[:, :, 0:ROW]).then_inc(stored, 16)
            sp.dma_start(st.gat_logits.rearrange("(w p) f -> p w f", p=P),
                         st.maxima[:].rearrange("p (w c) -> p w c", w=NW)).then_inc(stored, 16)
            sp.wait_ge(stored, 32)

        @block.scalar
        def _(act):
            with act.Fori(0, HW) as it:
                for h in range(2):
                    act.wait_ge(x_turned, 2 * it + h + 1)
                    act.sem_inc(turn, 1)
                    act.activation(x[:, h, :], st.x[:, bass.ds((2 * it + h) * D, D)], ACT.Copy).then_inc(x_set, 1)
                for h in range(2):
                    act.wait_ge(x_turned, 2 * it + h + 3)
                    act.wait_ge(summed, 2 * it + h + 1)
                    act.activation(x_t[:, h, :, :], turned[h][:, 0:D].rearrange("p (k n) -> p k n", k=KC), ACT.Copy
                                   ).then_inc(x_t_set, 1)

        @block.tensor
        def _(pe):
            pe.sem_inc(x_turned, 2)
            pe.sem_inc(summed, 2)
            pe.wait_ge(loaded, 48)
            with pe.Fori(0, HW) as it:
                for h in range(2):
                    pe.wait_ge(x_set, 2 * it + h + 1)
                    for k in range(KC):
                        last = pe.transpose(turned[h][:, k * P:(k + 1) * P], x[:, h, k * P:(k + 1) * P], st.ident[:])
                    last.then_inc(x_turned, 1)
                for h in range(2):
                    pe.wait_ge(x_t_set, 2 * it + h + 1)
                    pe.wait_ge(scaled_set, 2 * it + h + 1)
                    for k in range(KC):
                        last = pe.matmul(product[h][:, 0:D], x_t[:, h, k, :], w[:, k, :], start=(k == 0), stop=(k == KC - 1))
                    last.then_inc(summed, 1)

        @block.vector
        def _(dve):
            dve.sem_inc(scaled_set, 2)
            dve.wait_ge(loaded, 48)
            with dve.Fori(0, HW) as it:
                for h in range(2):
                    dve.wait_ge(summed, 2 * it + h + 3)
                    dve.sem_inc(turn, 1)
                    dve.tensor_copy(st.acc[:, bass.ds((2 * it + h) * WIDE, D)], product[h][:, 0:D]).then_inc(h_set, 1)
                    dve.wait_ge(logits_set, 2 * it + h + 1)
                    dve.tensor_tensor(scaled[:, h, :, :], product[h][:, 0:D].unsqueeze(1).broadcast_to([P, 2, D]), att[:], ALU.mult
                                      ).then_inc(scaled_set, 1)
                for h in range(2):
                    dve.wait_ge(scaled_set, 2 * it + h + 3)
                    dve.sem_inc(turn, 1)
                    dve.tensor_reduce(st.logits[:, bass.ds((2 * it + h) * 2 * HEADS, 2 * HEADS)],
                                      scaled[:, h, :, :].rearrange("p s (a c) -> p (s a) c", c=CH), AX.X, ALU.add
                                      ).then_inc(logits_set, 1)
            dve.wait_ge(h_set, NW)
            dve.wait_ge(logits_set, NW + 2)
            dve.tensor_copy(acc[:, :, D:ROW], logits[:, :, 0:HEADS]).then_inc(rows_set, 1)
            dve.tensor_reduce(least[:], logits[:, :, 0:HEADS].rearrange("p w a -> p a w"), AX.X, ALU.min).then_inc(chain, 1)
            dve.wait_ge(chain, 1)
            dve.tensor_single_scalar(most[:], least[:], -1.0, ALU.mult).then_inc(negated, 1)
            dve.wait_ge(reduced, 1)
            dve.tensor_single_scalar(st.shift[:], st.shift[:], 1.0, ALU.add).then_inc(chain, 1)
            dve.wait_ge(chain, 2)
            dve.tensor_tensor(st.maxima[:].rearrange("p (w c) -> p w c", w=NW), logits[:, :, 0:HEADS],
                              st.shift[:].unsqueeze(1).broadcast_to([P, NW, HEADS]), ALU.add).then_inc(rows_set, 1)

        @block.gpsimd
        def _(pool):
            pool.sem_inc(logits_set, 2)
            pool.wait_ge(negated, 1)
            pool.partition_all_reduce(st.shift[:], most[:], P, bass.bass_isa.ReduceOp.max).then_inc(reduced, 1)


def layer3_maxima(nc, st):
    with ExitStack() as ctx:
        phase_end(nc, ctx)

        def sb(name, shape, dt=F32):
            return ctx.enter_context(nc.sbuf_tensor("l3m_" + name, shape, dt))

        def sem(name):
            return phase_semaphore(nc, ctx, "l3m_" + name)

        ring, stage = sb("ring", [P, RING, HEADS]), sb("stage", [P, RING], I32)
        onehot, x_onehot = sb("onehot", [P, RING, P]), sb("x_onehot", [P, GROUP, P])
        diagonal, highest, x_highest = sb("diagonal", [P, RING, HEADS, P]), sb("highest", [P, 2, HEADS]), sb("x_highest", [P, HEADS])
        spread = [ctx.enter_context(nc.psum_tensor(f"l3m_spread{h}", [P, GROUP, HEADS, P], F32)) for h in range(2)]
        arrived = [sem(f"arrived{k}") for k in range(RING)]
        staged, diag_set, hot, hot_used, reduced, merged, x_hot, x_used, x_reduced, x_merged, turn = (
            sem(n) for n in ("staged", "diag_set", "hot", "hot_used", "reduced", "merged", "x_hot", "x_used",
                             "x_reduced", "x_merged", "turn"))
        block = ctx.enter_context(nc.Block())

        @block.gpsimd
        def _(pool):
            pool.sem_inc(diag_set, RING)
            with pool.Fori(0, HG) as it:
                for h in range(2):
                    pool.wait_ge(diag_set, RING * it + GROUP * (h + 1))
                    pool.sem_inc(turn, 1)
                    pool.tensor_copy(stage[:, GROUP * h:GROUP * (h + 1)],
                                     st.src[:, bass.ds((2 * it + h) * GROUP, GROUP)]).then_inc(staged, 1)
                    pool.wait_ge(staged, 2 * it + h + 1)
                    pool.sem_inc(turn, 1)
                    for k in range(GROUP * h, GROUP * (h + 1)):
                        pool.indirect_dma_start(ring[:, k, :], None, st.gat_logits,
                                                bass.IndirectOffsetOnAxis(ap=stage[:, k:k + 1], axis=0)
                                                ).then_inc(arrived[k], 16)

        @block.scalar
        def _(act):
            with act.Fori(0, HG) as it:
                for h in range(2):
                    act.wait_ge(merged, 2 * it + h + 1)
                    if h == 0:
                        ranges = group_ranges(nc, act, st, it)
                    act.wait_ge(x_merged, ranges[0][2] + 1)
                    for k in range(GROUP * h, GROUP * (h + 1)):
                        act.wait_ge(arrived[k], 16 * it + 16)
                        for a in range(HEADS):
                            last = act.activation(diagonal[:, k, a, :], st.ident[:], ACT.Copy, scale=ring[:, k, a:a + 1])
                        last.then_inc(diag_set, 1)

        @block.vector
        def _(dve):
            dve.sem_inc(x_merged, 1)

            def build(it, h, window):
                for k in range(GROUP * h, GROUP * (h + 1)):
                    dve.wait_ge(hot_used, RING * it + k + 1)
                    one_hot(dve, st, onehot[:, k, :], window, it * RING + k).then_inc(hot, 1)

            def trip(it, ahead):
                ranges = group_ranges(nc, dve, st, it)
                later = group_ranges(nc, dve, st, it + 1) if ahead else None
                for h in range(2):
                    if ahead:
                        build(it + 1, h, later[h][0])
                    first, more, before = ranges[h]
                    dve.wait_ge(hot_used, RING * it + GROUP * (h + 1) + 2 * GROUP)
                    dve.wait_ge(merged, 2 * it + h + 1)
                    dve.tensor_reduce(highest[:, h, :], spread[h][:].rearrange("p k a e -> p a k e"), AX.XY, ALU.max
                                      ).then_inc(reduced, 1)
                    dve.wait_ge(reduced, 2 * it + h + 3)
                    dve.wait_ge(merged, 2 * it + h + 2)
                    dve.wait_ge(x_merged, before + 1)
                    here = st.maxima[:, bass.ds(first * HEADS, HEADS)]
                    dve.tensor_tensor(here, here, highest[:, h, :], ALU.max).then_inc(merged, 1)
                    with dve.If(more > 0):
                        with dve.Fori(0, more) as j:
                            window = within(nc, first + 1 + j, NW - 1)
                            extra = before + j
                            for k in range(GROUP):
                                dve.wait_ge(x_used, GROUP * extra + k + 1)
                                one_hot(dve, st, x_onehot[:, k, :], window, it * RING + GROUP * h + k).then_inc(x_hot, 1)
                            dve.wait_ge(x_used, GROUP * extra + 2 * GROUP)
                            dve.wait_ge(x_merged, extra + 1)
                            dve.tensor_reduce(x_highest[:], spread[h][:].rearrange("p k a e -> p a k e"), AX.XY, ALU.max
                                              ).then_inc(x_reduced, 1)
                            dve.wait_ge(x_reduced, extra + 2)
                            dve.wait_ge(merged, 2 * it + h + 3)
                            here = st.maxima[:, bass.ds(window * HEADS, HEADS)]
                            dve.tensor_tensor(here, here, x_highest[:], ALU.max).then_inc(x_merged, 1)

            dve.sem_inc(merged, 2)
            ranges = group_ranges(nc, dve, st, 0)
            for h in range(2):
                build(0, h, ranges[h][0])
            with dve.Fori(0, HG - 1) as it:
                trip(it, True)
            trip(HG - 1, False)

        @block.tensor
        def _(pe):
            pe.sem_inc(hot_used, RING)
            pe.sem_inc(x_used, GROUP)
            pe.sem_inc(reduced, 2)
            pe.sem_inc(x_reduced, 1)
            with pe.Fori(0, HG) as it:
                ranges = group_ranges(nc, pe, st, it)
                for h in range(2):
                    _, more, before = ranges[h]
                    pe.wait_ge(reduced, 2 * it + h + 1)
                    pe.wait_ge(x_reduced, before + 1)
                    for k in range(GROUP * h, GROUP * (h + 1)):
                        pe.wait_ge(diag_set, RING * it + k + 1 + RING)
                        pe.wait_ge(hot, RING * it + k + 1)
                        pe.matmul(spread[h][:, k % GROUP, :, :], onehot[:, k, :], diagonal[:, k, :, :],
                                  start=True, stop=True).then_inc(hot_used, 1)
                    with pe.If(more > 0):
                        with pe.Fori(0, more) as j:
                            extra = before + j
                            pe.wait_ge(reduced, 2 * it + h + 3)
                            pe.wait_ge(x_reduced, extra + 1)
                            for k in range(GROUP):
                                pe.wait_ge(x_hot, GROUP * extra + k + 1)
                                pe.matmul(spread[h][:, k, :, :], x_onehot[:, k, :], diagonal[:, GROUP * h + k, :, :],
                                          start=True, stop=True).then_inc(x_used, 1)


def layer3_self_loops(nc, st):
    with ExitStack() as ctx:
        phase_end(nc, ctx)
        def sb(name, shape):
            return ctx.enter_context(nc.sbuf_tensor("l3s_" + name, shape, F32))

        def sem(name):
            return phase_semaphore(nc, ctx, "l3s_" + name)

        raw, self_logit = sb("raw", [P, NW, HEADS]), sb("self_logit", [P, NW, HEADS])
        chain, logit_set, weight_set = (sem(n) for n in ("chain", "logit_set", "weight_set"))
        block = ctx.enter_context(nc.Block())
        acc = st.acc[:].rearrange("p (w f) -> p w f", w=NW)
        logits = st.logits[:].rearrange("p (w c) -> p w c", w=NW)
        at_dst = st.at_dst[:].rearrange("p (w c) -> p w c", w=NW)

        @block.vector
        def _(dve):
            done = [0]

            def link(ins_):
                done[0] += 1
                ins_.then_inc(chain, 1)
                dve.wait_ge(chain, done[0])

            dve.tensor_copy(at_dst[:, :, 0:HEADS], logits[:, :, HEADS:2 * HEADS])
            link(dve.tensor_tensor(raw[:], st.maxima[:].rearrange("p (w c) -> p w c", w=NW),
                                   st.shift[:].unsqueeze(1).broadcast_to([P, NW, HEADS]), ALU.subtract))
            link(dve.tensor_tensor(raw[:], raw[:], logits[:, :, HEADS:2 * HEADS], ALU.add))
            link(dve.scalar_tensor_tensor(out=at_dst[:, :, HEADS:2 * HEADS], in0=raw[:], scalar=SLOPE, in1=raw[:],
                                          op0=ALU.mult, op1=ALU.max))
            link(dve.tensor_tensor(self_logit[:], logits[:, :, 0:HEADS], logits[:, :, HEADS:2 * HEADS], ALU.add))
            link(dve.scalar_tensor_tensor(out=raw[:], in0=self_logit[:], scalar=SLOPE, in1=self_logit[:],
                                          op0=ALU.mult, op1=ALU.max))
            dve.tensor_tensor(self_logit[:], raw[:], at_dst[:, :, HEADS:2 * HEADS], ALU.subtract).then_inc(logit_set, 1)
            dve.wait_ge(weight_set, 1)
            h4 = acc[:, :, 0:D].rearrange("p w (a c) -> p w a c", a=HEADS)
            link(dve.tensor_tensor(h4, h4, acc[:, :, D:D + HEADS].unsqueeze(3).broadcast_to([P, NW, HEADS, CH]), ALU.mult))

        @block.scalar
        def _(act):
            act.wait_ge(logit_set, 1)
            act.activation(acc[:, :, D:D + HEADS], self_logit[:], ACT.Exp).then_inc(weight_set, 1)


def layer3_edges(nc, st):
    ROW = D + HEADS
    with ExitStack() as ctx:
        phase_end(nc, ctx)

        def sb(name, shape, dt=F32):
            return ctx.enter_context(nc.sbuf_tensor("l3e_" + name, shape, dt))

        def sem(name):
            return phase_semaphore(nc, ctx, "l3e_" + name)

        ring, rows, stage = sb("ring", [P, RING, ROW]), sb("rows", [P, RING, ROW]), sb("stage", [P, RING], I32)
        onehot, x_onehot, onehot_t = sb("onehot", [P, RING, P]), sb("x_onehot", [P, GROUP, P]), sb("onehot_t", [P, GROUP, P])
        of_dst = sb("of_dst", [P, 2, GROUP, 2 * HEADS])
        logit, leaky = sb("logit", [P, 2, GROUP, HEADS]), sb("leaky", [P, 2, GROUP, HEADS])
        turned = ctx.enter_context(nc.psum_tensor("l3e_turned", [P, GROUP, 512], F32))
        fetched = ctx.enter_context(nc.psum_tensor("l3e_fetched", [P, 512], F32))
        total = [ctx.enter_context(nc.psum_tensor(f"l3e_total{h}", [P, 512], F32)) for h in range(2)]
        x_total = ctx.enter_context(nc.psum_tensor("l3e_x_total", [P, 512], F32))
        arrived = [sem(f"arrived{k}") for k in range(RING)]
        (staged, hot, turned_in, turned_out, got, got_out, chain, logit_set, weight_set, rows_set, hot_used, added,
         x_hot, x_used, x_turned_out, x_got, x_got_out, x_scatter, x_scattered, x_added, turn) = (
            sem(n) for n in ("staged", "hot", "turned_in", "turned_out", "got", "got_out", "chain", "logit_set",
                             "weight_set", "rows_set", "hot_used", "added", "x_hot", "x_used",
                             "x_turned_out", "x_got", "x_got_out", "x_scatter", "x_scattered", "x_added", "turn"))
        block = ctx.enter_context(nc.Block())
        CHAIN = 2
        fetched_view = fetched[:, 0:GROUP * 2 * HEADS].rearrange("p (k c) -> p k c", k=GROUP)

        @block.gpsimd
        def _(pool):
            pool.sem_inc(rows_set, RING)
            with pool.Fori(0, HG) as it:
                for h in range(2):
                    pool.wait_ge(rows_set, RING * it + GROUP * (h + 1))
                    pool.sem_inc(turn, 1)
                    pool.tensor_copy(stage[:, GROUP * h:GROUP * (h + 1)],
                                     st.src[:, bass.ds((2 * it + h) * GROUP, GROUP)]).then_inc(staged, 1)
                    pool.wait_ge(staged, 2 * it + h + 1)
                    pool.sem_inc(turn, 1)
                    for k in range(GROUP * h, GROUP * (h + 1)):
                        pool.indirect_dma_start(ring[:, k, :], None, st.gat_rows,
                                                bass.IndirectOffsetOnAxis(ap=stage[:, k:k + 1], axis=0)
                                                ).then_inc(arrived[k], 16)

        @block.scalar
        def _(act):
            def fetch_first(it, h, ranges):
                before = ranges[h][2]
                for k in range(GROUP):
                    act.wait_ge(turned_in, RING * it + GROUP * h + k + 1)
                    act.wait_ge(got, RING * it + GROUP * h + k + 1)
                    act.wait_ge(x_got, GROUP * before + k + 1)
                    act.activation(onehot_t[:, k, :], turned[:, k, 0:P], ACT.Copy).then_inc(turned_out, 1)

            def fetch_more(it, h, ranges):
                _, more, before = ranges[h]
                with act.If(more > 0):
                    with act.Fori(0, more) as j:
                        extra = before + j
                        for k in range(GROUP):
                            act.wait_ge(x_used, GROUP * extra + k + 1 + GROUP)
                            act.wait_ge(got, RING * it + GROUP * (h + 1) + GROUP)
                            act.wait_ge(x_got, GROUP * extra + k + 1)
                            act.activation(onehot_t[:, k, :], turned[:, k, 0:P], ACT.Copy).then_inc(x_turned_out, 1)

            def trip(it, ahead):
                ranges = group_ranges(nc, act, st, it)
                later = group_ranges(nc, act, st, it + 1) if ahead else None
                for h in range(2):
                    if h == 0:
                        fetch_first(it, 1, ranges)
                    elif ahead:
                        fetch_first(it + 1, 0, later)
                    act.wait_ge(logit_set, 2 * it + h + 1)
                    act.wait_ge(added, 2 * it + h + 1)
                    act.wait_ge(x_added, ranges[0][2] + 1)
                    act.activation(rows[:, GROUP * h:GROUP * (h + 1), D:ROW], logit[:, h, :, :], ACT.Exp
                                   ).then_inc(weight_set, 1)
                    if h == 0:
                        fetch_more(it, 1, ranges)
                    elif ahead:
                        fetch_more(it + 1, 0, later)

            ranges = group_ranges(nc, act, st, 0)
            fetch_first(0, 0, ranges)
            fetch_more(0, 0, ranges)
            with act.Fori(0, HG - 1) as it:
                trip(it, True)
            trip(HG - 1, False)

        @block.vector
        def _(dve):
            dve.sem_inc(got_out, 1)
            dve.sem_inc(x_got_out, 1)
            dve.sem_inc(added, 2)
            dve.sem_inc(x_added, 1)

            def build(it, h, ranges):
                for k in range(GROUP * h, GROUP * (h + 1)):
                    dve.wait_ge(hot_used, RING * it + k + 1)
                    one_hot(dve, st, onehot[:, k, :], ranges[h][0], it * RING + k).then_inc(hot, 1)

            def fetch(it, h, ranges):
                first, more, before = ranges[h]
                dve.wait_ge(got, RING * it + GROUP * (h + 1) + GROUP)
                dve.sem_inc(turn, 1)
                dve.tensor_copy(of_dst[:, h, :, :], fetched_view).then_inc(got_out, 1)
                with dve.If(more > 0):
                    with dve.Fori(0, more) as j:
                        window = within(nc, first + 1 + j, NW - 1)
                        extra = before + j
                        for k in range(GROUP):
                            dve.wait_ge(x_used, GROUP * extra + k + 1)
                            one_hot(dve, st, x_onehot[:, k, :], window, it * RING + GROUP * h + k).then_inc(x_hot, 1)
                        dve.wait_ge(x_got, GROUP * extra + 2 * GROUP)
                        dve.wait_ge(got_out, 2 * it + h + 2)
                        dve.wait_ge(x_got_out, extra + 1)
                        dve.tensor_tensor(of_dst[:, h, :, :], of_dst[:, h, :, :], fetched_view, ALU.add
                                          ).then_inc(x_got_out, 1)

            def trip(it, ahead):
                ranges = group_ranges(nc, dve, st, it)
                later = group_ranges(nc, dve, st, it + 1) if ahead else None
                for h in range(2):
                    half = slice(GROUP * h, GROUP * (h + 1))
                    chained = (2 * it + h) * CHAIN
                    first, more, before = ranges[h]
                    if h == 0:
                        build(it, 1, ranges)
                    elif ahead:
                        build(it + 1, 0, later)
                    dve.wait_ge(got_out, 2 * it + h + 2)
                    dve.wait_ge(x_got_out, before + more + 1)
                    for k in range(GROUP * h, GROUP * (h + 1)):
                        dve.wait_ge(arrived[k], 16 * it + 16)
                    dve.tensor_tensor(logit[:, h, :, :], ring[:, half, D:ROW], of_dst[:, h, :, 0:HEADS], ALU.add
                                      ).then_inc(chain, 1)
                    dve.wait_ge(chain, chained + 1)
                    dve.scalar_tensor_tensor(out=leaky[:, h, :, :], in0=logit[:, h, :, :], scalar=SLOPE,
                                             in1=logit[:, h, :, :], op0=ALU.mult, op1=ALU.max).then_inc(chain, 1)
                    dve.wait_ge(chain, chained + 2)
                    dve.tensor_tensor(logit[:, h, :, :], leaky[:, h, :, :], of_dst[:, h, :, HEADS:2 * HEADS], ALU.subtract
                                      ).then_inc(logit_set, 1)
                    dve.wait_ge(weight_set, 2 * it + h + 1)
                    for k in range(GROUP * h, GROUP * (h + 1)):
                        dve.tensor_tensor(rows[:, k, 0:D].rearrange("p (a c) -> p a c", a=HEADS),
                                          ring[:, k, 0:D].rearrange("p (a c) -> p a c", a=HEADS),
                                          rows[:, k, D:ROW].unsqueeze(2).broadcast_to([P, HEADS, CH]), ALU.mult
                                          ).then_inc(rows_set, 1)
                    dve.wait_ge(hot_used, RING * it + GROUP * (h + 1) + 2 * GROUP)
                    dve.wait_ge(added, 2 * it + h + 2)
                    dve.wait_ge(x_added, before + 1)
                    here = st.acc[:, bass.ds(first * WIDE, ROW)]
                    dve.tensor_tensor(here, here, total[h][:, 0:ROW], ALU.add).then_inc(added, 1)
                    with dve.If(more > 0):
                        with dve.Fori(0, more) as j:
                            window = within(nc, first + 1 + j, NW - 1)
                            extra = before + j
                            for k in range(GROUP):
                                dve.wait_ge(x_scattered, GROUP * extra + k + 1)
                                dve.wait_ge(x_used, GROUP * (before + more) + k + 1)
                                one_hot(dve, st, x_onehot[:, k, :], window, it * RING + GROUP * h + k
                                        ).then_inc(x_scatter, 1)
                            dve.wait_ge(x_scattered, GROUP * extra + 2 * GROUP)
                            dve.wait_ge(added, 2 * it + h + 3)
                            dve.wait_ge(x_added, extra + 1)
                            here = st.acc[:, bass.ds(window * WIDE, ROW)]
                            dve.tensor_tensor(here, here, x_total[:, 0:ROW], ALU.add).then_inc(x_added, 1)
                    if h == 0:
                        fetch(it, 1, ranges)
                    elif ahead:
                        fetch(it + 1, 0, later)

            ranges = group_ranges(nc, dve, st, 0)
            build(0, 0, ranges)
            fetch(0, 0, ranges)
            with dve.Fori(0, HG - 1) as it:
                trip(it, True)
            trip(HG - 1, False)

        @block.tensor
        def _(pe):
            pe.sem_inc(got, GROUP)
            pe.sem_inc(x_got, GROUP)
            pe.sem_inc(hot_used, RING)
            pe.sem_inc(x_used, GROUP)
            pe.sem_inc(x_scattered, GROUP)

            def fetch_first(it, h, ranges):
                first, _, before = ranges[h]
                for k in range(GROUP):
                    pe.wait_ge(hot, RING * it + GROUP * h + k + 1)
                    pe.transpose(turned[:, k, 0:P], onehot[:, GROUP * h + k, :], st.ident[:]).then_inc(turned_in, 1)
                pe.wait_ge(got_out, 2 * it + h + 1)
                pe.wait_ge(x_got_out, before + 1)
                for k in range(GROUP):
                    pe.wait_ge(turned_out, RING * it + GROUP * h + k + 1)
                    pe.sem_inc(turn, 1)
                    pe.matmul(fetched[:, 2 * HEADS * k:2 * HEADS * (k + 1)], onehot_t[:, k, :],
                              st.at_dst[:, bass.ds(2 * HEADS * first, 2 * HEADS)], start=True, stop=True).then_inc(got, 1)

            def fetch_more(it, h, ranges):
                first, more, before = ranges[h]
                with pe.If(more > 0):
                    with pe.Fori(0, more) as j:
                        window = within(nc, first + 1 + j, NW - 1)
                        extra = before + j
                        for k in range(GROUP):
                            pe.wait_ge(x_hot, GROUP * extra + k + 1)
                            pe.transpose(turned[:, k, 0:P], x_onehot[:, k, :], st.ident[:]).then_inc(x_used, 1)
                        pe.wait_ge(got_out, 2 * it + h + 2)
                        pe.wait_ge(x_got_out, extra + 1)
                        for k in range(GROUP):
                            pe.wait_ge(x_turned_out, GROUP * extra + k + 1)
                            pe.sem_inc(turn, 1)
                            pe.matmul(fetched[:, 2 * HEADS * k:2 * HEADS * (k + 1)], onehot_t[:, k, :],
                                      st.at_dst[:, bass.ds(2 * HEADS * window, 2 * HEADS)], start=True, stop=True
                                      ).then_inc(x_got, 1)

            def trip(it, ahead):
                ranges = group_ranges(nc, pe, st, it)
                later = group_ranges(nc, pe, st, it + 1) if ahead else None
                for h in range(2):
                    if h == 0:
                        fetch_first(it, 1, ranges)
                    elif ahead:
                        fetch_first(it + 1, 0, later)
                    pe.wait_ge(added, 2 * it + h + 1)
                    for k in range(GROUP * h, GROUP * (h + 1)):
                        pe.wait_ge(rows_set, RING * it + k + 1 + RING)
                        pe.matmul(total[h][:, 0:ROW], onehot[:, k, :], rows[:, k, :],
                                  start=(k % GROUP == 0), stop=(k % GROUP == GROUP - 1)).then_inc(hot_used, 1)
                    _, more, before = ranges[h]
                    with pe.If(more > 0):
                        with pe.Fori(0, more) as j:
                            extra = before + j
                            pe.wait_ge(x_added, extra + 1)
                            for k in range(GROUP):
                                pe.wait_ge(x_scatter, GROUP * extra + k + 1)
                                pe.matmul(x_total[:, 0:ROW], x_onehot[:, k, :], rows[:, GROUP * h + k, :],
                                          start=(k == 0), stop=(k == GROUP - 1)).then_inc(x_scattered, 1)
                    if h == 0:
                        fetch_more(it, 1, ranges)
                    elif ahead:
                        fetch_more(it + 1, 0, later)

            ranges = group_ranges(nc, pe, st, 0)
            fetch_first(0, 0, ranges)
            fetch_more(0, 0, ranges)
            with pe.Fori(0, HG - 1) as it:
                trip(it, True)
            trip(HG - 1, False)


def layer3_end(nc, st, ins):
    with ExitStack() as ctx:
        phase_end(nc, ctx)
        def sb(name, shape):
            return ctx.enter_context(nc.sbuf_tensor("l3z_" + name, shape, F32))

        def sem(name):
            return phase_semaphore(nc, ctx, "l3z_" + name)

        bias, per_weight = sb("bias", [P, D]), sb("per_weight", [P, NW, HEADS])
        squares, norm, per_norm = sb("squares", [P, NW]), sb("norm", [P, NW]), sb("per_norm", [P, NW])
        loaded, chain, biased, relued, summed, rooted = (
            sem(n) for n in ("loaded", "chain", "biased", "relued", "summed", "rooted"))
        block = ctx.enter_context(nc.Block())
        acc = st.acc[:].rearrange("p (w f) -> p w f", w=NW)
        value, spare = acc[:, :, 0:D], acc[:, :, D:2 * D]

        @block.sync
        def _(sp):
            sp.dma_start(bias[:], ins["L3_bias"].partition_broadcast(P)).then_inc(loaded, 16)
            sp.wait_ge(loaded, 16)

        @block.vector
        def _(dve):
            done = [0]

            def link(ins_):
                done[0] += 1
                ins_.then_inc(chain, 1)
                dve.wait_ge(chain, done[0])

            link(dve.reciprocal(per_weight[:], acc[:, :, D:D + HEADS]))
            value4 = value.rearrange("p w (a c) -> p w a c", a=HEADS)
            link(dve.tensor_tensor(value4, value4, per_weight[:].unsqueeze(3).broadcast_to([P, NW, HEADS, CH]), ALU.mult))
            dve.wait_ge(loaded, 16)
            dve.tensor_tensor(value, value, bias[:].unsqueeze(1).broadcast_to([P, NW, D]), ALU.add).then_inc(biased, 1)
            dve.wait_ge(relued, 2)
            dve.tensor_reduce(squares[:], spare, AX.X, ALU.add).then_inc(summed, 1)
            dve.wait_ge(rooted, 1)
            link(dve.tensor_single_scalar(norm[:], norm[:], 1e-12, ALU.max))
            link(dve.reciprocal(per_norm[:], norm[:]))
            link(dve.tensor_tensor(value, value, per_norm[:].unsqueeze(2).broadcast_to([P, NW, D]), ALU.mult))
            link(dve.tensor_tensor(value, value, st.x[:].rearrange("p (w f) -> p w f", w=NW), ALU.add))

        @block.scalar
        def _(act):
            act.wait_ge(biased, 1)
            act.activation(value, value, ACT.Relu).then_inc(relued, 1)
            act.wait_ge(relued, 1)
            act.activation(spare, value, ACT.Square).then_inc(relued, 1)
            act.wait_ge(summed, 1)
            act.activation(norm[:], squares[:], ACT.Sqrt).then_inc(rooted, 1)


def layer3(nc, st, ins):
    layer3_nodes(nc, st, ins)
    layer3_maxima(nc, st)
    layer3_self_loops(nc, st)
    layer3_edges(nc, st)
    layer3_end(nc, st, ins)
    layer_norm(nc, st, "ln4_", st.acc, WIDE)


def start_layer0(nc, st):
    with ExitStack() as ctx:
        phase_end(nc, ctx)
        copied = phase_semaphore(nc, ctx, "start0_copied")
        block = ctx.enter_context(nc.Block())

        @block.vector
        def _(dve):
            acc = st.acc[:].rearrange("p (w f) -> p w f", w=NW)
            dve.memset(acc[:, :, D:D + 1], 0.0).then_inc(copied, 1)
            dve.tensor_copy(acc[:, :, 0:D], st.x[:].rearrange("p (w f) -> p w f", w=NW)).then_inc(copied, 1)


def finish(nc, st, out):
    with ExitStack() as ctx:
        phase_end(nc, ctx)
        stored = phase_semaphore(nc, ctx, "finish_stored")
        block = ctx.enter_context(nc.Block())
        full = N // P

        @block.sync
        def _(sp):
            sp.dma_start(out[0:full * P, :].rearrange("(w p) f -> p w f", p=P),
                         st.x[:, 0:full * D].rearrange("p (w f) -> p w f", f=D)).then_inc(stored, 16)
            sp.dma_start(out[full * P:N, :], st.x[0:N - full * P, full * D:(full + 1) * D]).then_inc(stored, 16)
            sp.wait_ge(stored, 32)


def build(nc, ins, out):
    with ExitStack() as ctx:
        st = State()

        def sb(name, shape, dt=F32):
            return ctx.enter_context(nc.sbuf_tensor(name, shape, dt))

        st.x = sb("x", [P, NW * D])
        st.iota = sb("iota", [P, P])
        st.ident = sb("ident", [P, P])
        st.window_start = sb("window_start", [P, NW])
        st.dst = sb("dst", [P, NT])
        st.src = sb("src", [P, NT], I32)
        st.src_type = sb("src_type", [P, NT], I32)
        st.weight = sb("weight", [P, NT])
        st.ranges = sb("ranges", [1, HG], I32)
        st.dst_row = sb("dst_row", [P, NT], I32)
        st.degree = sb("degree", [P, NW])
        st.in_edges = sb("in_edges", [P, NW])
        st.dinv = sb("dinv", [P, NW])

        def rows(name, width):
            return nc.dram_tensor(name, [NP, width], F32, kind="Internal").ap()

        st.logits = sb("logits", [P, NW * 2 * HEADS])
        st.at_dst = sb("at_dst", [P, NW * 2 * HEADS])
        st.maxima = sb("maxima", [P, NW * HEADS])
        st.shift = sb("shift", [P, HEADS])
        st.gat_rows = rows("attention_table", D + HEADS)
        st.gat_logits = rows("attention_logit_table", HEADS)
        st.table1 = rows("conv1_table", D)
        st.table2 = rows("conv2_table", D)
        st.src_rows = rows("message_src_table", HID2)
        st.dst_rows = rows("message_dst_table", HID2)
        st.ranges_dram = nc.dram_tensor("group_table", [NG, 3], I32, kind="Internal").ap()
        st.rel_rows = nc.dram_tensor("relation_table", [NP * RELS, D], F32, kind="Internal").ap()
        prepare(nc, st, ins)
        transform_by_relation(nc, st, ins)
        st.acc = sb("acc", [P, NW * WIDE])
        start_layer0(nc, st)
        aggregate(nc, st, "l0_", st.rel_rows, st.src_type, st.weight)
        layer_norm(nc, st, "ln0_", st.acc, WIDE)
        layer1(nc, st, ins)
        layer2(nc, st, ins)
        layer3(nc, st, ins)
        finish(nc, st, out)


def kernel(**inputs):
    import concourse.bacc as bacc
    from concourse.bass_utils import run_bass_kernel_spmd

    given = {name: np.asarray(a) for name, a in inputs.items()}

    def padded(a, fill):
        rows = np.full((EP,), fill, a.dtype)
        rows[:E] = a.reshape(-1)
        return rows

    def by_tile(a):
        return np.ascontiguousarray(a.reshape(NT, P).T)

    x = np.zeros((NP, D), given["x"].dtype)
    x[:N] = given["x"]
    attr = np.zeros((EP, EDIM), given["edge_attr_64"].dtype)
    attr[:E] = given["edge_attr_64"]
    dst = padded(given["dst"], PAD_NODE)
    arrays = {
        "x": x, "x_t": np.ascontiguousarray(x.T),
        "src": by_tile(padded(given["src"], 0)), "dst": by_tile(dst),
        "dst_by_group": dst.reshape(NG, GROUP * P),
        "edge_type": by_tile(padded(given["edge_type_16"], 0)),
        "edge_weight": by_tile(padded(given["edge_weight1"], 0)),
        "edge_attr_t": np.ascontiguousarray(attr.T),
    }
    for name, a in given.items():
        if name.startswith("L"):
            arrays[name.replace("_gnn", "")] = np.ascontiguousarray(a)
    nc = bacc.Bacc("TRN2", target_bir_lowering=False, num_devices=1)
    ins = {name: nc.dram_tensor("in_" + name, a.shape, mybir.dt.from_np(a.dtype), kind="ExternalInput").ap()
           for name, a in arrays.items()}
    out = nc.dram_tensor("out", [N, D], F32, kind="ExternalOutput").ap()
    build(nc, ins, out)
    result = run_bass_kernel_spmd(nc, [{"in_" + name: a for name, a in arrays.items()}], core_ids=[0])
    return result.results[0]["out"]
```

```python
from contextlib import ExitStack

import numpy as np
import concourse.bass as bass
import concourse.mybir as mybir
from concourse.alu_op_type import AluOpType as ALU

F32 = mybir.dt.float32
I32 = mybir.dt.int32
ACT = mybir.ActivationFunctionType
AX = mybir.AxisListType

P = 128
N = 3125
E = 50000
D = 256
RELS = 16
HID1 = 300
HC = 3
HR = HID1 // HC
HID2 = 512
EDIM = 64
HEADS = 4
CH = D // HEADS
NW = 26
NP = NW * P
GROUP = 4
NG = -(-E // (P * GROUP))
EP = NG * GROUP * P
NT = NG * GROUP
RING = 2 * GROUP
PART = GROUP // 2
PARTS = RING // PART
HG = NG // 2
HW = NW // 2
STRETCH = NW // 2
PAD_NODE = N + 74
WIDE = 512
EPS = 1e-5
SLOPE = 0.2
assert NG % 2 == 0 and NW % 2 == 0 and N <= PAD_NODE < NP


class State:
    pass


def phase_end(nc, ctx):
    ctx.semaphores = []
    ctx.callback(nc.all_engine_barrier)
    ctx.callback(nc.clear_and_free_semaphores, ctx.semaphores)


def phase_semaphore(nc, ctx, name):
    handle = nc.alloc_semaphore(name)
    ctx.semaphores.append(handle)
    return handle


def within(nc, value, top):
    return nc.s_assert_within(value, 0, top, skip_runtime_bounds_check_because=(
        "the group ranges are computed from node numbers below N"))


def group_ranges(nc, eng, st, trip):
    return unpack_ranges(nc, eng, eng.value_load(st.ranges[0:1, bass.ds(trip, 1)]))


def two_trips_ranges(nc, eng, st, trip):
    _, words = nc.values_load_multi_w_load_instructions(
        st.ranges[0:1, bass.ds(trip, 2)], engines=[eng.engine],
        skip_runtime_bounds_check_because="the fields are taken out of it before they are used")
    return [unpack_ranges(nc, eng, word) for word in words]


def unpack_ranges(nc, eng, word):
    def field(low, bits, most):
        value = (word >> low) & ((1 << bits) - 1)
        return eng.snap(nc.s_assert_within(value, 0, most, skip_runtime_bounds_check_because="prepare packs it so"))

    before = field(20, 12, NG * (NW - 1))
    first0, more0 = field(0, 5, NW - 1), field(5, 5, NW - 1)
    first1, more1 = field(10, 5, NW - 1), field(15, 5, NW - 1)
    return (first0, more0, before), (first1, more1, eng.snap(before + more0))


def one_hot(dve, st, out, window, tile):
    return dve.tensor_scalar(out, st.iota[:], st.window_start[:, bass.ds(window, 1)], st.dst[:, bass.ds(tile, 1)],
                             ALU.add, ALU.is_equal)


def build_extra(nc, dve, st, it, h, window, extra, x_onehot, x_hot, x_used, turn):
    window = within(nc, window, NW - 1)
    dve.wait_ge(x_used, extra + 1)
    dve.sem_inc(turn, 1)
    dve.tensor_tensor(x_onehot[:], st.node_ids[:, bass.ds(window * P, P)].unsqueeze(1).broadcast_to([P, GROUP, P]),
                      st.dst[:, bass.ds((2 * it + h) * GROUP, GROUP)].unsqueeze(2).broadcast_to([P, GROUP, P]),
                      ALU.is_equal).then_inc(x_hot, 1)


def add_extra(nc, dve, st, window, extra, x_total, width, x_used, x_added):
    window = within(nc, window, NW - 1)
    dve.wait_ge(x_used, extra + 2)
    dve.wait_ge(x_added, extra + 1)
    here = st.acc[:, bass.ds(window * WIDE, width)]
    dve.tensor_tensor(here, here, x_total[:, 0:width], ALU.add).then_inc(x_added, 1)


def add_extras(nc, dve, st, ranges, it, h, x_onehot, x_total, width, added, x_hot, x_used, x_added, turn):
    first, more, before = ranges[h]
    with dve.If(more > 0):
        dve.wait_ge(added, 2 * it + h + 3)
        dve.sem_inc(turn, 1)
        with dve.If(more > 1):
            with dve.Fori(1, more) as j:
                add_extra(nc, dve, st, first + j, before + j - 1, x_total, width, x_used, x_added)
                build_extra(nc, dve, st, it, h, first + 1 + j, before + j, x_onehot, x_hot, x_used, turn)
        add_extra(nc, dve, st, first + more, before + more - 1, x_total, width, x_used, x_added)


def prepare(nc, st, ins):
    with ExitStack() as ctx:
        phase_end(nc, ctx)
        def sb(name, shape, dt):
            return ctx.enter_context(nc.sbuf_tensor("pre_" + name, shape, dt))

        def sem(name):
            return phase_semaphore(nc, ctx, "pre_" + name)

        src_i = sb("src_i", [P, NT], I32)
        type_i = sb("type_i", [P, NT], I32)
        dst_g = sb("dst_g", [NG, GROUP * P], I32)
        dst_f = sb("dst_f", [NG, GROUP * P], F32)
        low_high = sb("low_high", [NG, 2], I32)
        windows = sb("windows", [NG, 2], I32)
        windows_f = sb("windows_f", [NG, 2], F32)
        table = sb("table", [NG, 3], F32)
        table_i = sb("table_i", [NG, 3], I32)
        row = sb("row", [1, 3 * NG], I32)
        earlier = sb("earlier", [NG, NG], F32)
        ones = sb("ones", [P, P], F32)
        src_f = sb("src_f", [P, NT], F32)
        steps_psum = ctx.enter_context(nc.psum_tensor("pre_steps", [P, 512], F32))
        loaded, summed, filled, iotas, chain, counted, stepped, spilled, fetched, dst_set = (
            sem(n) for n in ("loaded", "summed", "filled", "iotas", "chain", "counted", "stepped", "spilled", "fetched", "dst_set"))
        block = ctx.enter_context(nc.Block())

        @block.scalar
        def _(act):
            for b in range(RELS // 2):
                act.dma_start(st.rel_weights[:, b, :, :, :],
                              ins["L0_weight"].rearrange("r (c k) o -> k r c o", c=D // P)[:, 2 * b:2 * b + 2, :, :]
                              ).then_inc(st.rel_loaded[b], 16)

        @block.sync
        def _(sp):
            sp.dma_start(st.dst_row[:], ins["dst"]).then_inc(loaded, 16)
            sp.dma_start(src_i[:], ins["src"]).then_inc(loaded, 16)
            sp.dma_start(type_i[:], ins["edge_type"]).then_inc(loaded, 16)
            sp.dma_start(dst_g[:], ins["dst_by_group"]).then_inc(loaded, 16)
            sp.dma_start(st.weight[:], ins["edge_weight"]).then_inc(loaded, 16)
            sp.wait_ge(loaded, 5 * 16)
            sp.wait_ge(dst_set, 1)
            sp.dma_start(st.dst_rows_f, dst_f[:]).then_inc(spilled, 16)
            sp.wait_ge(stepped, 1)
            sp.dma_start(st.ranges_dram, table_i[:]).then_inc(spilled, 16)
            sp.wait_ge(spilled, 32)
            sp.dma_start(row[:], st.ranges_dram.rearrange("(a g) c -> a (g c)", a=1)).then_inc(fetched, 16)
            sp.wait_ge(fetched, 16)

        @block.gpsimd
        def _(pool):
            pool.memset(ones[:], 1.0).then_inc(filled, 1)
            pool.iota(st.iota[:], pattern=[[1, P]], base=0, channel_multiplier=0,
                      allow_small_or_imprecise_dtypes=True).then_inc(iotas, 1)
            pool.iota(st.node_ids[:], pattern=[[1, NW * P]], base=0, channel_multiplier=0,
                      allow_small_or_imprecise_dtypes=True).then_inc(iotas, 1)
            pool.iota(st.node[:], pattern=[[0, 1]], base=0, channel_multiplier=1,
                      allow_small_or_imprecise_dtypes=True).then_inc(iotas, 1)
            pool.iota(st.window_start[:], pattern=[[P, NW]], base=0, channel_multiplier=0,
                      allow_small_or_imprecise_dtypes=True).then_inc(iotas, 1)
            pool.wait_ge(filled, 1)
            pool.affine_select(out=st.ident[:], in_=ones[:], compare_op=ALU.is_equal, fill=0.0, base=0,
                               pattern=[[-1, P]], channel_multiplier=1).then_inc(iotas, 1)
            pool.affine_select(out=earlier[:], in_=ones[0:NG, 0:NG], compare_op=ALU.is_gt, fill=0.0, base=0,
                               pattern=[[1, NG]], channel_multiplier=-1).then_inc(filled, 1)

        @block.vector
        def _(dve):
            done = [0]

            def link(ins_):
                done[0] += 1
                ins_.then_inc(chain, 1)
                dve.wait_ge(chain, done[0])

            dve.wait_ge(loaded, 5 * 16)
            dve.tensor_copy(st.dst[:], st.dst_row[:])
            dve.tensor_copy(dst_f[:], dst_g[:]).then_inc(dst_set, 1)
            dve.tensor_copy(st.src[:], src_i[:])
            link(dve.tensor_copy(src_f[:], src_i[:]))
            dve.scalar_tensor_tensor(out=st.src_type[:], in0=src_f[:], scalar=float(RELS), in1=type_i[:],
                                     op0=ALU.mult, op1=ALU.add)
            dve.tensor_reduce(low_high[:, 0:1], dst_g[:], AX.X, ALU.min)
            link(dve.tensor_reduce(low_high[:, 1:2], dst_g[:], AX.X, ALU.max))
            link(dve.tensor_single_scalar(windows[:], low_high[:], 7, ALU.arith_shift_right))
            link(dve.tensor_copy(windows_f[:], windows[:]))
            dve.tensor_copy(table[:, 0:1], windows_f[:, 0:1])
            dve.tensor_tensor(table[:, 1:2], windows_f[:, 1:2], windows_f[:, 0:1], ALU.subtract).then_inc(counted, 1)
            dve.wait_ge(summed, 1)
            link(dve.tensor_copy(table[:, 2:3], steps_psum[0:NG, 0:1]))
            dve.tensor_copy(table_i[:], table[:]).then_inc(stepped, 1)
            dve.wait_ge(fetched, 16)
            pair = row[:].rearrange("a (t f) -> a t f", f=6)
            places = ((0, 0), (1, 5), (3, 10), (4, 15), (2, 20))
            for column, low in places[1:]:
                link(dve.tensor_single_scalar(pair[:, :, column], pair[:, :, column], low, ALU.logical_shift_left))
            link(dve.tensor_copy(st.ranges[:], pair[:, :, 0]))
            for column, _ in places[1:]:
                link(dve.tensor_tensor(st.ranges[:], st.ranges[:], pair[:, :, column], ALU.bitwise_or))

        @block.tensor
        def _(pe):
            pe.wait_ge(filled, 2)
            pe.wait_ge(counted, 1)
            pe.matmul(steps_psum[0:NG, 0:1], earlier[:], table[:, 1:2], start=True, stop=True).then_inc(summed, 1)


def transform_by_relation(nc, st, ins):
    KC = D // P
    PAIRS = RELS // 2
    with ExitStack() as ctx:
        phase_end(nc, ctx)
        def sb(name, shape, dt):
            return ctx.enter_context(nc.sbuf_tensor("rel_" + name, shape, dt))

        def sem(name):
            return phase_semaphore(nc, ctx, "rel_" + name)

        x_t = sb("x_t", [P, 2, KC, P], F32)
        rows = sb("rows", [P, 2, RELS * D], F32)
        banks = [ctx.enter_context(nc.psum_tensor(f"rel_pair{b}", [P, 2 * D], F32)) for b in range(PAIRS)]
        paired, out_act, out_dve = (sem(n) for n in ("paired", "out_act", "out_dve"))
        x_in = [sem("x_in0"), sem("x_in1")]
        stored = [sem("stored0"), sem("stored1")]
        x_sb_in = sem("x_sb_in")
        turn = sem("turn")
        block = ctx.enter_context(nc.Block())

        @block.sync
        def _(sp):
            with sp.Fori(0, HW) as it:
                for h in range(2):
                    sp.wait_ge(paired, PAIRS * (2 * it + h) + PAIRS)
                    sp.dma_start(x_t[:, h, :, :],
                                 ins["x_t"].rearrange("(c k) n -> k c n", c=KC)[:, :, bass.ds((2 * it + h) * P, P)]
                                 ).then_inc(x_in[h], 16)
            sp.dma_start(st.x[:].rearrange("p (w f) -> p w f", w=NW),
                         ins["x"].rearrange("(w p) f -> p w f", p=P)).then_inc(x_sb_in, 16)
            sp.wait_ge(x_sb_in, 16)

        @block.tensor
        def _(pe):
            pe.sem_inc(paired, 2 * PAIRS)
            with pe.Fori(0, HW) as it:
                for h in range(2):
                    pe.wait_ge(x_in[h], 16 * it + 16)
                    for b in range(PAIRS):
                        pe.wait_ge(st.rel_loaded[b], 16)
                        pe.wait_ge([out_act, out_dve][b % 2], (2 * it + h) * (PAIRS // 2) + b // 2 + 1)
                        for k in range(KC):
                            last = pe.matmul(banks[b][:], x_t[:, h, k, :], st.rel_weights[:, b, :, k, :],
                                             start=(k == 0), stop=(k == KC - 1))
                        last.then_inc(paired, 1)

        @block.scalar
        def _(act):
            act.sem_inc(out_act, PAIRS // 2)
            act.sem_inc(stored[0], 16)
            act.sem_inc(stored[1], 16)
            with act.Fori(0, HW) as it:
                for h in range(2):
                    act.wait_ge(stored[h], 16 * it + 16)
                    for b in range(0, PAIRS, 2):
                        act.wait_ge(paired, PAIRS * (2 * it + h + 2) + b + 1)
                        act.activation(rows[:, h, 2 * D * b:2 * D * (b + 1)], banks[b][:], ACT.Copy).then_inc(out_act, 1)
                    act.wait_ge(out_act, (2 * it + h + 2) * (PAIRS // 2))
                    act.wait_ge(out_dve, (2 * it + h + 2) * (PAIRS // 2))
                    act.sem_inc(turn, 1)
                    act.dma_start(st.rel_rows.rearrange("(n r) f -> n (r f)", r=RELS)[bass.ds((2 * it + h) * P, P), :],
                                  rows[:, h, :]).then_inc(stored[h], 16)
            for h in range(2):
                act.wait_ge(stored[h], 16 * (HW + 1))

        @block.vector
        def _(dve):
            dve.sem_inc(out_dve, PAIRS // 2)
            with dve.Fori(0, HW) as it:
                for h in range(2):
                    dve.wait_ge(stored[h], 16 * it + 16)
                    for b in range(1, PAIRS, 2):
                        dve.wait_ge(paired, PAIRS * (2 * it + h + 2) + b + 1)
                        dve.tensor_copy(rows[:, h, 2 * D * b:2 * D * (b + 1)], banks[b][:]).then_inc(out_dve, 1)


def aggregate(nc, st, name, table, index, weight, start_loads=None):
    width = D if weight is None else D + 1
    with ExitStack() as ctx:
        phase_end(nc, ctx)

        def sem(part):
            return phase_semaphore(nc, ctx, name + part)

        ring = ctx.enter_context(nc.sbuf_tensor(name + "ring", [P, RING, D], F32))
        stage = ctx.enter_context(nc.sbuf_tensor(name + "stage", [P, RING], I32))
        onehot = ctx.enter_context(nc.sbuf_tensor(name + "onehot", [P, RING, P], F32))
        x_onehot = ctx.enter_context(nc.sbuf_tensor(name + "x_onehot", [P, GROUP, P], F32))
        rows = ctx.enter_context(nc.sbuf_tensor(name + "rows", [P, RING, D + 4], F32))
        total = [ctx.enter_context(nc.psum_tensor(name + f"total{h}", [P, 512], F32)) for h in range(2)]
        x_total = ctx.enter_context(nc.psum_tensor(name + "x_total", [P, 512], F32))
        arrived = [sem(f"arrived{k}") for k in range(RING)]
        staged, hot, hot_used, added, x_hot, x_used, x_added, group_done, scaled, turn, ones_set = (
            sem(n) for n in ("staged", "hot", "hot_used", "added", "x_hot", "x_used", "x_added", "group_done", "scaled",
                             "turn", "ones_set"))
        block = ctx.enter_context(nc.Block())

        if start_loads is not None:
            @block.sync
            def _(sp):
                start_loads(sp)

        @block.gpsimd
        def _(pool):
            if weight is not None:
                pool.memset(rows[:, :, D:D + 1], 1.0).then_inc(ones_set, 1)
            pool.sem_inc(scaled, RING)
            with pool.Fori(0, HG) as it:
                for q in range(PARTS):
                    pool.wait_ge(scaled, RING * it + PART * (q + 1))
                    pool.wait_ge(staged, PARTS * it + q + 1)
                    pool.sem_inc(turn, 1)
                    for k in range(PART * q, PART * (q + 1)):
                        pool.indirect_dma_start(ring[:, k, :], None, table,
                                                bass.IndirectOffsetOnAxis(ap=stage[:, k:k + 1], axis=0)
                                                ).then_inc(arrived[k], 16)

        @block.scalar
        def _(act):
            def set_out(it, q):
                act.activation(stage[:, PART * q:PART * (q + 1)], index[:, bass.ds(RING * it + PART * q, PART)],
                               ACT.Copy).then_inc(staged, 1)

            def trip(it, ahead):
                for h in range(2):
                    act.wait_ge(group_done, 2 * it + h + 1)
                    for k in range(GROUP * h, GROUP * (h + 1)):
                        act.wait_ge(arrived[k], 16 * it + 16)
                        act.sem_inc(turn, 1)
                        factor = 1.0 if weight is None else weight[:, bass.ds(it * RING + k, 1)]
                        act.activation(rows[:, k, 0:D], ring[:, k, :], ACT.Copy, scale=factor).then_inc(scaled, 1)
                        if ahead and k % PART == PART - 1:
                            set_out(it + 1, k // PART)

            for q in range(PARTS):
                set_out(0, q)
            with act.Fori(0, HG - 1) as it:
                trip(it, True)
            trip(HG - 1, False)

        @block.vector
        def _(dve):
            dve.sem_inc(added, 2)
            dve.sem_inc(x_added, 1)

            def build(it, h, window):
                for k in range(GROUP * h, GROUP * (h + 1)):
                    dve.wait_ge(hot_used, RING * it + k + 1)
                    one_hot(dve, st, onehot[:, k, :], window, it * RING + k).then_inc(hot, 1)

            def trip(it, ahead):
                ranges, later = two_trips_ranges(nc, dve, st, it) if ahead else (group_ranges(nc, dve, st, it), None)
                for h in range(2):
                    first, more, before = ranges[h]
                    with dve.If(more > 0):
                        build_extra(nc, dve, st, it, h, first + 1, before, x_onehot, x_hot, x_used, turn)
                    if ahead:
                        build(it + 1, h, later[h][0])
                    dve.wait_ge(hot_used, RING * it + GROUP * (h + 1) + 2 * GROUP)
                    dve.wait_ge(added, 2 * it + h + 2)
                    dve.wait_ge(x_added, before + 1)
                    here = st.acc[:, bass.ds(first * WIDE, width)]
                    dve.tensor_tensor(here, here, total[h][:, 0:width], ALU.add).then_inc(added, 1)
                    add_extras(nc, dve, st, ranges, it, h, x_onehot, x_total, width, added, x_hot, x_used, x_added, turn)

            ranges = group_ranges(nc, dve, st, 0)
            for h in range(2):
                build(0, h, ranges[h][0])
            with dve.Fori(0, HG - 1) as it:
                trip(it, True)
            trip(HG - 1, False)

        @block.tensor
        def _(pe):
            pe.sem_inc(hot_used, RING)
            pe.sem_inc(x_used, 1)
            pe.sem_inc(group_done, 2)
            if weight is not None:
                pe.wait_ge(ones_set, 1)
            with pe.Fori(0, HG) as it:
                ranges = group_ranges(nc, pe, st, it)
                for h in range(2):
                    pe.wait_ge(added, 2 * it + h + 1)
                    for k in range(GROUP * h, GROUP * (h + 1)):
                        pe.wait_ge(scaled, RING * it + k + 1 + RING)
                        pe.wait_ge(hot, RING * it + k + 1)
                        pe.matmul(total[h][:, 0:width], onehot[:, k, :], rows[:, k, 0:width],
                                  start=(k % GROUP == 0), stop=(k % GROUP == GROUP - 1)).then_inc(hot_used, 1)
                    _, more, before = ranges[h]
                    with pe.If(more > 0):
                        with pe.Fori(0, more) as j:
                            extra = before + j
                            pe.wait_ge(x_added, extra + 1)
                            pe.wait_ge(x_hot, extra + 1)
                            for k in range(GROUP):
                                last = pe.matmul(x_total[:, 0:width], x_onehot[:, k, :], rows[:, GROUP * h + k, 0:width],
                                                 start=(k == 0), stop=(k == GROUP - 1))
                            last.then_inc(x_used, 1)
                    pe.drain().then_inc(group_done, 1)


def layer_norm(nc, st, name, source, stride, column=0, out=None, out_column=0, gamma_beta=None):
    out, out_stride = (st.x, D) if out is None else (out, WIDE)
    with ExitStack() as ctx:
        phase_end(nc, ctx)
        def sb(part, shape):
            return ctx.enter_context(nc.sbuf_tensor(name + part, shape, F32))

        def sem(part):
            return phase_semaphore(nc, ctx, name + part)

        stats, total, diff, square, std = sb("stats", [P, NW, 6]), sb("total", [P, NW]), sb("diff", [P, NW]), \
            sb("square", [P, NW]), sb("std", [P, NW])
        mean, var, rstd = sb("mean", [P, NW]), sb("var", [P, NW]), sb("rstd", [P, NW])
        counted, chain, var_set, rooted, normed = (sem(n) for n in ("counted", "chain", "var_set", "rooted", "normed"))
        loaded, shifted, centred = sem("loaded"), sem("shifted"), sem("centred")
        if gamma_beta is not None:
            gamma, beta = sb("gamma", [P, D]), sb("beta", [P, D])
        block = ctx.enter_context(nc.Block())

        if gamma_beta is not None:
            @block.sync
            def _(sp):
                sp.dma_start(gamma[:], gamma_beta[0].partition_broadcast(P)).then_inc(loaded, 16)
                sp.dma_start(beta[:], gamma_beta[1].partition_broadcast(P)).then_inc(loaded, 16)
                sp.wait_ge(loaded, 32)

            @block.gpsimd
            def _(pool):
                pool.wait_ge(loaded, 32)
                view = out[:].rearrange("p (w f) -> p w f", w=NW)[:, :, out_column:out_column + D]
                pool.tensor_tensor(view, st.x[:].rearrange("p (w f) -> p w f", w=NW),
                                   beta[:].unsqueeze(1).broadcast_to([P, NW, D]), ALU.add).then_inc(shifted, 1)

        @block.vector
        def _(dve):
            done = [0]

            def link(ins_):
                done[0] += 1
                ins_.then_inc(chain, 1)
                dve.wait_ge(chain, done[0])

            flat_stats = stats[:].rearrange("p w s -> p (w s)")
            with dve.Fori(0, NW // STRETCH) as t:
                for u in range(STRETCH):
                    w = STRETCH * t + u
                    dve.bn_stats(flat_stats[:, bass.ds(6 * w, 6)], source[:, bass.ds(stride * w + column, D)]
                                 ).then_inc(counted, 1)
            dve.wait_ge(counted, NW)
            dve.tensor_tensor(total[:], stats[:, :, 1], stats[:, :, 4], ALU.add)
            dve.tensor_tensor(square[:], stats[:, :, 2], stats[:, :, 5], ALU.add)
            link(dve.tensor_tensor(diff[:], stats[:, :, 1], stats[:, :, 4], ALU.subtract))
            dve.tensor_single_scalar(mean[:], total[:], 0.5, ALU.mult)
            link(dve.scalar_tensor_tensor(out=diff[:], in0=diff[:], scalar=0.25, in1=diff[:], op0=ALU.mult, op1=ALU.mult))
            link(dve.scalar_tensor_tensor(out=var[:], in0=square[:], scalar=1.0 / D, in1=diff[:], op0=ALU.mult, op1=ALU.add))
            dve.tensor_single_scalar(var[:], var[:], EPS, ALU.add).then_inc(var_set, 1)
            dve.wait_ge(rooted, 1)
            link(dve.reciprocal(rstd[:], std[:]))
            if gamma_beta is not None:
                dve.wait_ge(shifted, 1)
            with dve.Fori(0, NW // STRETCH) as t:
                for u in range(STRETCH):
                    w = STRETCH * t + u
                    to = out[:, bass.ds(out_stride * w + out_column, D)]
                    here = source[:, bass.ds(stride * w + column, D)]
                    if gamma_beta is None:
                        dve.tensor_scalar(to, here, mean[:, bass.ds(w, 1)], rstd[:, bass.ds(w, 1)], ALU.subtract, ALU.mult
                                          ).then_inc(normed, 1)
                    else:
                        dve.scalar_tensor_tensor(out=here, in0=here, scalar=mean[:, bass.ds(w, 1)], in1=gamma[:],
                                                 op0=ALU.subtract, op1=ALU.mult).then_inc(centred, 1)
            if gamma_beta is not None:
                dve.wait_ge(centred, NW)
                with dve.Fori(0, NW // STRETCH) as t:
                    for u in range(STRETCH):
                        w = STRETCH * t + u
                        to = out[:, bass.ds(out_stride * w + out_column, D)]
                        dve.scalar_tensor_tensor(out=to, in0=source[:, bass.ds(stride * w + column, D)],
                                                 scalar=rstd[:, bass.ds(w, 1)], in1=to, op0=ALU.mult, op1=ALU.add
                                                 ).then_inc(normed, 1)
            dve.wait_ge(normed, NW)

        @block.scalar
        def _(act):
            act.wait_ge(var_set, 1)
            act.activation(std[:], var[:], ACT.Sqrt).then_inc(rooted, 1)


def scale_to_table(nc, st, name, table):
    with ExitStack() as ctx:
        phase_end(nc, ctx)
        def sem(part):
            return phase_semaphore(nc, ctx, name + part)

        scaled, stored, chain, rooted = (sem(n) for n in ("scaled", "stored", "chain", "rooted"))
        std = ctx.enter_context(nc.sbuf_tensor(name + "std", [P, NW], F32))
        block = ctx.enter_context(nc.Block())

        @block.vector
        def _(dve):
            acc = st.acc[:].rearrange("p (w f) -> p w f", w=NW)
            dve.tensor_copy(st.in_edges[:], acc[:, :, D]).then_inc(chain, 1)
            dve.tensor_single_scalar(st.degree[:], acc[:, :, D], 1.0, ALU.add).then_inc(chain, 1)
            dve.wait_ge(rooted, 1)
            dve.reciprocal(st.dinv[:], std[:]).then_inc(chain, 1)
            dve.wait_ge(chain, 3)
            with dve.Fori(0, NW // STRETCH) as t:
                for u in range(STRETCH):
                    w = STRETCH * t + u
                    dve.tensor_scalar(st.acc[:, bass.ds(WIDE * w, D)], st.x[:, bass.ds(D * w, D)],
                                      st.dinv[:, bass.ds(w, 1)], None, ALU.mult).then_inc(scaled, 1)

        @block.scalar
        def _(act):
            act.wait_ge(chain, 2)
            act.activation(std[:], st.degree[:], ACT.Sqrt).then_inc(rooted, 1)

        @block.sync
        def _(sp):
            sp.wait_ge(scaled, NW)
            sp.dma_start(table.rearrange("(w p) f -> p w f", p=P),
                         st.acc[:].rearrange("p (w f) -> p w f", w=NW)[:, :, 0:D]).then_inc(stored, 16)
            sp.wait_ge(stored, 16)


def layer1_weights(nc, ctx, ins):
    def sb(name, shape):
        return ctx.enter_context(nc.sbuf_tensor("l1_" + name, shape, F32))

    w1, w2, b1 = sb("w1", [P, D // P, HID1]), sb("w2", [HR, HC, D]), sb("b1", [HR, HC])
    loaded = phase_semaphore(nc, ctx, "l1_loaded")

    def start_loads(sp):
        sp.dma_start(w1[:], ins["L1_w1"].rearrange("(c k) h -> k c h", k=P)).then_inc(loaded, 16)
        sp.dma_start(w2[:], ins["L1_w2"].rearrange("(c k) f -> k c f", c=HC)).then_inc(loaded, 16)
        sp.dma_start(b1[:], ins["L1_b1"].rearrange("(c k) -> k c", c=HC), allow_slow_non_contiguous=True).then_inc(loaded, 16)

    return (w1, w2, b1, loaded), start_loads


def layer1_nodes(nc, st, weights):
    KC = D // P
    with ExitStack() as ctx:
        phase_end(nc, ctx)
        def sb(name, shape):
            return ctx.enter_context(nc.sbuf_tensor("l1_" + name, shape, F32))

        def psum(name):
            return [ctx.enter_context(nc.psum_tensor(f"l1_{name}{h}", [P, 512], F32)) for h in range(2)]

        def sem(name):
            return phase_semaphore(nc, ctx, "l1_" + name)

        y, y_t, z_t = sb("y", [P, 2, D]), sb("y_t", [P, 2, KC, P]), sb("z_t", [HR, 2, HC, P])
        turned, hidden, back = psum("turned"), psum("hidden"), psum("back")
        w1, w2, b1, loaded = weights
        y_set, y_turned, y_t_set, z_sum, z_set, back_sum, acc_set, stored = (
            sem(n) for n in ("y_set", "y_turned", "y_t_set", "z_sum", "z_set", "back_sum", "acc_set", "stored"))
        turn = sem("turn")
        block = ctx.enter_context(nc.Block())

        @block.sync
        def _(sp):
            sp.wait_ge(acc_set, NW + 2)
            sp.dma_start(st.table2.rearrange("(w p) f -> p w f", p=P),
                         st.acc[:].rearrange("p (w f) -> p w f", w=NW)[:, :, 0:D]).then_inc(stored, 16)
            sp.wait_ge(stored, 16)

        @block.vector
        def _(dve):
            dve.sem_inc(acc_set, 2)
            with dve.Fori(0, HW) as it:
                for h in range(2):
                    dve.wait_ge(back_sum, 2 * it + h + 3)
                    dve.tensor_scalar(st.acc[:, bass.ds((2 * it + h) * WIDE, D)], back[h][:, 0:D],
                                      st.dinv[:, bass.ds(2 * it + h, 1)], None, ALU.mult).then_inc(acc_set, 1)

        @block.tensor
        def _(pe):
            pe.sem_inc(y_turned, 2)
            pe.sem_inc(back_sum, 2)
            pe.wait_ge(loaded, 48)
            with pe.Fori(0, HW) as it:
                for h in range(2):
                    pe.wait_ge(y_set, 2 * it + h + 1)
                    for k in range(KC):
                        last = pe.transpose(turned[h][:, k * P:(k + 1) * P], y[:, h, k * P:(k + 1) * P], st.ident[:])
                    last.then_inc(y_turned, 1)
                for h in range(2):
                    pe.wait_ge(y_t_set, 2 * it + h + 1)
                    for c in range(HC):
                        for k in range(KC):
                            last = pe.matmul(hidden[h][0:HR, c * P:(c + 1) * P], w1[:, k, c * HR:(c + 1) * HR],
                                             y_t[:, h, k, :], start=(k == 0), stop=(k == KC - 1))
                    last.then_inc(z_sum, 1)
                for h in range(2):
                    pe.wait_ge(z_set, 2 * it + h + 1)
                    pe.wait_ge(acc_set, 2 * it + h + 1)
                    for c in range(HC):
                        last = pe.matmul(back[h][:, 0:D], z_t[:, h, c, :], w2[:, c, :], start=(c == 0), stop=(c == HC - 1))
                    last.then_inc(back_sum, 1)

        @block.scalar
        def _(act):
            with act.Fori(0, HW) as it:
                for h in range(2):
                    act.wait_ge(y_turned, 2 * it + h + 1)
                    act.sem_inc(turn, 1)
                    act.activation(y[:, h, :], st.acc[:, bass.ds((2 * it + h) * WIDE, D)], ACT.Copy,
                                   scale=st.dinv[:, bass.ds(2 * it + h, 1)]).then_inc(y_set, 1)
                for h in range(2):
                    act.wait_ge(y_turned, 2 * it + h + 3)
                    act.activation(y_t[:, h, :, :], turned[h][:, 0:D].rearrange("p (k n) -> p k n", k=KC), ACT.Copy
                                   ).then_inc(y_t_set, 1)
                for h in range(2):
                    act.wait_ge(z_sum, 2 * it + h + 1)
                    act.wait_ge(back_sum, 2 * it + h + 1)
                    for c in range(HC):
                        last = act.activation(z_t[:, h, c, :], hidden[h][0:HR, c * P:(c + 1) * P], ACT.Relu,
                                              bias=b1[:, c:c + 1])
                    last.then_inc(z_set, 1)


def layer1_end(nc, st, ins):
    with ExitStack() as ctx:
        phase_end(nc, ctx)
        b2 = ctx.enter_context(nc.sbuf_tensor("l1_b2", [P, D], F32))
        loaded, added = (phase_semaphore(nc, ctx, "l1_end_" + n) for n in ("loaded", "added"))
        block = ctx.enter_context(nc.Block())

        @block.sync
        def _(sp):
            sp.dma_start(b2[:], ins["L1_b2"].partition_broadcast(P)).then_inc(loaded, 16)
            sp.wait_ge(loaded, 16)

        @block.vector
        def _(dve):
            acc = st.acc[:].rearrange("p (w f) -> p w f", w=NW)[:, :, 0:D]
            with dve.Fori(0, NW // STRETCH) as t:
                for u in range(STRETCH):
                    w = STRETCH * t + u
                    here = st.acc[:, bass.ds(WIDE * w, D)]
                    dve.scalar_tensor_tensor(out=here, in0=here, scalar=st.dinv[:, bass.ds(w, 1)],
                                             in1=st.x[:, bass.ds(D * w, D)], op0=ALU.mult, op1=ALU.add).then_inc(added, 1)
            dve.wait_ge(added, NW)
            dve.wait_ge(loaded, 16)
            dve.tensor_tensor(acc, acc, b2[:].unsqueeze(1).broadcast_to([P, NW, D]), ALU.add).then_inc(added, 1)


def layer1(nc, st, ins):
    scale_to_table(nc, st, "l1_scale_", st.table1)
    with ExitStack() as ctx:
        phase_end(nc, ctx)
        weights, start_loads = layer1_weights(nc, ctx, ins)
        aggregate(nc, st, "l1a_", st.table1, st.src, None, start_loads)
        layer1_nodes(nc, st, weights)
    aggregate(nc, st, "l1b_", st.table2, st.src, None)
    layer1_end(nc, st, ins)
    layer_norm(nc, st, "ln1_", st.acc, WIDE)


def layer2_tables(nc, st, ins):
    KC = D // P
    with ExitStack() as ctx:
        phase_end(nc, ctx)
        def sb(name, shape):
            return ctx.enter_context(nc.sbuf_tensor("l2t_" + name, shape, F32))

        def psum(name):
            return [ctx.enter_context(nc.psum_tensor(f"l2t_{name}{h}", [P, 512], F32)) for h in range(2)]

        def sem(name):
            return phase_semaphore(nc, ctx, "l2t_" + name)

        w_nodes, b1 = sb("w_nodes", [P, 2 * KC, HID2]), sb("b1", [P, HID2])
        x, x_t, rows = sb("x", [P, 2, D]), sb("x_t", [P, 2, KC, P]), sb("rows", [P, 2, 2 * HID2])
        turned, of_src, of_dst = psum("turned"), psum("of_src"), psum("of_dst")
        loaded, x_set, x_turned, x_t_set, src_sum, dst_sum, src_out, dst_out, cleared = (
            sem(n) for n in ("loaded", "x_set", "x_turned", "x_t_set", "src_sum", "dst_sum", "src_out", "dst_out", "cleared"))
        stored = [sem("stored0"), sem("stored1")]
        turn = sem("turn")
        block = ctx.enter_context(nc.Block())

        @block.sync
        def _(sp):
            sp.dma_start(w_nodes[:], ins["L2_eW1"][0:2 * D, :].rearrange("(c k) h -> k c h", k=P)).then_inc(loaded, 16)
            sp.dma_start(b1[:], ins["L2_eb1"].partition_broadcast(P)).then_inc(loaded, 16)
            sp.sem_inc(stored[0], 16)
            sp.sem_inc(stored[1], 16)
            sp.wait_ge(loaded, 32)
            with sp.Fori(0, HW) as it:
                for h in range(2):
                    sp.wait_ge(src_out, 2 * it + h + 3)
                    sp.wait_ge(dst_out, 2 * it + h + 3)
                    here = bass.ds((2 * it + h) * P, P)
                    sp.dma_start(st.src_rows[here, :], rows[:, h, 0:HID2]).then_inc(stored[h], 16)
                    sp.dma_start(st.dst_rows[here, :], rows[:, h, HID2:2 * HID2]).then_inc(stored[h], 16)
            for h in range(2):
                sp.wait_ge(stored[h], 32 * HW + 16)

        @block.gpsimd
        def _(pool):
            pool.memset(st.acc[:], 0.0).then_inc(cleared, 1)

        @block.scalar
        def _(act):
            act.sem_inc(src_out, 2)
            with act.Fori(0, HW) as it:
                for h in range(2):
                    act.wait_ge(x_turned, 2 * it + h + 1)
                    act.sem_inc(turn, 1)
                    act.activation(x[:, h, :], st.x[:, bass.ds((2 * it + h) * D, D)], ACT.Copy).then_inc(x_set, 1)
                for h in range(2):
                    act.wait_ge(x_turned, 2 * it + h + 3)
                    act.wait_ge(dst_sum, 2 * it + h + 1)
                    act.activation(x_t[:, h, :, :], turned[h][:, 0:D].rearrange("p (k n) -> p k n", k=KC), ACT.Copy
                                   ).then_inc(x_t_set, 1)
                for h in range(2):
                    act.wait_ge(src_sum, 2 * it + h + 1)
                    act.wait_ge(stored[h], 32 * it + 16)
                    act.activation(rows[:, h, 0:HID2], of_src[h][:], ACT.Copy).then_inc(src_out, 1)

        @block.vector
        def _(dve):
            dve.sem_inc(dst_out, 2)
            dve.wait_ge(loaded, 32)
            with dve.Fori(0, HW) as it:
                for h in range(2):
                    dve.wait_ge(dst_sum, 2 * it + h + 3)
                    dve.wait_ge(stored[h], 32 * it + 16)
                    dve.tensor_tensor(rows[:, h, HID2:2 * HID2], of_dst[h][:], b1[:], ALU.add).then_inc(dst_out, 1)

        @block.tensor
        def _(pe):
            pe.sem_inc(x_turned, 2)
            pe.sem_inc(dst_sum, 2)
            pe.wait_ge(loaded, 32)
            with pe.Fori(0, HW) as it:
                for h in range(2):
                    pe.wait_ge(x_set, 2 * it + h + 1)
                    for k in range(KC):
                        last = pe.transpose(turned[h][:, k * P:(k + 1) * P], x[:, h, k * P:(k + 1) * P], st.ident[:])
                    last.then_inc(x_turned, 1)
                for h in range(2):
                    pe.wait_ge(x_t_set, 2 * it + h + 1)
                    pe.wait_ge(src_out, 2 * it + h + 1)
                    pe.wait_ge(dst_out, 2 * it + h + 1)
                    for part, bank, summed in ((0, of_src, src_sum), (1, of_dst, dst_sum)):
                        for k in range(KC):
                            last = pe.matmul(bank[h][:], x_t[:, h, k, :], w_nodes[:, KC * part + k, :],
                                             start=(k == 0), stop=(k == KC - 1))
                        last.then_inc(summed, 1)


def layer2_edges(nc, st, ins, start_loads):
    with ExitStack() as ctx:
        phase_end(nc, ctx)

        def sb(name, shape, dt=F32):
            return ctx.enter_context(nc.sbuf_tensor("l2e_" + name, shape, dt))

        def sem(name):
            return phase_semaphore(nc, ctx, "l2e_" + name)

        w_edge, attr_t = sb("w_edge", [EDIM, HID2]), sb("attr_t", [EDIM, 2, GROUP * P])
        from_src, from_dst, hidden = (sb(n, [P, RING, HID2]) for n in ("from_src", "from_dst", "hidden"))
        stage_src, stage_dst = sb("stage_src", [P, RING], I32), sb("stage_dst", [P, RING], I32)
        onehot, x_onehot = sb("onehot", [P, RING, P]), sb("x_onehot", [P, GROUP, P])
        edge_sum = [ctx.enter_context(nc.psum_tensor(f"l2e_edge_sum{k}", [P, HID2], F32)) for k in range(GROUP)]
        total = [ctx.enter_context(nc.psum_tensor(f"l2e_total{h}", [P, HID2], F32)) for h in range(2)]
        x_total = ctx.enter_context(nc.psum_tensor("l2e_x_total", [P, HID2], F32))
        src_in = [sem(f"src_in{k}") for k in range(RING)]
        dst_in = [sem(f"dst_in{k}") for k in range(RING)]
        attr_in = [sem("attr_in0"), sem("attr_in1")]
        w_in, staged, attr_summed, half_added, all_added, relued, hot, hot_used, added, x_hot, x_used, x_added, turn = (
            sem(n) for n in ("w_in", "staged", "attr_summed", "half_added", "all_added", "relued", "hot", "hot_used",
                             "added", "x_hot", "x_used", "x_added", "turn"))
        block = ctx.enter_context(nc.Block())

        @block.sync
        def _(sp):
            sp.dma_start(w_edge[:], ins["L2_eW1"][2 * D:2 * D + EDIM, :]).then_inc(w_in, 16)
            start_loads(sp)
            with sp.Fori(0, HG) as it:
                for h in range(2):
                    sp.wait_ge(attr_summed, RING * it + GROUP * (h + 1))
                    sp.dma_start(attr_t[:, h, :], ins["edge_attr_t"][:, bass.ds((2 * it + h) * GROUP * P, GROUP * P)]
                                 ).then_inc(attr_in[h], 16)
            sp.wait_ge(w_in, 16)

        @block.gpsimd
        def _(pool):
            pool.sem_inc(all_added, RING)
            with pool.Fori(0, HG) as it:
                for q in range(PARTS):
                    pool.wait_ge(all_added, RING * it + PART * (q + 1))
                    pool.wait_ge(staged, PARTS * it + q + 1)
                    pool.sem_inc(turn, 1)
                    for k in range(PART * q, PART * (q + 1)):
                        for ring, stage, table, arrived in ((from_src, stage_src, st.src_rows, src_in),
                                                            (from_dst, stage_dst, st.dst_rows, dst_in)):
                            pool.indirect_dma_start(ring[:, k, :], None, table,
                                                    bass.IndirectOffsetOnAxis(ap=stage[:, k:k + 1], axis=0)
                                                    ).then_inc(arrived[k], 16)

        @block.scalar
        def _(act):
            def set_out(it, q):
                for stage, index in ((stage_src, st.src), (stage_dst, st.dst_row)):
                    last = act.activation(stage[:, PART * q:PART * (q + 1)], index[:, bass.ds(RING * it + PART * q, PART)],
                                          ACT.Copy)
                last.then_inc(staged, 1)

            def trip(it, ahead):
                for k in range(RING):
                    act.wait_ge(all_added, RING * it + k + 1 + RING)
                    act.activation(hidden[:, k, :], hidden[:, k, :], ACT.Relu).then_inc(relued, 1)
                    if ahead and k % PART == PART - 1:
                        set_out(it + 1, k // PART)

            for q in range(PARTS):
                set_out(0, q)
            with act.Fori(0, HG - 1) as it:
                trip(it, True)
            trip(HG - 1, False)

        @block.vector
        def _(dve):
            dve.sem_inc(added, 2)
            dve.sem_inc(x_added, 1)

            def build(it, h, window):
                for k in range(GROUP * h, GROUP * (h + 1)):
                    dve.wait_ge(hot_used, RING * it + k + 1)
                    one_hot(dve, st, onehot[:, k, :], window, it * RING + k).then_inc(hot, 1)

            def messages(it, h):
                for k in range(GROUP * h, GROUP * (h + 1)):
                    dve.wait_ge(attr_summed, RING * it + k + 1 + RING)
                    dve.wait_ge(src_in[k], 16 * it + 16)
                    dve.tensor_tensor(hidden[:, k, :], edge_sum[k % GROUP][:], from_src[:, k, :], ALU.add
                                      ).then_inc(half_added, 1)
                for k in range(GROUP * h, GROUP * (h + 1)):
                    dve.wait_ge(half_added, RING * it + k + 1 + GROUP)
                    dve.wait_ge(dst_in[k], 16 * it + 16)
                    dve.tensor_tensor(hidden[:, k, :], hidden[:, k, :], from_dst[:, k, :], ALU.add
                                      ).then_inc(all_added, 1)

            def trip(it, ahead):
                ranges, later = two_trips_ranges(nc, dve, st, it) if ahead else (group_ranges(nc, dve, st, it), None)
                for h in range(2):
                    first, more, before = ranges[h]
                    with dve.If(more > 0):
                        build_extra(nc, dve, st, it, h, first + 1, before, x_onehot, x_hot, x_used, turn)
                    dve.wait_ge(hot_used, RING * it + GROUP * (h + 1) + 2 * GROUP)
                    dve.wait_ge(added, 2 * it + h + 2)
                    dve.wait_ge(x_added, before + 1)
                    here = st.acc[:, bass.ds(first * WIDE, HID2)]
                    dve.tensor_tensor(here, here, total[h][:], ALU.add).then_inc(added, 1)
                    add_extras(nc, dve, st, ranges, it, h, x_onehot, x_total, HID2, added, x_hot, x_used, x_added, turn)
                    if ahead:
                        build(it + 1, h, later[h][0])
                        messages(it + 1, h)

            ranges = group_ranges(nc, dve, st, 0)
            for h in range(2):
                build(0, h, ranges[h][0])
                messages(0, h)
            with dve.Fori(0, HG - 1) as it:
                trip(it, True)
            trip(HG - 1, False)

        @block.tensor
        def _(pe):
            pe.sem_inc(hot_used, RING)
            pe.sem_inc(x_used, 1)
            pe.sem_inc(half_added, GROUP)
            pe.sem_inc(attr_summed, RING)
            pe.wait_ge(w_in, 16)

            def attributes(it, h):
                pe.wait_ge(attr_in[h], 16 * it + 16)
                for k in range(GROUP):
                    pe.wait_ge(half_added, RING * it + GROUP * h + k + 1)
                    pe.matmul(edge_sum[k][:], attr_t[:, h, k * P:(k + 1) * P], w_edge[:],
                              start=True, stop=True).then_inc(attr_summed, 1)

            def trip(it, ahead):
                ranges = group_ranges(nc, pe, st, it)
                for h in range(2):
                    pe.wait_ge(added, 2 * it + h + 1)
                    for k in range(GROUP * h, GROUP * (h + 1)):
                        pe.wait_ge(relued, RING * it + k + 1)
                        pe.wait_ge(hot, RING * it + k + 1)
                        pe.matmul(total[h][:], onehot[:, k, :], hidden[:, k, :],
                                  start=(k % GROUP == 0), stop=(k % GROUP == GROUP - 1)).then_inc(hot_used, 1)
                    _, more, before = ranges[h]
                    with pe.If(more > 0):
                        with pe.Fori(0, more) as j:
                            extra = before + j
                            pe.wait_ge(x_added, extra + 1)
                            pe.wait_ge(x_hot, extra + 1)
                            for k in range(GROUP):
                                last = pe.matmul(x_total[:], x_onehot[:, k, :], hidden[:, GROUP * h + k, :],
                                                 start=(k == 0), stop=(k == GROUP - 1))
                            last.then_inc(x_used, 1)
                    if ahead:
                        attributes(it + 1, h)

            attributes(0, 0)
            attributes(0, 1)
            with pe.Fori(0, HG - 1) as it:
                trip(it, True)
            trip(HG - 1, False)


def layer2_weights(nc, ctx, ins):
    KC, HCH = D // P, HID2 // P

    def sb(name, shape):
        return ctx.enter_context(nc.sbuf_tensor("l2n_" + name, shape, F32))

    e_w2, n_w1, n_w2 = sb("e_w2", [P, HCH, D]), sb("n_w1", [P, 2 * KC, HID2]), sb("n_w2", [P, HCH, D])
    e_b2, n_b1, n_b2 = sb("e_b2", [P, D]), sb("n_b1", [P, HCH]), sb("n_b2", [P, D])
    loaded = phase_semaphore(nc, ctx, "l2n_loaded")

    def start_loads(sp):
        sp.dma_start(e_w2[:], ins["L2_eW2"].rearrange("(c k) f -> k c f", k=P)).then_inc(loaded, 16)
        sp.dma_start(n_w1[:], ins["L2_nW1"].rearrange("(c k) f -> k c f", k=P)).then_inc(loaded, 16)
        sp.dma_start(n_w2[:], ins["L2_nW2"].rearrange("(c k) f -> k c f", k=P)).then_inc(loaded, 16)
        sp.dma_start(n_b1[:], ins["L2_nb1"].rearrange("(c k) -> k c", k=P), allow_slow_non_contiguous=True).then_inc(loaded, 16)
        sp.dma_start(e_b2[:], ins["L2_eb2"].partition_broadcast(P)).then_inc(loaded, 16)
        sp.dma_start(n_b2[:], ins["L2_nb2"].partition_broadcast(P)).then_inc(loaded, 16)

    return (e_w2, n_w1, n_w2, e_b2, n_b1, n_b2, loaded), start_loads


def layer2_nodes(nc, st, weights):
    KC, HCH = D // P, HID2 // P
    with ExitStack() as ctx:
        phase_end(nc, ctx)
        def sb(name, shape):
            return ctx.enter_context(nc.sbuf_tensor("l2n_" + name, shape, F32))

        def psum(name):
            return [ctx.enter_context(nc.psum_tensor(f"l2n_{name}{h}", [P, 512], F32)) for h in range(2)]

        def sem(name):
            return phase_semaphore(nc, ctx, "l2n_" + name)

        e_w2, n_w1, n_w2, e_b2, n_b1, n_b2, loaded = weights
        sums, sums_t = sb("sums", [P, 2, HID2]), sb("sums_t", [P, 2, HCH, P])
        both, both_t = sb("both", [P, 2, 2 * D]), sb("both_t", [P, 2, 2 * KC, P])
        hidden_t = sb("hidden_t", [P, 2, HCH, P])
        sums_turned, both_turned, hidden = psum("sums_turned"), psum("both_turned"), psum("hidden")
        outs = psum("outs")
        (slots_set, turned_a, sums_t_set, agg_sum, agg_set, turned_b, both_t_set, hidden_sum, hidden_set,
         upd_sum, upd_set, turn) = (sem(n) for n in (
             "slots_set", "turned_a", "sums_t_set", "agg_sum", "agg_set", "turned_b", "both_t_set",
             "hidden_sum", "hidden_set", "upd_sum", "upd_set", "turn"))
        x_added = sem("x_added")
        LOADS = 6
        block = ctx.enter_context(nc.Block())

        @block.scalar
        def _(act):
            act.wait_ge(loaded, LOADS * 16)
            with act.Fori(0, HW) as it:
                for h in range(2):
                    act.wait_ge(turned_a, 2 * it + h + 1)
                    act.wait_ge(turned_b, 2 * it + h + 1)
                    act.sem_inc(turn, 1)
                    act.activation(sums[:, h, :], st.acc[:, bass.ds((2 * it + h) * WIDE, HID2)], ACT.Copy)
                    act.activation(both[:, h, 0:D], st.x[:, bass.ds((2 * it + h) * D, D)], ACT.Copy).then_inc(slots_set, 1)
                for h in range(2):
                    act.wait_ge(turned_a, 2 * it + h + 3)
                    act.wait_ge(agg_sum, 2 * it + h + 1)
                    act.activation(sums_t[:, h, :, :], sums_turned[h][:].rearrange("p (k n) -> p k n", k=HCH), ACT.Copy
                                   ).then_inc(sums_t_set, 1)
                for h in range(2):
                    act.wait_ge(turned_b, 2 * it + h + 3)
                    act.wait_ge(hidden_sum, 2 * it + h + 1)
                    act.activation(both_t[:, h, :, :], both_turned[h][:].rearrange("p (k n) -> p k n", k=2 * KC), ACT.Copy
                                   ).then_inc(both_t_set, 1)
                for h in range(2):
                    act.wait_ge(hidden_sum, 2 * it + h + 3)
                    act.wait_ge(upd_sum, 2 * it + h + 1)
                    for c in range(HCH):
                        last = act.activation(hidden_t[:, h, c, :], hidden[h][:, c * P:(c + 1) * P], ACT.Relu,
                                              bias=n_b1[:, c:c + 1])
                    last.then_inc(hidden_set, 1)

        @block.vector
        def _(dve):
            dve.sem_inc(upd_set, 2)
            dve.wait_ge(loaded, LOADS * 16)
            with dve.Fori(0, HW) as it:
                for h in range(2):
                    dve.wait_ge(agg_sum, 2 * it + h + 3)
                    dve.scalar_tensor_tensor(out=both[:, h, D:2 * D], in0=e_b2[:],
                                             scalar=st.in_edges[:, bass.ds(2 * it + h, 1)], in1=outs[h][:, 0:D],
                                             op0=ALU.mult, op1=ALU.add).then_inc(agg_set, 1)
                for h in range(2):
                    dve.wait_ge(upd_sum, 2 * it + h + 3)
                    here = st.acc[:, bass.ds((2 * it + h) * WIDE, D)]
                    dve.tensor_tensor(here, outs[h][:, D:2 * D], n_b2[:], ALU.add).then_inc(upd_set, 1)
                    dve.wait_ge(upd_set, 2 * it + h + 3)
                    dve.sem_inc(turn, 1)
                    dve.tensor_tensor(here, here, st.x[:, bass.ds((2 * it + h) * D, D)], ALU.add).then_inc(x_added, 1)

        @block.tensor
        def _(pe):
            for credit in (turned_a, turned_b, agg_sum, hidden_sum, upd_sum):
                pe.sem_inc(credit, 2)
            pe.wait_ge(loaded, LOADS * 16)
            with pe.Fori(0, HW) as it:
                for h in range(2):
                    pe.wait_ge(slots_set, 2 * it + h + 1)
                    for k in range(HCH):
                        last = pe.transpose(sums_turned[h][:, k * P:(k + 1) * P], sums[:, h, k * P:(k + 1) * P], st.ident[:])
                    last.then_inc(turned_a, 1)
                for h in range(2):
                    pe.wait_ge(sums_t_set, 2 * it + h + 1)
                    pe.wait_ge(upd_set, 2 * it + h + 1)
                    for k in range(HCH):
                        last = pe.matmul(outs[h][:, 0:D], sums_t[:, h, k, :], e_w2[:, k, :],
                                         start=(k == 0), stop=(k == HCH - 1))
                    last.then_inc(agg_sum, 1)
                for h in range(2):
                    pe.wait_ge(agg_set, 2 * it + h + 1)
                    for k in range(2 * KC):
                        last = pe.transpose(both_turned[h][:, k * P:(k + 1) * P], both[:, h, k * P:(k + 1) * P], st.ident[:])
                    last.then_inc(turned_b, 1)
                for h in range(2):
                    pe.wait_ge(both_t_set, 2 * it + h + 1)
                    for c in range(HCH):
                        for k in range(2 * KC):
                            last = pe.matmul(hidden[h][:, c * P:(c + 1) * P], n_w1[:, k, c * P:(c + 1) * P],
                                             both_t[:, h, k, :], start=(k == 0), stop=(k == 2 * KC - 1))
                    last.then_inc(hidden_sum, 1)
                for h in range(2):
                    pe.wait_ge(hidden_set, 2 * it + h + 1)
                    for k in range(HCH):
                        last = pe.matmul(outs[h][:, D:2 * D], hidden_t[:, h, k, :], n_w2[:, k, :],
                                         start=(k == 0), stop=(k == HCH - 1))
                    last.then_inc(upd_sum, 1)


def layer2(nc, st, ins):
    layer2_tables(nc, st, ins)
    with ExitStack() as ctx:
        phase_end(nc, ctx)
        weights, start_loads = layer2_weights(nc, ctx, ins)
        layer2_edges(nc, st, ins, start_loads)
        layer2_nodes(nc, st, weights)
    layer_norm(nc, st, "ln2_", st.acc, WIDE, out=st.acc, out_column=D, gamma_beta=(ins["L2_ln_gamma"], ins["L2_ln_beta"]))
    layer_norm(nc, st, "ln3_", st.acc, WIDE, column=D)


def layer3_nodes(nc, st, ins):
    KC = D // P
    ROW = D + HEADS
    with ExitStack() as ctx:
        phase_end(nc, ctx)
        def sb(name, shape):
            return ctx.enter_context(nc.sbuf_tensor("l3n_" + name, shape, F32))

        def psum(name):
            return [ctx.enter_context(nc.psum_tensor(f"l3n_{name}{h}", [P, 512], F32)) for h in range(2)]

        def sem(name):
            return phase_semaphore(nc, ctx, "l3n_" + name)

        w, att = sb("w", [P, KC, D]), sb("att", [P, 2, D])
        x, x_t, scaled = sb("x", [P, 2, D]), sb("x_t", [P, 2, KC, P]), sb("scaled", [P, 2, 2, D])
        least, most = sb("least", [P, HEADS]), sb("most", [P, HEADS])
        turned, product = psum("turned"), psum("product")
        loaded, x_set, x_turned, x_t_set, summed, h_set, scaled_set, logits_set, chain, negated, reduced, rows_set, stored, turn = (
            sem(n) for n in ("loaded", "x_set", "x_turned", "x_t_set", "summed", "h_set", "scaled_set", "logits_set",
                             "chain", "negated", "reduced", "rows_set", "stored", "turn"))
        block = ctx.enter_context(nc.Block())
        acc = st.acc[:].rearrange("p (w f) -> p w f", w=NW)
        logits = st.logits[:].rearrange("p (w c) -> p w c", w=NW)

        @block.sync
        def _(sp):
            sp.dma_start(w[:], ins["L3_W"].rearrange("(c k) f -> k c f", k=P)).then_inc(loaded, 16)
            sp.dma_start(att[:, 0, :], ins["L3_att_src"].rearrange("h c -> (h c)").partition_broadcast(P)).then_inc(loaded, 16)
            sp.dma_start(att[:, 1, :], ins["L3_att_dst"].rearrange("h c -> (h c)").partition_broadcast(P)).then_inc(loaded, 16)
            sp.wait_ge(loaded, 48)
            sp.wait_ge(rows_set, 2)
            sp.dma_start(st.gat_logits.rearrange("(w p) f -> p w f", p=P),
                         st.maxima[:].rearrange("p (w c) -> p w c", w=NW)).then_inc(stored, 16)
            sp.wait_ge(stored, 16)

        @block.scalar
        def _(act):
            with act.Fori(0, HW) as it:
                for h in range(2):
                    act.wait_ge(x_turned, 2 * it + h + 1)
                    act.sem_inc(turn, 1)
                    act.activation(x[:, h, :], st.x[:, bass.ds((2 * it + h) * D, D)], ACT.Copy).then_inc(x_set, 1)
                for h in range(2):
                    act.wait_ge(x_turned, 2 * it + h + 3)
                    act.wait_ge(summed, 2 * it + h + 1)
                    act.activation(x_t[:, h, :, :], turned[h][:, 0:D].rearrange("p (k n) -> p k n", k=KC), ACT.Copy
                                   ).then_inc(x_t_set, 1)

        @block.tensor
        def _(pe):
            pe.sem_inc(x_turned, 2)
            pe.sem_inc(summed, 2)
            pe.wait_ge(loaded, 48)
            with pe.Fori(0, HW) as it:
                for h in range(2):
                    pe.wait_ge(x_set, 2 * it + h + 1)
                    for k in range(KC):
                        last = pe.transpose(turned[h][:, k * P:(k + 1) * P], x[:, h, k * P:(k + 1) * P], st.ident[:])
                    last.then_inc(x_turned, 1)
                for h in range(2):
                    pe.wait_ge(x_t_set, 2 * it + h + 1)
                    pe.wait_ge(scaled_set, 2 * it + h + 1)
                    for k in range(KC):
                        last = pe.matmul(product[h][:, 0:D], x_t[:, h, k, :], w[:, k, :], start=(k == 0), stop=(k == KC - 1))
                    last.then_inc(summed, 1)

        @block.vector
        def _(dve):
            dve.sem_inc(scaled_set, 2)
            dve.wait_ge(loaded, 48)
            with dve.Fori(0, HW) as it:
                for h in range(2):
                    dve.wait_ge(summed, 2 * it + h + 3)
                    dve.sem_inc(turn, 1)
                    dve.tensor_copy(st.acc[:, bass.ds((2 * it + h) * WIDE, D)], product[h][:, 0:D]).then_inc(h_set, 1)
                    dve.wait_ge(logits_set, 2 * it + h + 1)
                    dve.tensor_tensor(scaled[:, h, :, :], product[h][:, 0:D].unsqueeze(1).broadcast_to([P, 2, D]), att[:], ALU.mult
                                      ).then_inc(scaled_set, 1)
                for h in range(2):
                    dve.wait_ge(scaled_set, 2 * it + h + 3)
                    dve.sem_inc(turn, 1)
                    dve.tensor_reduce(st.logits[:, bass.ds((2 * it + h) * 2 * HEADS, 2 * HEADS)],
                                      scaled[:, h, :, :].rearrange("p s (a c) -> p (s a) c", c=CH), AX.X, ALU.add
                                      ).then_inc(logits_set, 1)
            dve.wait_ge(h_set, NW)
            dve.wait_ge(logits_set, NW + 2)
            dve.tensor_copy(acc[:, :, D:ROW], logits[:, :, 0:HEADS]).then_inc(rows_set, 1)
            dve.tensor_reduce(least[:], logits[:, :, 0:HEADS].rearrange("p w a -> p a w"), AX.X, ALU.min).then_inc(chain, 1)
            dve.wait_ge(chain, 1)
            dve.tensor_single_scalar(most[:], least[:], -1.0, ALU.mult).then_inc(negated, 1)
            dve.wait_ge(reduced, 1)
            dve.tensor_single_scalar(st.shift[:], st.shift[:], 1.0, ALU.add).then_inc(chain, 1)
            dve.wait_ge(chain, 2)
            dve.tensor_tensor(st.maxima[:].rearrange("p (w c) -> p w c", w=NW), logits[:, :, 0:HEADS],
                              st.shift[:].unsqueeze(1).broadcast_to([P, NW, HEADS]), ALU.add).then_inc(rows_set, 1)

        @block.gpsimd
        def _(pool):
            pool.sem_inc(logits_set, 2)
            pool.wait_ge(negated, 1)
            pool.partition_all_reduce(st.shift[:], most[:], P, bass.bass_isa.ReduceOp.max).then_inc(reduced, 1)


def layer3_maxima(nc, st):
    with ExitStack() as ctx:
        phase_end(nc, ctx)

        def sb(name, shape, dt=F32):
            return ctx.enter_context(nc.sbuf_tensor("l3m_" + name, shape, dt))

        def sem(name):
            return phase_semaphore(nc, ctx, "l3m_" + name)

        ring, stage = sb("ring", [P, RING, HEADS]), sb("stage", [P, RING], I32)
        onehot, x_onehot = sb("onehot", [P, RING, P]), sb("x_onehot", [P, GROUP, P])
        diagonal, highest, x_highest = sb("diagonal", [P, RING, HEADS, P]), sb("highest", [P, 2, HEADS]), sb("x_highest", [P, HEADS])
        spread = [ctx.enter_context(nc.psum_tensor(f"l3m_spread{h}", [P, GROUP, HEADS, P], F32)) for h in range(2)]
        arrived = [sem(f"arrived{k}") for k in range(RING)]
        stored = sem("stored")
        staged, diag_set, hot, spread_set, reduced, merged, x_hot, x_spread, x_reduced, x_merged, turn = (
            sem(n) for n in ("staged", "diag_set", "hot", "spread_set", "reduced", "merged", "x_hot", "x_spread",
                             "x_reduced", "x_merged", "turn"))
        half_done = [sem(f"half_done{h}") for h in range(2)]
        block = ctx.enter_context(nc.Block())

        @block.sync
        def _(sp):
            sp.dma_start(st.gat_rows.rearrange("(w p) f -> p w f", p=P),
                         st.acc[:].rearrange("p (w f) -> p w f", w=NW)[:, :, 0:D + HEADS]).then_inc(stored, 16)
            sp.wait_ge(stored, 16)

        @block.gpsimd
        def _(pool):
            pool.sem_inc(diag_set, RING)
            with pool.Fori(0, HG) as it:
                for h in range(2):
                    pool.wait_ge(diag_set, RING * it + GROUP * (h + 1))
                    pool.sem_inc(turn, 1)
                    pool.tensor_copy(stage[:, GROUP * h:GROUP * (h + 1)],
                                     st.src[:, bass.ds((2 * it + h) * GROUP, GROUP)]).then_inc(staged, 1)
                    pool.wait_ge(staged, 2 * it + h + 1)
                    pool.sem_inc(turn, 1)
                    for k in range(GROUP * h, GROUP * (h + 1)):
                        pool.indirect_dma_start(ring[:, k, :], None, st.gat_logits,
                                                bass.IndirectOffsetOnAxis(ap=stage[:, k:k + 1], axis=0)
                                                ).then_inc(arrived[k], 16)

        @block.scalar
        def _(act):
            with act.Fori(0, HG) as it:
                for h in range(2):
                    act.wait_ge(half_done[h], it + 1)
                    for k in range(GROUP * h, GROUP * (h + 1)):
                        act.wait_ge(arrived[k], 16 * it + 16)
                        for a in range(HEADS):
                            last = act.activation(diagonal[:, k, a, :], st.ident[:], ACT.Copy, scale=ring[:, k, a:a + 1])
                        last.then_inc(diag_set, 1)

        @block.vector
        def _(dve):
            dve.sem_inc(x_merged, 1)
            dve.sem_inc(merged, 2)

            def one_hots(out, it, h, window):
                return dve.tensor_tensor(
                    out, st.node_ids[:, bass.ds(window * P, P)].unsqueeze(1).broadcast_to([P, GROUP, P]),
                    st.dst[:, bass.ds((2 * it + h) * GROUP, GROUP)].unsqueeze(2).broadcast_to([P, GROUP, P]), ALU.is_equal)

            def build(it, h, window):
                dve.wait_ge(spread_set, 2 * it + h + 1)
                dve.sem_inc(turn, 1)
                one_hots(onehot[:, GROUP * h:GROUP * (h + 1), :], it, h, window).then_inc(hot, 1)

            def build_extra(it, h, window, extra):
                dve.wait_ge(x_spread, extra + 1)
                dve.sem_inc(turn, 1)
                one_hots(x_onehot[:], it, h, within(nc, window, NW - 1)).then_inc(x_hot, 1)

            def merge_extra(h, window, extra):
                dve.wait_ge(x_spread, extra + 2)
                dve.wait_ge(x_merged, extra + 1)
                dve.tensor_reduce(x_highest[:], spread[h][:].rearrange("p k a e -> p a k e"), AX.XY, ALU.max
                                  ).then_inc(x_reduced, 1)
                dve.wait_ge(x_reduced, extra + 2)
                here = st.maxima[:, bass.ds(within(nc, window, NW - 1) * HEADS, HEADS)]
                dve.tensor_tensor(here, here, x_highest[:], ALU.max).then_inc(x_merged, 1)

            def group(it, h, ranges, later):
                first, more, before = ranges[h]
                g = 2 * it + h
                with dve.If(more > 0):
                    build_extra(it, h, first + 1, before)
                dve.wait_ge(spread_set, g + 3)
                dve.wait_ge(merged, g + 1)
                dve.tensor_reduce(highest[:, h, :], spread[h][:].rearrange("p k a e -> p a k e"), AX.XY, ALU.max
                                  ).then_inc(reduced, 1)
                if later is not None:
                    build(it + 1, h, later[h][0])
                dve.wait_ge(reduced, g + 3)
                dve.wait_ge(merged, g + 2)
                dve.wait_ge(x_merged, before + 1)
                here = st.maxima[:, bass.ds(first * HEADS, HEADS)]
                dve.tensor_tensor(here, here, highest[:, h, :], ALU.max).then_inc(merged, 1)
                with dve.If(more > 0):
                    dve.wait_ge(merged, g + 3)
                    dve.sem_inc(turn, 1)
                    with dve.If(more > 1):
                        with dve.Fori(1, more) as j:
                            merge_extra(h, first + j, before + j - 1)
                            build_extra(it, h, first + 1 + j, before + j)
                    merge_extra(h, first + more, before + more - 1)

            ranges = group_ranges(nc, dve, st, 0)
            for h in range(2):
                build(0, h, ranges[h][0])
            with dve.Fori(0, HG - 1) as it:
                ranges, later = two_trips_ranges(nc, dve, st, it)
                for h in range(2):
                    group(it, h, ranges, later)
            ranges = group_ranges(nc, dve, st, HG - 1)
            for h in range(2):
                group(HG - 1, h, ranges, None)

        @block.tensor
        def _(pe):
            pe.sem_inc(spread_set, 2)
            pe.sem_inc(x_spread, 1)
            pe.sem_inc(half_done[0], 1)
            pe.sem_inc(half_done[1], 1)
            pe.sem_inc(reduced, 2)
            pe.sem_inc(x_reduced, 1)

            def first_step(it, h, extras_before, more):
                g = 2 * it + h
                pe.wait_ge(reduced, g + 1)
                pe.wait_ge(x_reduced, extras_before + 1)
                pe.wait_ge(hot, g + 1)
                for k in range(GROUP * h, GROUP * (h + 1)):
                    pe.wait_ge(diag_set, RING * it + k + 1 + RING)
                    last = pe.matmul(spread[h][:, k % GROUP, :, :], onehot[:, k, :], diagonal[:, k, :, :],
                                     start=True, stop=True)
                last.then_inc(spread_set, 1)
                with pe.If(more < 1):
                    pe.drain().then_inc(half_done[h], 1)

            def further_steps(it, h, ranges):
                _, more, before = ranges[h]
                with pe.If(more > 0):
                    pe.wait_ge(reduced, 2 * it + h + 3)
                    pe.sem_inc(turn, 1)
                    with pe.Fori(0, more) as j:
                        pe.wait_ge(x_reduced, before + j + 1)
                        pe.wait_ge(x_hot, before + j + 1)
                        for k in range(GROUP):
                            last = pe.matmul(spread[h][:, k, :, :], x_onehot[:, k, :], diagonal[:, GROUP * h + k, :, :],
                                             start=True, stop=True)
                        last.then_inc(x_spread, 1)
                    pe.drain().then_inc(half_done[h], 1)

            ranges = group_ranges(nc, pe, st, 0)
            first_step(0, 0, ranges[0][2], ranges[0][1])
            with pe.Fori(0, HG - 1) as it:
                ranges, later = two_trips_ranges(nc, pe, st, it)
                first_step(it, 1, ranges[0][2], ranges[1][1])
                further_steps(it, 0, ranges)
                first_step(it + 1, 0, ranges[1][2], later[0][1])
                further_steps(it, 1, ranges)
            ranges = group_ranges(nc, pe, st, HG - 1)
            first_step(HG - 1, 1, ranges[0][2], ranges[1][1])
            further_steps(HG - 1, 0, ranges)
            further_steps(HG - 1, 1, ranges)


def layer3_self_loops(nc, st):
    with ExitStack() as ctx:
        phase_end(nc, ctx)
        def sb(name, shape):
            return ctx.enter_context(nc.sbuf_tensor("l3s_" + name, shape, F32))

        def sem(name):
            return phase_semaphore(nc, ctx, "l3s_" + name)

        raw, self_logit = sb("raw", [P, NW, HEADS]), sb("self_logit", [P, NW, HEADS])
        chain, logit_set, weight_set = (sem(n) for n in ("chain", "logit_set", "weight_set"))
        block = ctx.enter_context(nc.Block())
        acc = st.acc[:].rearrange("p (w f) -> p w f", w=NW)
        logits = st.logits[:].rearrange("p (w c) -> p w c", w=NW)
        at_dst = st.at_dst[:].rearrange("p (w c) -> p w c", w=NW)

        @block.vector
        def _(dve):
            done = [0]

            def link(ins_):
                done[0] += 1
                ins_.then_inc(chain, 1)
                dve.wait_ge(chain, done[0])

            dve.tensor_copy(at_dst[:, :, 0:HEADS], logits[:, :, HEADS:2 * HEADS])
            link(dve.tensor_tensor(raw[:], st.maxima[:].rearrange("p (w c) -> p w c", w=NW),
                                   st.shift[:].unsqueeze(1).broadcast_to([P, NW, HEADS]), ALU.subtract))
            link(dve.tensor_tensor(raw[:], raw[:], logits[:, :, HEADS:2 * HEADS], ALU.add))
            link(dve.scalar_tensor_tensor(out=at_dst[:, :, HEADS:2 * HEADS], in0=raw[:], scalar=SLOPE, in1=raw[:],
                                          op0=ALU.mult, op1=ALU.max))
            link(dve.tensor_tensor(self_logit[:], logits[:, :, 0:HEADS], logits[:, :, HEADS:2 * HEADS], ALU.add))
            link(dve.scalar_tensor_tensor(out=raw[:], in0=self_logit[:], scalar=SLOPE, in1=self_logit[:],
                                          op0=ALU.mult, op1=ALU.max))
            dve.tensor_tensor(self_logit[:], raw[:], at_dst[:, :, HEADS:2 * HEADS], ALU.subtract).then_inc(logit_set, 1)
            dve.wait_ge(weight_set, 1)
            h4 = acc[:, :, 0:D].rearrange("p w (a c) -> p w a c", a=HEADS)
            link(dve.tensor_tensor(h4, h4, acc[:, :, D:D + HEADS].unsqueeze(3).broadcast_to([P, NW, HEADS, CH]), ALU.mult))

        @block.scalar
        def _(act):
            act.wait_ge(logit_set, 1)
            act.activation(acc[:, :, D:D + HEADS], self_logit[:], ACT.Exp).then_inc(weight_set, 1)


def layer3_edges(nc, st):
    ROW = D + HEADS
    with ExitStack() as ctx:
        phase_end(nc, ctx)

        def sb(name, shape, dt=F32):
            return ctx.enter_context(nc.sbuf_tensor("l3e_" + name, shape, dt))

        def bank(name):
            return ctx.enter_context(nc.psum_tensor("l3e_" + name, [P, 512], F32))

        def sem(name):
            return phase_semaphore(nc, ctx, "l3e_" + name)

        ring, rows, stage = sb("ring", [P, RING, ROW]), sb("rows", [P, RING, ROW]), sb("stage", [P, RING], I32)
        onehot, x_onehot = sb("onehot", [P, RING, P]), sb("x_onehot", [P, GROUP, P])
        dst_all, onehot_t = sb("dst_all", [P, 2, GROUP * P]), sb("onehot_t", [P, 2, GROUP * P])
        x_onehot_t = sb("x_onehot_t", [P, GROUP * P])
        logit, leaky = sb("logit", [P, 2, GROUP, HEADS]), sb("leaky", [P, 2, GROUP, HEADS])
        fetched = [bank(f"fetched{h}") for h in range(2)]
        total = [bank(f"total{h}") for h in range(2)]
        x_total = bank("x_total")
        arrived = [sem(f"arrived{k}") for k in range(RING)]
        dst_arrived = [sem(f"dst_arrived{h}") for h in range(2)]
        (staged, taken, dst_free, turned, got, x_turned, x_got, chain, logit_set, weight_set, hot, rows_set, scattered,
         added, x_hot, x_scattered, x_added, group_done, turn) = (
            sem(n) for n in ("staged", "taken", "dst_free", "turned", "got", "x_turned", "x_got", "chain", "logit_set",
                             "weight_set", "hot", "rows_set", "scattered", "added", "x_hot", "x_scattered", "x_added",
                             "group_done", "turn"))
        block = ctx.enter_context(nc.Block())

        @block.sync
        def _(sp):
            sp.sem_inc(dst_free, 2)
            with sp.Fori(0, HG) as it:
                for h in range(2):
                    sp.wait_ge(dst_free, 2 * it + h + 1)
                    sp.sem_inc(turn, 1)
                    sp.dma_start(dst_all[:, h, :], st.dst_rows_f[bass.ds(2 * it + h, 1), :].broadcast_to([P, GROUP * P])
                                 ).then_inc(dst_arrived[h], 16)

        @block.gpsimd
        def _(pool):
            pool.sem_inc(taken, RING)
            with pool.Fori(0, HG) as it:
                for q in range(PARTS):
                    pool.wait_ge(taken, RING * it + PART * (q + 1))
                    pool.wait_ge(staged, PARTS * it + q + 1)
                    pool.sem_inc(turn, 1)
                    for k in range(PART * q, PART * (q + 1)):
                        pool.indirect_dma_start(ring[:, k, :], None, st.gat_rows,
                                                bass.IndirectOffsetOnAxis(ap=stage[:, k:k + 1], axis=0)
                                                ).then_inc(arrived[k], 16)

        @block.scalar
        def _(act):
            def set_out(it, q):
                act.activation(stage[:, PART * q:PART * (q + 1)], st.src[:, bass.ds(RING * it + PART * q, PART)],
                               ACT.Copy).then_inc(staged, 1)

            def take(it, h, ahead=True):
                act.wait_ge(group_done, 2 * it + h + 1)
                for k in range(GROUP * h, GROUP * (h + 1)):
                    act.wait_ge(arrived[k], 16 * it + 16)
                    act.activation(rows[:, k, :], ring[:, k, :], ACT.Copy).then_inc(taken, 1)
                    if ahead and k % PART == PART - 1:
                        set_out(it + 1, k // PART)

            def weights(it, h):
                act.wait_ge(logit_set, 2 * it + h + 1 + 2)
                act.activation(rows[:, GROUP * h:GROUP * (h + 1), D:ROW], logit[:, h, :, :], ACT.Exp).then_inc(weight_set, 1)

            for q in range(PARTS):
                set_out(0, q)
            take(0, 0)
            weights(0, 0)
            with act.Fori(0, HG - 2) as it:
                take(it, 1)
                weights(it, 1)
                take(it + 1, 0)
                weights(it + 1, 0)
            take(HG - 2, 1)
            weights(HG - 2, 1)
            take(HG - 1, 0, False)
            weights(HG - 1, 0)
            take(HG - 1, 1, False)
            weights(HG - 1, 1)

        @block.vector
        def _(dve):
            dve.sem_inc(logit_set, 2)
            dve.sem_inc(added, 2)
            dve.sem_inc(x_added, 1)

            def build_turned(it, h, ranges):
                first, more, before = ranges[h]
                dve.wait_ge(dst_arrived[h], 16 * it + 16)
                dve.sem_inc(turn, 1)
                dve.tensor_scalar(onehot_t[:, h, :], dst_all[:, h, :], st.window_start[:, bass.ds(first, 1)],
                                  st.node[:], ALU.subtract, ALU.is_equal).then_inc(turned, 1)
                with dve.If(more > 0):
                    with dve.Fori(0, more) as j:
                        dve.wait_ge(x_got, GROUP * (before + j) + GROUP)
                        dve.sem_inc(turn, 1)
                        window = within(nc, first + 1 + j, NW - 1)
                        dve.tensor_scalar(x_onehot_t[:], dst_all[:, h, :], st.window_start[:, bass.ds(window, 1)],
                                          st.node[:], ALU.subtract, ALU.is_equal).then_inc(x_turned, 1)

            def logits(it, h):
                g = 2 * it + h
                view = fetched[h][:, 0:GROUP * 2 * HEADS].rearrange("p (k c) -> p k c", k=GROUP)
                dve.wait_ge(got, GROUP * g + GROUP)
                dve.wait_ge(taken, GROUP * g + GROUP + RING)
                dve.sem_inc(turn, 1)
                dve.tensor_tensor(logit[:, h, :, :], rows[:, GROUP * h:GROUP * (h + 1), D:ROW], view[:, :, 0:HEADS], ALU.add
                                  ).then_inc(chain, 1)
                dve.wait_ge(chain, 2 * g + 1)
                dve.scalar_tensor_tensor(out=leaky[:, h, :, :], in0=logit[:, h, :, :], scalar=SLOPE,
                                         in1=logit[:, h, :, :], op0=ALU.mult, op1=ALU.max).then_inc(chain, 1)
                dve.wait_ge(chain, 2 * g + 2)
                dve.tensor_tensor(logit[:, h, :, :], leaky[:, h, :, :], view[:, :, HEADS:2 * HEADS], ALU.subtract
                                  ).then_inc(logit_set, 1)

            def add(it, h, ranges):
                first, more, before = ranges[h]
                g = 2 * it + h
                dve.wait_ge(scattered, g + 1)
                dve.wait_ge(added, g + 2)
                dve.wait_ge(x_added, before + 1)
                here = st.acc[:, bass.ds(first * WIDE, ROW)]
                dve.tensor_tensor(here, here, total[h][:, 0:ROW], ALU.add).then_inc(added, 1)
                with dve.If(more > 0):
                    dve.wait_ge(added, g + 3)
                    add_extra(first + more, before + more - 1)

            def build(it, h, ranges):
                first = ranges[h][0]
                dve.tensor_tensor(onehot[:, GROUP * h:GROUP * (h + 1), :],
                                  st.node_ids[:, bass.ds(first * P, P)].unsqueeze(1).broadcast_to([P, GROUP, P]),
                                  st.dst[:, bass.ds((2 * it + h) * GROUP, GROUP)].unsqueeze(2).broadcast_to([P, GROUP, P]),
                                  ALU.is_equal).then_inc(hot, 1)

            def add_extra(window, extra):
                dve.wait_ge(x_scattered, extra + 2)
                dve.wait_ge(x_added, extra + 1)
                window = within(nc, window, NW - 1)
                here = st.acc[:, bass.ds(window * WIDE, ROW)]
                dve.tensor_tensor(here, here, x_total[:, 0:ROW], ALU.add).then_inc(x_added, 1)

            def build_extra(it, h, window, extra):
                dve.wait_ge(x_scattered, extra + 1)
                dve.sem_inc(turn, 1)
                window = within(nc, window, NW - 1)
                dve.tensor_tensor(x_onehot[:], st.node_ids[:, bass.ds(window * P, P)].unsqueeze(1).broadcast_to([P, GROUP, P]),
                                  st.dst[:, bass.ds((2 * it + h) * GROUP, GROUP)].unsqueeze(2).broadcast_to([P, GROUP, P]),
                                  ALU.is_equal).then_inc(x_hot, 1)

            def weigh(it, h):
                half = slice(GROUP * h, GROUP * (h + 1))
                dve.wait_ge(weight_set, 2 * it + h + 1)
                value = rows[:, half, 0:D].rearrange("p k (a c) -> p k a c", a=HEADS)
                dve.tensor_tensor(value, value, rows[:, half, D:ROW].unsqueeze(3).broadcast_to([P, GROUP, HEADS, CH]),
                                  ALU.mult).then_inc(rows_set, 1)

            def build_extras(it, h, ranges):
                first, more, before = ranges[h]
                with dve.If(more > 0):
                    build_extra(it, h, first + 1, before)
                    with dve.If(more > 1):
                        with dve.Fori(1, more) as j:
                            dve.wait_ge(added, 2 * it + h + 2)
                            add_extra(first + j, before + j - 1)
                            build_extra(it, h, first + 1 + j, before + j)

            ranges = group_ranges(nc, dve, st, 0)
            build_turned(0, 0, ranges)
            build(0, 0, ranges)
            build_turned(0, 1, ranges)
            logits(0, 0)
            weigh(0, 0)
            build(0, 1, ranges)
            build_extras(0, 0, ranges)
            with dve.Fori(0, HG - 1) as it:
                ranges, later = two_trips_ranges(nc, dve, st, it)
                build_turned(it + 1, 0, later)
                logits(it, 1)
                weigh(it, 1)
                add(it, 0, ranges)
                build(it + 1, 0, later)
                build_extras(it, 1, ranges)
                build_turned(it + 1, 1, later)
                logits(it + 1, 0)
                weigh(it + 1, 0)
                add(it, 1, ranges)
                build(it + 1, 1, later)
                build_extras(it + 1, 0, later)
            ranges = group_ranges(nc, dve, st, HG - 1)
            logits(HG - 1, 1)
            weigh(HG - 1, 1)
            add(HG - 1, 0, ranges)
            build_extras(HG - 1, 1, ranges)
            add(HG - 1, 1, ranges)

        @block.tensor
        def _(pe):
            pe.sem_inc(x_got, GROUP)
            pe.sem_inc(x_scattered, 1)
            pe.sem_inc(group_done, 2)

            def fetch(it, h, ranges):
                first, more, before = ranges[h]
                g = 2 * it + h
                pe.wait_ge(logit_set, g + 1)
                pe.wait_ge(turned, g + 1)
                pe.sem_inc(turn, 1)

                def fetch_tile(k):
                    pe.matmul(fetched[h][:, 2 * HEADS * k:2 * HEADS * (k + 1)], onehot_t[:, h, k * P:(k + 1) * P],
                              st.at_dst[:, bass.ds(2 * HEADS * first, 2 * HEADS)], start=(k == 0), stop=(k == GROUP - 1)
                              ).then_inc(got, 1)

                for k in range(GROUP - 1):
                    fetch_tile(k)
                with pe.If(more > 0):
                    with pe.Fori(0, more) as j:
                        window = within(nc, first + 1 + j, NW - 1)
                        pe.wait_ge(x_turned, before + j + 1)
                        pe.sem_inc(turn, 1)
                        for k in range(GROUP):
                            pe.matmul(fetched[h][:, 2 * HEADS * k:2 * HEADS * (k + 1)], x_onehot_t[:, k * P:(k + 1) * P],
                                      st.at_dst[:, bass.ds(2 * HEADS * window, 2 * HEADS)], start=False, stop=False
                                      ).then_inc(x_got, 1)
                fetch_tile(GROUP - 1)
                pe.sem_inc(dst_free, 1)

            def scatter(it, h, ranges):
                _, more, before = ranges[h]
                g = 2 * it + h
                pe.wait_ge(added, g + 1)
                pe.wait_ge(hot, g + 1)
                pe.wait_ge(rows_set, g + 1)
                for k in range(GROUP):
                    last = pe.matmul(total[h][:, 0:ROW], onehot[:, GROUP * h + k, :], rows[:, GROUP * h + k, :],
                                     start=(k == 0), stop=(k == GROUP - 1))
                last.then_inc(scattered, 1)
                with pe.If(more > 0):
                    with pe.Fori(0, more) as j:
                        pe.wait_ge(x_added, before + j + 1)
                        pe.wait_ge(x_hot, before + j + 1)
                        for k in range(GROUP):
                            last = pe.matmul(x_total[:, 0:ROW], x_onehot[:, k, :], rows[:, GROUP * h + k, :],
                                             start=(k == 0), stop=(k == GROUP - 1))
                        last.then_inc(x_scattered, 1)
                pe.drain().then_inc(group_done, 1)

            ranges = group_ranges(nc, pe, st, 0)
            fetch(0, 0, ranges)
            fetch(0, 1, ranges)
            scatter(0, 0, ranges)
            with pe.Fori(0, HG - 1) as it:
                ranges, later = two_trips_ranges(nc, pe, st, it)
                fetch(it + 1, 0, later)
                scatter(it, 1, ranges)
                fetch(it + 1, 1, later)
                scatter(it + 1, 0, later)
            scatter(HG - 1, 1, group_ranges(nc, pe, st, HG - 1))


def layer3_end(nc, st, ins):
    with ExitStack() as ctx:
        phase_end(nc, ctx)
        def sb(name, shape):
            return ctx.enter_context(nc.sbuf_tensor("l3z_" + name, shape, F32))

        def sem(name):
            return phase_semaphore(nc, ctx, "l3z_" + name)

        bias, per_weight = sb("bias", [P, D]), sb("per_weight", [P, NW, HEADS])
        squares, norm, per_norm = sb("squares", [P, NW]), sb("norm", [P, NW]), sb("per_norm", [P, NW])
        loaded, chain, biased, relued, summed, rooted, x_added = (
            sem(n) for n in ("loaded", "chain", "biased", "relued", "summed", "rooted", "x_added"))
        halves = slice(0, HW), slice(HW, NW)
        block = ctx.enter_context(nc.Block())
        acc = st.acc[:].rearrange("p (w f) -> p w f", w=NW)
        value, spare = acc[:, :, 0:D], acc[:, :, D:2 * D]

        @block.sync
        def _(sp):
            sp.dma_start(bias[:], ins["L3_bias"].partition_broadcast(P)).then_inc(loaded, 16)
            sp.wait_ge(loaded, 16)

        @block.vector
        def _(dve):
            done = [0]

            def link(ins_):
                done[0] += 1
                ins_.then_inc(chain, 1)
                dve.wait_ge(chain, done[0])

            link(dve.reciprocal(per_weight[:], acc[:, :, D:D + HEADS]))
            for half in halves:
                value4 = value[:, half].rearrange("p w (a c) -> p w a c", a=HEADS)
                link(dve.tensor_tensor(value4, value4, per_weight[:, half].unsqueeze(3).broadcast_to([P, HW, HEADS, CH]),
                                       ALU.mult))
                dve.wait_ge(loaded, 16)
                dve.tensor_tensor(value[:, half], value[:, half], bias[:].unsqueeze(1).broadcast_to([P, HW, D]), ALU.add
                                  ).then_inc(biased, 1)
            for n, half in enumerate(halves):
                dve.wait_ge(relued, 2 * n + 2)
                dve.tensor_reduce(squares[:, half], spare[:, half], AX.X, ALU.add).then_inc(summed, 1)
            dve.wait_ge(rooted, 1)
            link(dve.tensor_single_scalar(norm[:], norm[:], 1e-12, ALU.max))
            link(dve.reciprocal(per_norm[:], norm[:]))
            with dve.Fori(0, NW // STRETCH) as t:
                for u in range(STRETCH):
                    w = STRETCH * t + u
                    here = st.acc[:, bass.ds(WIDE * w, D)]
                    dve.scalar_tensor_tensor(out=here, in0=here, scalar=per_norm[:, bass.ds(w, 1)],
                                             in1=st.x[:, bass.ds(D * w, D)], op0=ALU.mult, op1=ALU.add).then_inc(x_added, 1)
            dve.wait_ge(x_added, NW)

        @block.scalar
        def _(act):
            for n, half in enumerate(halves):
                act.wait_ge(biased, n + 1)
                act.activation(value[:, half], value[:, half], ACT.Relu).then_inc(relued, 1)
                act.wait_ge(relued, 2 * n + 1)
                act.activation(spare[:, half], value[:, half], ACT.Square).then_inc(relued, 1)
            act.wait_ge(summed, 2)
            act.activation(norm[:], squares[:], ACT.Sqrt).then_inc(rooted, 1)


def layer3(nc, st, ins):
    layer3_nodes(nc, st, ins)
    layer3_maxima(nc, st)
    layer3_self_loops(nc, st)
    layer3_edges(nc, st)
    layer3_end(nc, st, ins)
    layer_norm(nc, st, "ln4_", st.acc, WIDE)


def start_layer0(nc, st):
    with ExitStack() as ctx:
        phase_end(nc, ctx)
        copied = phase_semaphore(nc, ctx, "start0_copied")
        block = ctx.enter_context(nc.Block())

        @block.vector
        def _(dve):
            acc = st.acc[:].rearrange("p (w f) -> p w f", w=NW)
            dve.memset(acc[:, :, D:D + 1], 0.0).then_inc(copied, 1)
            dve.tensor_copy(acc[:, :, 0:D], st.x[:].rearrange("p (w f) -> p w f", w=NW)).then_inc(copied, 1)


def finish(nc, st, out):
    with ExitStack() as ctx:
        phase_end(nc, ctx)
        stored = phase_semaphore(nc, ctx, "finish_stored")
        block = ctx.enter_context(nc.Block())
        full = N // P

        @block.sync
        def _(sp):
            sp.dma_start(out[0:full * P, :].rearrange("(w p) f -> p w f", p=P),
                         st.x[:, 0:full * D].rearrange("p (w f) -> p w f", f=D)).then_inc(stored, 16)
            sp.dma_start(out[full * P:N, :], st.x[0:N - full * P, full * D:(full + 1) * D]).then_inc(stored, 16)
            sp.wait_ge(stored, 32)


def build(nc, ins, out):
    with ExitStack() as ctx:
        st = State()

        def sb(name, shape, dt=F32):
            return ctx.enter_context(nc.sbuf_tensor(name, shape, dt))

        st.x = sb("x", [P, NW * D])
        st.iota = sb("iota", [P, P])
        st.ident = sb("ident", [P, P])
        st.node_ids = sb("node_ids", [P, NW * P])
        st.node = sb("node", [P, 1])
        st.window_start = sb("window_start", [P, NW])
        st.dst = sb("dst", [P, NT])
        st.src = sb("src", [P, NT], I32)
        st.src_type = sb("src_type", [P, NT], I32)
        st.weight = sb("weight", [P, NT])
        st.ranges = sb("ranges", [1, HG], I32)
        st.dst_row = sb("dst_row", [P, NT], I32)
        st.degree = sb("degree", [P, NW])
        st.in_edges = sb("in_edges", [P, NW])
        st.dinv = sb("dinv", [P, NW])

        def rows(name, width):
            return nc.dram_tensor(name, [NP, width], F32, kind="Internal").ap()

        st.logits = sb("logits", [P, NW * 2 * HEADS])
        st.at_dst = sb("at_dst", [P, NW * 2 * HEADS])
        st.maxima = sb("maxima", [P, NW * HEADS])
        st.shift = sb("shift", [P, HEADS])
        st.gat_rows = rows("attention_table", D + HEADS)
        st.gat_logits = rows("attention_logit_table", HEADS)
        st.table1 = rows("conv1_table", D)
        st.table2 = rows("conv2_table", D)
        st.src_rows = rows("message_src_table", HID2)
        st.dst_rows = rows("message_dst_table", HID2)
        st.dst_rows_f = nc.dram_tensor("dst_by_group_table", [NG, GROUP * P], F32, kind="Internal").ap()
        st.ranges_dram = nc.dram_tensor("group_table", [NG, 3], I32, kind="Internal").ap()
        st.rel_rows = nc.dram_tensor("relation_table", [NP * RELS, D], F32, kind="Internal").ap()
        with ExitStack() as early:
            phase_end(nc, early)
            st.rel_weights = early.enter_context(nc.sbuf_tensor("rel_weights", [P, RELS // 2, 2, D // P, D], F32))
            st.rel_loaded = [phase_semaphore(nc, early, f"rel_loaded{b}") for b in range(RELS // 2)]
            prepare(nc, st, ins)
            transform_by_relation(nc, st, ins)
        st.acc = sb("acc", [P, NW * WIDE])
        start_layer0(nc, st)
        aggregate(nc, st, "l0_", st.rel_rows, st.src_type, st.weight)
        layer_norm(nc, st, "ln0_", st.acc, WIDE)
        layer1(nc, st, ins)
        layer2(nc, st, ins)
        layer3(nc, st, ins)
        finish(nc, st, out)


def kernel(**inputs):
    import concourse.bacc as bacc
    from concourse.bass_utils import run_bass_kernel_spmd

    given = {name: np.asarray(a) for name, a in inputs.items()}

    def padded(a, fill):
        rows = np.full((EP,), fill, a.dtype)
        rows[:E] = a.reshape(-1)
        return rows

    def by_tile(a):
        return np.ascontiguousarray(a.reshape(NT, P).T)

    x = np.zeros((NP, D), given["x"].dtype)
    x[:N] = given["x"]
    attr = np.zeros((EP, EDIM), given["edge_attr_64"].dtype)
    attr[:E] = given["edge_attr_64"]
    dst = padded(given["dst"], PAD_NODE)
    arrays = {
        "x": x, "x_t": np.ascontiguousarray(x.T),
        "src": by_tile(padded(given["src"], 0)), "dst": by_tile(dst),
        "dst_by_group": dst.reshape(NG, GROUP * P),
        "edge_type": by_tile(padded(given["edge_type_16"], 0)),
        "edge_weight": by_tile(padded(given["edge_weight1"], 0)),
        "edge_attr_t": np.ascontiguousarray(attr.T),
    }
    for name, a in given.items():
        if name.startswith("L"):
            arrays[name.replace("_gnn", "")] = np.ascontiguousarray(a)
    nc = bacc.Bacc("TRN2", target_bir_lowering=False, num_devices=1)
    ins = {name: nc.dram_tensor("in_" + name, a.shape, mybir.dt.from_np(a.dtype), kind="ExternalInput").ap()
           for name, a in arrays.items()}
    out = nc.dram_tensor("out", [N, D], F32, kind="ExternalOutput").ap()
    build(nc, ins, out)
    result = run_bass_kernel_spmd(nc, [{"in_" + name: a for name, a in arrays.items()}], core_ids=[0])
    return result.results[0]["out"]
```
